# Optimizing a Trainium2 kernel written in Bass

```python
import numpy as np
import jax
import jax.numpy as jnp

def _softmax(x, axis=-1):
    return jax.nn.softmax(x, axis=axis)

def _gelu(x):
    return jax.nn.gelu(x, approximate=True)

def _silu(x):
    return jax.nn.silu(x)

def _sigmoid(x):
    return jax.nn.sigmoid(x)

def _layernorm(x, axis=-1, eps=1e-05):
    m = jnp.mean(x, axis=axis, keepdims=True)
    v = jnp.var(x, axis=axis, keepdims=True)
    return (x - m) / jnp.sqrt(v + eps)

def _scatter_add(tgt, idx, src, axis=0):
    return tgt.at[idx].add(src)

def _segment_sum(src, seg, n):
    return jax.ops.segment_sum(src, seg, n)
kernel_name = 'mk_decoder_postln_d1_seqx_r4_b2467e'

def setup_inputs(seed: int=0):
    np.random.seed(seed)
    _w = jnp.asarray

    def _rec_inputs():
        import jax
        import jax.numpy as jnp
        _rk = jax.random.key(seed)
        x = 7.22e-05 + 1 * jax.random.normal(jax.random.fold_in(_rk, 1), (8, 256, 256), jnp.float32)
        _lenS = 256 - jax.random.randint(jax.random.fold_in(_rk, 7), (8,), 0, max(1, 256 // 4) + 1, jnp.int32)
        _lenS2 = 256 - jax.random.randint(jax.random.fold_in(_rk, 8), (8,), 0, max(1, 256 // 4) + 1, jnp.int32)
        _ctx_768P = jax.random.normal(jax.random.fold_in(_rk, 11), (8, 16, 192), jnp.float32)
        _ctx_768c = jax.random.dirichlet(jax.random.fold_in(_rk, 511), 0.3 * jnp.ones((16,), jnp.float32), (8, 256))
        _ctx_768t = jnp.einsum('bsk,bkd->bsd', _ctx_768c, _ctx_768P)
        _ctx_768t = _ctx_768t * jax.lax.rsqrt(jnp.mean(jnp.square(_ctx_768t)) + 1e-12) * 0.953939
        ctx_768 = -7.36909e-05 + 0.999899 * (_ctx_768t + 0.3 * jax.random.normal(jax.random.fold_in(_rk, 611), (8, 256, 192), jnp.float32))
        return (x, ctx_768)
    x, ctx_768 = _rec_inputs()

    def _L0_attn_setup():
        import jax, jax.numpy as jnp
        import numpy as np
        B, T, D, H = (2, 256, 256, 16)
        DH = D // H
        _PAIRS = [(0, 1), (0, 2), (0, 3), (1, 2), (1, 3), (2, 3)]
        _J6 = jnp.array([[0, 0, 0, 0, 0, 1], [0, 0, 0, 0, -1, 0], [0, 0, 0, 1, 0, 0], [0, 0, 1, 0, 0, 0], [0, -1, 0, 0, 0, 0], [1, 0, 0, 0, 0, 0]], dtype=jnp.float32)

        def exterior(p1, p2):
            parts = [p1[..., i] * p2[..., j] - p1[..., j] * p2[..., i] for i, j in _PAIRS]
            L = jnp.stack(parts, axis=-1)
            n = jnp.maximum(jnp.linalg.norm(L, axis=-1, keepdims=True), 1e-12)
            return L / n
        key = jax.random.key(seed)
        ks = jax.random.split(key, 10)
        s = 0.02
        return {'x': jax.random.normal(ks[0], (B, T, D), jnp.float32), 'Wqkv': jax.random.normal(ks[1], (3 * D, D), jnp.float32) * s, 'bqkv': jnp.zeros((3 * D,), jnp.float32), 'W1w': jax.random.normal(ks[2], (4 * H, D), jnp.float32) * s, 'W2w': jax.random.normal(ks[3], (4 * H, D), jnp.float32) * s, 'W1r': jax.random.normal(ks[4], (4 * H, D), jnp.float32) * s, 'W2r': jax.random.normal(ks[5], (4 * H, D), jnp.float32) * s, 'bias_scale': jnp.full((H,), 0.1, jnp.float32), 'Wout': jax.random.normal(ks[6], (D, D), jnp.float32) * s, 'bout': jnp.zeros((D,), jnp.float32)}
    _L0_attn_all = _L0_attn_setup()
    _L0_attn_in = {k: v for k, v in _L0_attn_all.items() if k in ('Wqkv', 'bqkv', 'W1w', 'W2w', 'W1r', 'W2r', 'bias_scale', 'Wout', 'bout')}
    del _L0_attn_all

    def _L0_xattn_setup():
        import jax, jax.numpy as jnp
        import numpy as np
        NUM_HEADS = 16
        HEAD_DIM = 64
        INNER = NUM_HEADS * HEAD_DIM
        QUERY_DIM = 256
        CONTEXT_DIM = 192
        SCALE = HEAD_DIM ** (-0.5)
        key = jax.random.key(seed)
        ks = jax.random.split(key, 6)
        B, NQ, NKV = (8, 256, 512)
        query = jax.random.normal(ks[0], (B, NQ, QUERY_DIM), dtype=jnp.float32)
        context = jax.random.normal(ks[1], (B, NKV, CONTEXT_DIM), dtype=jnp.float32)
        w_q = jax.random.normal(ks[2], (QUERY_DIM, INNER), dtype=jnp.float32) * QUERY_DIM ** (-0.5)
        w_kv = jax.random.normal(ks[3], (CONTEXT_DIM, 2 * INNER), dtype=jnp.float32) * CONTEXT_DIM ** (-0.5)
        w_out = jax.random.normal(ks[4], (INNER, QUERY_DIM), dtype=jnp.float32) * INNER ** (-0.5)
        b_out = jax.random.normal(ks[5], (QUERY_DIM,), dtype=jnp.float32) * 0.01
        return {'query': query, 'context': context, 'w_q': w_q, 'w_kv': w_kv, 'w_out': w_out, 'b_out': b_out}
    _L0_xattn_all = _L0_xattn_setup()
    _L0_xattn_in = {k: v for k, v in _L0_xattn_all.items() if k in ('w_q', 'w_kv', 'w_out', 'b_out')}
    del _L0_xattn_all

    def _L0_ffn_setup():
        import jax, jax.numpy as jnp
        import numpy as np
        E = 32
        K = 4
        H = 256
        I = 128
        B, S = (2, 512)
        T = B * S
        C = 256
        ROUTED_SCALE = 1.0

        def _silu_and_mul(gu):
            g, u = jnp.split(gu, 2, axis=-1)
            return jax.nn.silu(g) * u
        key = jax.random.key(seed)
        ks = jax.random.split(key, 6)
        s = 0.02
        return {'hidden_states': jax.random.normal(ks[0], (B, S, H), jnp.float32), 'gate_w': jax.random.normal(ks[1], (E, H), jnp.float32) * s, 'w_gate_up': jax.random.normal(ks[2], (E, H, 2 * I), jnp.float32) * s, 'w_down': jax.random.normal(ks[3], (E, I, H), jnp.float32) * s, 'shared_w_gate_up': jax.random.normal(ks[4], (H, 2 * I), jnp.float32) * s, 'shared_w_down': jax.random.normal(ks[5], (I, H), jnp.float32) * s}
    _L0_ffn_all = _L0_ffn_setup()
    _L0_ffn_in = {k: v for k, v in _L0_ffn_all.items() if k in ('gate_w', 'w_gate_up', 'w_down', 'shared_w_gate_up', 'shared_w_down')}
    del _L0_ffn_all
    return {'x': x, 'ctx_768': ctx_768, 'L0_attn_Wqkv': _L0_attn_in['Wqkv'], 'L0_attn_bqkv': _L0_attn_in['bqkv'], 'L0_attn_W1w': _L0_attn_in['W1w'], 'L0_attn_W2w': _L0_attn_in['W2w'], 'L0_attn_W1r': _L0_attn_in['W1r'], 'L0_attn_W2r': _L0_attn_in['W2r'], 'L0_attn_bias_scale': _L0_attn_in['bias_scale'], 'L0_attn_Wout': _L0_attn_in['Wout'], 'L0_attn_bout': _L0_attn_in['bout'], 'L0_xattn_w_q': _L0_xattn_in['w_q'], 'L0_xattn_w_kv': _L0_xattn_in['w_kv'], 'L0_xattn_w_out': _L0_xattn_in['w_out'], 'L0_xattn_b_out': _L0_xattn_in['b_out'], 'L0_ffn_gate_w': _L0_ffn_in['gate_w'], 'L0_ffn_w_gate_up': _L0_ffn_in['w_gate_up'], 'L0_ffn_w_down': _L0_ffn_in['w_down'], 'L0_ffn_shared_w_gate_up': _L0_ffn_in['shared_w_gate_up'], 'L0_ffn_shared_w_down': _L0_ffn_in['shared_w_down']}

def reference(x, ctx_768, L0_attn_Wqkv, L0_attn_bqkv, L0_attn_W1w, L0_attn_W2w, L0_attn_W1r, L0_attn_W2r, L0_attn_bias_scale, L0_attn_Wout, L0_attn_bout, L0_xattn_w_q, L0_xattn_w_kv, L0_xattn_w_out, L0_xattn_b_out, L0_ffn_gate_w, L0_ffn_w_gate_up, L0_ffn_w_down, L0_ffn_shared_w_gate_up, L0_ffn_shared_w_down):
    import jax
    import jax.numpy as jnp

    def _L0_attn_ref(x, Wqkv, bqkv, W1w, W2w, W1r, W2r, bias_scale, Wout, bout):
        import jax, jax.numpy as jnp
        import numpy as np
        B, T, D, H = (2, 256, 256, 16)
        DH = D // H
        _PAIRS = [(0, 1), (0, 2), (0, 3), (1, 2), (1, 3), (2, 3)]
        _J6 = jnp.array([[0, 0, 0, 0, 0, 1], [0, 0, 0, 0, -1, 0], [0, 0, 0, 1, 0, 0], [0, 0, 1, 0, 0, 0], [0, -1, 0, 0, 0, 0], [1, 0, 0, 0, 0, 0]], dtype=jnp.float32)

        def exterior(p1, p2):
            parts = [p1[..., i] * p2[..., j] - p1[..., j] * p2[..., i] for i, j in _PAIRS]
            L = jnp.stack(parts, axis=-1)
            n = jnp.maximum(jnp.linalg.norm(L, axis=-1, keepdims=True), 1e-12)
            return L / n
        Bb, Tt, Dd = x.shape
        scale = DH ** (-0.5)
        qkv = (x @ Wqkv.T + bqkv).reshape(Bb, Tt, 3, H, DH)
        q = jnp.transpose(qkv[:, :, 0], (0, 2, 1, 3))
        k = jnp.transpose(qkv[:, :, 1], (0, 2, 1, 3))
        v = jnp.transpose(qkv[:, :, 2], (0, 2, 1, 3))
        std_logits = jnp.einsum('bhtd,bhsd->bhts', q, k) * scale
        x_prev = jnp.concatenate([jnp.zeros((Bb, 1, Dd), x.dtype), x[:, :-1]], axis=1)
        w1 = (x_prev @ W1w.T).reshape(Bb, Tt, H, 4)
        w2 = (x @ W2w.T).reshape(Bb, Tt, H, 4)
        write_lines = exterior(w1, w2)
        r1 = (x @ W1r.T).reshape(Bb, Tt, H, 4)
        r2 = (x @ W2r.T).reshape(Bb, Tt, H, 4)
        read_lines = exterior(r1, r2)
        Jw = jnp.einsum('bthi,ij->bhtj', write_lines, _J6)
        rd = jnp.transpose(read_lines, (0, 2, 1, 3))
        outer = Jw[..., :, None] * Jw[..., None, :]
        M_causal = jnp.cumsum(outer, axis=2)
        rd_M = jnp.einsum('bhti,bhtij->bhtj', rd, M_causal)
        bias_raw = jnp.einsum('bhti,bhsi->bhts', rd_M, Jw)
        bias = jnp.abs(bias_raw) * bias_scale.reshape(1, H, 1, 1)
        logits = std_logits + bias
        mask = jnp.triu(jnp.ones((Tt, Tt), bool), 1)
        logits = jnp.where(mask, -jnp.inf, logits)
        attn = jax.nn.softmax(logits, axis=-1)
        out = jnp.einsum('bhts,bhsd->bthd', attn, v).reshape(Bb, Tt, Dd)
        return out @ Wout.T + bout

    def _L0_xattn_ref(query, context, w_q, w_kv, w_out, b_out):
        import jax, jax.numpy as jnp
        import numpy as np
        NUM_HEADS = 16
        HEAD_DIM = 64
        INNER = NUM_HEADS * HEAD_DIM
        QUERY_DIM = 256
        CONTEXT_DIM = 192
        SCALE = HEAD_DIM ** (-0.5)
        B, NQ, _ = query.shape
        NKV = context.shape[1]
        q = query @ w_q
        kv = context @ w_kv
        k, v = jnp.split(kv, 2, axis=-1)
        q = q.reshape(B, NQ, NUM_HEADS, HEAD_DIM).transpose(0, 2, 1, 3)
        k = k.reshape(B, NKV, NUM_HEADS, HEAD_DIM).transpose(0, 2, 1, 3)
        v = v.reshape(B, NKV, NUM_HEADS, HEAD_DIM).transpose(0, 2, 1, 3)
        scores = jnp.einsum('bhqd,bhkd->bhqk', q, k) * SCALE
        attn = jax.nn.softmax(scores, axis=-1)
        out = jnp.einsum('bhqk,bhkd->bhqd', attn, v)
        out = out.transpose(0, 2, 1, 3).reshape(B, NQ, INNER)
        return out @ w_out + b_out

    def _L0_ffn_ref(hidden_states, gate_w, w_gate_up, w_down, shared_w_gate_up, shared_w_down):
        import jax, jax.numpy as jnp
        import numpy as np
        E = 32
        K = 4
        H = 256
        I = 128
        B, S = (2, 512)
        T = B * S
        C = 256
        ROUTED_SCALE = 1.0

        def _silu_and_mul(gu):
            g, u = jnp.split(gu, 2, axis=-1)
            return jax.nn.silu(g) * u
        b, s, h = hidden_states.shape
        x = hidden_states.reshape(-1, h)
        t = x.shape[0]
        logits = x @ gate_w.T
        probs = jax.nn.softmax(logits, axis=-1)
        topk_w, topk_idx = jax.lax.top_k(probs, K)
        topk_w = topk_w / jnp.sum(topk_w, axis=-1, keepdims=True)
        topk_w = topk_w * ROUTED_SCALE
        e_flat = topk_idx.reshape(-1)
        w_flat = topk_w.reshape(-1)
        t_flat = jnp.repeat(jnp.arange(t), K)
        order = jnp.argsort(e_flat)
        e_s, w_s, t_s = (e_flat[order], w_flat[order], t_flat[order])
        counts = jax.ops.segment_sum(jnp.ones_like(e_s), e_s, num_segments=E)
        starts = jnp.cumsum(counts) - counts
        pos = jnp.arange(t * K) - starts[e_s]
        slot = jnp.minimum(pos, C)
        buf = jnp.zeros((E, C + 1, h), x.dtype).at[e_s, slot].set(x[t_s])
        gu = jnp.einsum('ech,ehi->eci', buf[:, :C], w_gate_up)
        expert_out = jnp.einsum('eci,eih->ech', _silu_and_mul(gu), w_down)
        expert_out = jnp.pad(expert_out, ((0, 0), (0, 1), (0, 0)))
        gate = jnp.where(pos < C, w_s, 0.0)[:, None]
        routed = jnp.zeros_like(x).at[t_s].add(expert_out[e_s, slot] * gate)
        shared = _silu_and_mul(x @ shared_w_gate_up) @ shared_w_down
        return (routed + shared).reshape(b, s, h)
    x = _layernorm(x + _L0_attn_ref(x, L0_attn_Wqkv, L0_attn_bqkv, L0_attn_W1w, L0_attn_W2w, L0_attn_W1r, L0_attn_W2r, L0_attn_bias_scale, L0_attn_Wout, L0_attn_bout), axis=-1)
    x = _layernorm(x + _L0_xattn_ref(x, ctx_768, L0_xattn_w_q, L0_xattn_w_kv, L0_xattn_w_out, L0_xattn_b_out), axis=-1)
    x = _layernorm(x + _L0_ffn_ref(x, L0_ffn_gate_w, L0_ffn_w_gate_up, L0_ffn_w_down, L0_ffn_shared_w_gate_up, L0_ffn_shared_w_down), axis=-1)
    return x

_drawn_inputs = setup_inputs


def setup_inputs(seed=0):
    import zlib

    import numpy as np

    out = dict(_drawn_inputs(seed))
    spreads = {'L0_attn_bqkv': (0.0, 0.1),
     'L0_attn_bias_scale': (0.10000000149011612, 0.6),
     'L0_attn_bout': (0.0, 0.1)}
    factors = {'L0_attn_Wqkv': 3.624,
     'L0_attn_W1w': 8.0,
     'L0_attn_W2w': 8.0,
     'L0_attn_W1r': 8.0,
     'L0_attn_W2r': 8.0,
     'L0_xattn_b_out': 6.1,
     'L0_ffn_gate_w': 8.0,
     'L0_ffn_w_gate_up': 8.0,
     'L0_ffn_w_down': 8.0,
     'L0_ffn_shared_w_gate_up': 4.704,
     'L0_ffn_shared_w_down': 4.713}
    for name, (base, spread) in spreads.items():
        noise = np.random.default_rng([zlib.crc32(name.encode()), seed]).standard_normal(out[name].shape)
        drawn = base * np.exp(spread * noise) if base else spread * noise
        out[name] = jnp.asarray(drawn.astype(out[name].dtype))
    for name, factor in factors.items():
        out[name] = (out[name] * factor).astype(out[name].dtype)
    return out
```

```python
from contextlib import ExitStack

import numpy as np

import concourse.bass as bass
from concourse import mybir

F32 = mybir.dt.float32
BF16 = mybir.dt.bfloat16
U32 = mybir.dt.uint32
ALU = mybir.AluOpType
ACT = mybir.ActivationFunctionType
X = mybir.AxisListType.X

P = 128
B, T, D = 8, 256, 256
TT = T // P
H, DH = 16, 16
XH, XD = 16, 64
C = 192
CP = C // 2
E, K, CAP, I = 32, 4, 256, 128
N = B * T
SLOTS = E * CAP
EPS = 1e-5
NEG = -1e30

RD, RA, RO = 3, 3, 2
GROUPS = H // 4
LOOK = 2
RING = 4
VEC_STEPS = 34


def plan():
    d, a, o = [], [], []
    for j in range(TT):
        d += [("g1", j), ("g2", j)]
    a += [("k", n) for n in range(4)] + [("v", n) for n in range(4)]
    d += [("m", j, f) for j in range(TT) for f in range(2)]
    a += [("t", w, j) for w in range(3) for j in range(TT)]
    for h in range(-LOOK, H):
        if h + LOOK < H:
            d.append(("x", h + LOOK))
            a.append(("y", h + LOOK))
        if h >= 0:
            d.append(("pt", h))
    o += [("o", 0), ("o", 1)]
    a.append(("ot",))
    d += [("out",), ("x1t",)]
    a += [("q", n) for n in range(4)]
    for h in range(-LOOK, XH):
        if h + LOOK < XH:
            a.append(("s", h + LOOK))
        if h >= 0:
            d.append(("pt2", h))
    o += [("o2", n) for n in range(4)]
    a += [("o2t", n) for n in range(4)]
    d += [("out2",), ("x2t",), ("lg",)]
    a += [("sg", 0), ("sg", 1)]
    d += [("sh",), ("pos",)]
    d += [("pad", n) for n in range(-len(d) % RD)]
    a += [("pad", n) for n in range(-len(a) % RA)]
    assert len(o) % RO == 0
    return [{u: n for n, u in enumerate(r)} for r in (d, a, o)]


def build(nc, x, xT, ctxT, wall, bias, wout, wq, wkv, wo, gate, wgu, wdn, shgu, shdn, const, out):
    dn, an, on = plan()
    UD, UA, UO = len(dn), len(an), len(on)
    ctx = ExitStack()
    with ctx:
        def sb(name, shape, dt=F32):
            return ctx.enter_context(nc.sbuf_tensor(name, shape, dt))

        def sem(name):
            return ctx.enter_context(nc.semaphore(name))

        bank = [ctx.enter_context(nc.psum_tensor(f"bank{i}", [P, 512], F32)) for i in range(8)]
        slots = nc.dram_tensor("slots", [SLOTS + N * K, D], F32, kind="Internal").ap()
        expert_rows = nc.dram_tensor("expert_rows", [SLOTS, D], F32, kind="Internal").ap()

        def d_bank(*u):
            return bank[dn[u] % RD]

        def a_bank(*u):
            return bank[RD + an[u] % RA]

        def o_bank(*u):
            return bank[RD + RA + on[u] % RO]

        cst = sb("cst", [P, 3 * P + E + TT * K])
        ident, tri, mask = cst[:, 0:P], cst[:, P:2 * P], cst[:, 2 * P:3 * P]
        iota, spare0 = cst[:, 3 * P:3 * P + E], cst[:, 3 * P + E:]
        ident_b = sb("ident_b", [P, P], BF16)
        before_b = sb("before_b", [P, P], BF16)
        ones_b = sb("ones_b", [P, P], BF16)
        ones = sb("ones", [P, P])
        mask_s = sb("mask_s", [P, H, P], BF16)
        wall_s = sb("wall_s", [P, 2, 1024])
        bias_s = sb("bias_s", [P, 3 * D + 2 * D + H])
        bqkv, bout, bo = bias_s[:, 0:3 * D], bias_s[:, 3 * D:4 * D], bias_s[:, 4 * D:5 * D]
        bscale = bias_s[:, 5 * D:]
        sgn, nsgn, absb = sb("sgn", [P, H]), sb("nsgn", [P, H]), sb("absb", [P, H])
        wout_s = sb("wout_s", [P, 2, D])
        wq_s = sb("wq_s", [P, 2, XH * XD])
        wkv_s = sb("wkv_s", [CP, 2, 2 * XH * XD])
        wo_s = sb("wo_s", [P, 8, D])
        gate_s = sb("gate_s", [P, 2, E])
        shgu_s, shdn_s = sb("shgu_s", [P, 2, 2 * I]), sb("shdn_s", [P, D])
        powers = sb("powers", [P, 2 * TT * H])
        zero = sb("zero", [P, 1024])
        scratch, turn_p, turn_a = sb("scratch", [P, 64]), sb("turn_p", [P, 4]), sb("turn_a", [P, 4])

        xp = sb("xp", [P, 2, T + 1])
        xr = sb("xr", [P, TT, D])
        ct = sb("ct", [CP, 2, T])
        qr = sb("qr", [P, TT * H, 32])
        ka = sb("ka", [P, TT * H, 32])
        kb = sb("kb", [P, TT * H, 32])
        v = sb("v", [P, TT, D])
        lw = sb("lw", [P, 4, TT * 64])
        ll = sb("ll", [P, 2, TT * H, 6])
        sq = sb("sq", [P, 2 * TT * H, 6])
        ss = sb("ss", [P, 2 * TT * H])
        rn = sb("rn", [P, 2 * TT * H])
        rd = sb("rd", [P, TT * H, 6])
        oo = sb("oo", [P, TT, H * 36])
        mr = sb("mr", [P, TT * 2, 8 * 6, 6])
        pp = mr[:, :, :, :].rearrange("p a n c -> p (a n c)")[:, 0:2 * TT * H * 16].rearrange(
            "p (w h i k) -> p w h i k", w=2, i=4, k=4)
        rm = sb("rm", [P, TT * H, 6])
        qrt = sb("qrt", [P, GROUPS, T])
        kt = sb("kt", [P, 2, GROUPS, T])
        abnl = sb("abnl", [P, 2 * RING * 384])
        ab = abnl[:, 0:RING * 384].rearrange("p (r n) -> p r n", r=RING)
        nl = abnl[:, RING * 384:].rearrange("p (r n) -> p r n", r=RING)
        nm = sb("nm", [P, RING, TT])
        pr = sb("pr", [P, RING, 512])
        pt = sb("pt", [P, RING, 512])
        rs, ri = sb("rs", [P, TT, H]), sb("ri", [P, TT, H])
        oh = sb("oh", [P, TT, D])
        oht = sb("oht", [P, 2, T])
        y1 = sb("y1", [P, TT, D])
        st, mv, va, rv = sb("st", [P, TT, 6]), sb("mv", [P, TT, 2]), sb("va", [P, TT]), sb("rv", [P, TT])
        x1 = sb("x1", [P, TT, D])
        x1t = sb("x1t", [P, 2, T])
        qt = abnl[:, 0:8 * T].rearrange("p (c t) -> p c t", c=8)
        kt2 = sb("kt2", [P, 8, T])
        v2 = sb("v2", [P, TT, XH * XD])
        nm2 = sb("nm2", [P, RING, TT])
        rs2, ri2 = sb("rs2", [P, TT, XH]), sb("ri2", [P, TT, XH])
        o2 = sb("o2", [P, TT, XH * XD])
        o2t = kt[:, :, :, :].rearrange("p w g t -> p (w g) t")
        x2 = sb("x2", [P, TT, D])
        x2t = sb("x2t", [P, 2, T])
        lg, m8 = sb("lg", [P, TT, E]), sb("m8", [P, TT, 8])
        i8 = sb("i8", [P, TT, 8], U32)
        ix = sb("ix", [P, TT * K])
        nmx, ew, ws, wi = sb("nmx", [P, TT]), sb("ew", [P, TT, K]), sb("ws", [P, TT]), sb("wi", [P, TT])
        hot = sb("hot", [P, TT * K, E])
        hp = sb("hp", [P, TT * K, E])
        chosen = sb("chosen", [P, TT, E], BF16)
        before = sb("before", [P, E], BF16)
        ps, vd, fl, fd, gi = (sb(n, [P, TT * K]) for n in ("ps", "vd", "fl", "fd", "gi"))
        spare = sb("spare", [P, TT * K])
        slot_i = sb("slot_i", [P, TT * K], U32)
        sge, sgg, sgu, sgr = (mr[:, n, :, :].rearrange("p a c -> p (a c)")[:, 0:T] for n in range(4))
        sgh = sb("sgh", [P, T])
        base_all = sb("base_all", [P, B, TT, D])
        gates_all = sb("gates_all", [P, B, TT * K])
        rows_all = sb("rows_all", [P, B, TT * K], U32)

        we = sb("we", [P, 4, 2, 2 * I])
        wd = zero[:, :].rearrange("p (s n) -> p s n", s=4)
        xe = qt[:, :, :].rearrange("p (s c) n -> p s c n", c=2)
        xet = o2[:, :, :].rearrange("p j (a n) -> p (j a) n", n=CAP).rearrange("p (s c) n -> p s c n", c=2)
        ye = o2t[:, :, :].rearrange("p (s c) n -> p s c n", c=2)
        sl = v2[:, 0, :].rearrange("p (s n) -> p s n", s=4)
        he = v2[:, 1, :].rearrange("p (s n) -> p s n", s=4)
        gr = kt2[:, :, :].rearrange("p (s c) n -> p s c n", c=K)
        rows_s, gates_s = sb("rows_s", [P, 2, K], U32), sb("gates_s", [P, 2, K])
        acc, yo = y1, oh
        st3, mv3, va3, rv3 = sb("st3", [P, 2, 6]), sb("mv3", [P, 2, 2]), sb("va3", [P, 2]), sb("rv3", [P, 2])

        loaded, zeroed = sem("loaded"), sem("zeroed")
        prepared, pooled = sem("prepared"), sem("pooled")
        xt_loaded, xr_loaded, ctx_loaded = sem("xt_loaded"), sem("xr_loaded"), sem("ctx_loaded")
        xt_used, ctx_used = sem("xt_used"), sem("ctx_used")
        d_ready, d_done = sem("d_ready"), sem("d_done")
        a_ready, a_done = sem("a_ready"), sem("a_done")
        o_ready, o_done = sem("o_ready"), sem("o_done")
        vec_step = sem("vec_step")
        norms_asked, norms_done = sem("norms_asked"), sem("norms_done")
        outer_done, heads_ready = sem("outer_done"), sem("heads_ready")
        probs_ready = sem("probs_ready")
        x1_ready, rowmax_ready = sem("x1_ready"), sem("rowmax_ready")
        x2_ready, top_ready, ew_ready, chosen_ready = (sem("x2_ready"), sem("top_ready"), sem("ew_ready"),
                                                       sem("chosen_ready"))
        sge_ready, sgh_ready = sem("sge_ready"), sem("sgh_ready")
        slots_known, scattered, x2_free = sem("slots_known"), sem("scattered"), sem("x2_free")
        routed = sem("routed")
        ex_loaded = [sem(f"ex_loaded{s}") for s in range(4)]
        xet_ready, xet_done = sem("xet_ready"), sem("xet_done")
        gu_ready, sl_ready, he_ready = sem("gu_ready"), sem("sl_ready"), sem("he_ready")
        ye_ready, ye_done, ye_stored = sem("ye_ready"), sem("ye_done"), sem("ye_stored")
        picks_ready, gr_used = sem("picks_ready"), sem("gr_used")
        gathered = [sem(f"gathered{s}") for s in range(2)]
        var_ready, rstd_ready = sem("var_ready"), sem("rstd_ready")
        yo_ready, fin_step = sem("yo_ready"), sem("fin_step")
        stored = [sem(f"stored{s}") for s in range(2)]

        LOADS = 12
        block = ctx.enter_context(nc.Block())

        @block.sync
        def _(sp):
            for dst, src in (
                (cst[:, :], const),
                (wall_s[:, :, :], wall.rearrange("(k p) n -> p k n", p=P)),
                (bias_s[:, :], bias),
                (wkv_s[:, :, :], wkv.rearrange("(k p) n -> p k n", p=CP)),
                (wout_s[:, :, :], wout.rearrange("(k p) n -> p k n", p=P)),
                (wq_s[:, :, :], wq.rearrange("(k p) n -> p k n", p=P)),
                (wo_s[:, :, :], wo.rearrange("(k p) n -> p k n", p=P)),
                (gate_s[:, :, :], gate.rearrange("(k p) n -> p k n", p=P)),
                (shgu_s[:, :, :], shgu.rearrange("(k p) n -> p k n", p=P)),
                (shdn_s[:, :], shdn),
            ):
                sp.dma_start(dst, src).then_inc(loaded, 16)
            sp.wait_ge(prepared, 1)
            rows = 1024 // D
            for c in range(SLOTS // (P * rows)):
                sp.dma_start(slots[c * P * rows:(c + 1) * P * rows, :].rearrange("(p r) n -> p (r n)", p=P),
                             zero[:, :]).then_inc(zeroed, 16)
            with sp.Fori(0, B) as b:
                sp.wait_ge(xt_used, b + 1)
                sp.dma_start(xp[:, :, 1:T + 1], xT[bass.ds(b, 1), :, :].rearrange("o (k p) t -> p (o k) t", p=P)
                             ).then_inc(xt_loaded, 16)
                sp.wait_ge(ctx_used, b + 1)
                sp.dma_start(ct[:, :, :], ctxT[bass.ds(b, 1), :, :].rearrange("o (k p) t -> p (o k) t", p=CP)
                             ).then_inc(ctx_loaded, 16)
                sp.wait_ge(vec_step, VEC_STEPS * b + 2)
                sp.dma_start(xr[:, :, :], x[bass.ds(b, 1), :, :].rearrange("o (j p) n -> p (o j) n", p=P)
                             ).then_inc(xr_loaded, 16)

            def load_expert(e, s):
                sp.dma_start(we[:, s, :, :], wgu[e, :, :].rearrange("o (k p) n -> p (o k) n", p=P)
                             ).then_inc(ex_loaded[s], 16)
                sp.dma_start(wd[:, s, :], wdn[e, :, :].rearrange("o p n -> p (o n)")
                             ).then_inc(ex_loaded[s], 16)

            def load_slots(c, s):
                sp.dma_start(xe[:, s, :, :], slots[c, :].rearrange("(k p) n -> p k n", p=P)
                             ).then_inc(ex_loaded[s], 16)

            sp.wait_ge(zeroed, 16 * SLOTS * D // (P * 1024))
            for s in range(4):
                load_expert(slice(s, s + 1), s)
            sp.wait_ge(scattered, 16 * N * K // P)
            for s in range(4):
                load_slots(slice(s * CAP, (s + 1) * CAP), s)
            with sp.Fori(1, E // 4) as i:
                for s in range(4):
                    sp.wait_ge(ye_ready, 4 * i + (s - 3))
                    load_expert(bass.ds(4 * i + s, 1), s)
                    load_slots(bass.ds((4 * i + s) * CAP, CAP), s)
            with sp.Fori(0, N // P // 2) as i:
                for s in range(2):
                    sp.wait_ge(yo_ready, 2 * i + (s + 1))
                    sp.dma_start(out[bass.ds((2 * i + s) * P, P), :], yo[:, s, :]).then_inc(stored[s], 16)
            for s in range(2):
                sp.wait_ge(stored[s], 16 * (N // P // 2) + 16)

        @block.tensor
        def _(pe):
            pe.sem_inc(xt_used, 1)
            pe.sem_inc(ctx_used, 1)
            pe.wait_ge(loaded, 16 * 10)
            pe.wait_ge(prepared, 12)
            with pe.Fori(0, B) as b:
                ud, ua, uo = pe.snap(b * UD), pe.snap(b * UA), pe.snap(b * UO)
                b16 = pe.snap(b * 16)

                def d_free(*u):
                    pe.wait_ge(d_done, ud + (dn[u] + 1))

                def a_free(*u):
                    pe.wait_ge(a_done, ua + (an[u] + 1))

                def o_free(*u):
                    pe.wait_ge(o_done, uo + (on[u] + 1))

                pe.wait_ge(xt_loaded, 16 * b + 16)
                for j in range(TT):
                    d_free("g1", j)
                    for k in range(2):
                        mm = pe.matmul(d_bank("g1", j)[:, :], xp[:, k, 1 + j * P:1 + (j + 1) * P],
                                       wall_s[:, k, 0:512], start=(k == 0), stop=(k == 1))
                    mm.then_inc(d_ready, 1)
                    d_free("g2", j)
                    for k in range(2):
                        pe.matmul(d_bank("g2", j)[:, 0:448], xp[:, k, 1 + j * P:1 + (j + 1) * P],
                                  wall_s[:, k, 512:960], start=(k == 0), stop=(k == 1))
                    for k in range(2):
                        mm = pe.matmul(d_bank("g2", j)[:, 448:512], xp[:, k, j * P:(j + 1) * P],
                                       wall_s[:, k, 960:1024], start=(k == 0), stop=(k == 1))
                    mm.then_inc(d_ready, 1)
                pe.drain().then_inc(xt_used, 1)

                pe.wait_ge(ctx_loaded, 16 * b + 16)
                for n in range(4):
                    a_free("k", n)
                    for c in range(2):
                        cols = slice((2 * n + c) * P, (2 * n + c + 1) * P)
                        o = a_bank("k", n)[:, c * T:(c + 1) * T]
                        for k in range(2):
                            mm = pe.matmul(o, wkv_s[:, k, cols], ct[:, k, :], start=(k == 0), stop=(k == 1))
                    mm.then_inc(a_ready, 1)
                for n in range(4):
                    j, f = n // 2, n % 2
                    cols = slice(XH * XD + f * 512, XH * XD + (f + 1) * 512)
                    a_free("v", n)
                    for k in range(2):
                        mm = pe.matmul(a_bank("v", n)[:, :], ct[:, k, j * P:(j + 1) * P], wkv_s[:, k, cols],
                                       start=(k == 0), stop=(k == 1))
                    mm.then_inc(a_ready, 1)
                pe.drain().then_inc(ctx_used, 1)

                for j in range(TT):
                    pe.wait_ge(outer_done, 2 * b + (j + 1))
                    for f in range(2):
                        d_free("m", j, f)
                        o, cols = d_bank("m", j, f)[:, 0:288], slice(f * 288, (f + 1) * 288)
                        for i in range(j):
                            pe.matmul(o, ones[:, :], oo[:, i, cols], start=(i == 0), stop=False)
                        pe.matmul(o, tri, oo[:, j, cols], start=(j == 0), stop=True).then_inc(d_ready, 1)

                pe.wait_ge(heads_ready, b + 1)
                for w, src in enumerate((qr, ka, kb)):
                    for j in range(TT):
                        a_free("t", w, j)
                        for g in range(GROUPS):
                            r = j * H + 4 * g
                            mm = pe.transpose(a_bank("t", w, j)[:, g * P:(g + 1) * P],
                                              src[:, r:r + 4, :].rearrange("p a c -> p (a c)"), ident)
                        mm.then_inc(a_ready, 1)
                pe.wait_ge(a_done, ua + (an["t", 2, TT - 1] + 1 + RA))

                def scores(h):
                    g, r = h // 4, 32 * (h % 4)
                    sx, sy = d_bank("x", h), a_bank("y", h)
                    d_free("x", h)
                    for j in range(TT):
                        lhs = qrt[r:r + 32, g, j * P:(j + 1) * P]
                        cols = slice(0, P) if j == 0 else slice(P, 3 * P)
                        pe.matmul(sx[:, cols], lhs, kt[r:r + 32, 0, g, 0:(j + 1) * P], start=True, stop=False)
                        mm = pe.matmul(sx[:, 2 * j * P:(2 * j + 1) * P], ident_b[:, :], mask_s[:, h, :],
                                       start=False, stop=True)
                    mm.then_inc(d_ready, 1)
                    a_free("y", h)
                    for j in range(TT):
                        lhs = qrt[r:r + 32, g, j * P:(j + 1) * P]
                        cols = slice(0, P) if j == 0 else slice(P, 3 * P)
                        mm = pe.matmul(sy[:, cols], lhs, kt[r:r + 32, 1, g, 0:(j + 1) * P], start=True, stop=True)
                    mm.then_inc(a_ready, 1)

                def turn(h):
                    pe.wait_ge(probs_ready, b16 + (h + 1))
                    d_free("pt", h)
                    for c in range(3):
                        mm = pe.transpose(d_bank("pt", h)[:, c * P:(c + 1) * P],
                                          pr[:, h % RING, c * P:(c + 1) * P], ident)
                    mm.then_inc(d_ready, 1)

                def values(h):
                    pe.wait_ge(d_done, ud + (dn["pt", h] + 1 + RD))
                    if h % 8 == 0:
                        o_free("o", h // 8)
                    for j in range(TT):
                        o = o_bank("o", h // 8)[:, j * P + (h % 8) * DH:j * P + (h % 8 + 1) * DH]
                        for i in range(j + 1):
                            mm = pe.matmul(o, pt[:, h % RING, (j + i) * P:(j + i + 1) * P],
                                           v[:, i, h * DH:(h + 1) * DH], start=(i == 0), stop=(i == j))
                    if h % 8 == 7:
                        mm.then_inc(o_ready, 1)

                for h in range(-LOOK, H + 1):
                    if h + LOOK < H:
                        scores(h + LOOK)
                    if 0 <= h < H:
                        turn(h)
                    if h >= 1:
                        values(h - 1)

                pe.wait_ge(o_done, uo + (on["o", 1] + 1 + RO))
                a_free("ot")
                for j in range(TT):
                    for k in range(2):
                        mm = pe.transpose(a_bank("ot")[:, k * T + j * P:k * T + (j + 1) * P],
                                          oh[:, j, k * P:(k + 1) * P], ident)
                mm.then_inc(a_ready, 1)
                pe.wait_ge(a_done, ua + (an["ot",] + 1 + RA))
                d_free("out")
                for j in range(TT):
                    for k in range(2):
                        mm = pe.matmul(d_bank("out")[:, j * D:(j + 1) * D], oht[:, k, j * P:(j + 1) * P],
                                       wout_s[:, k, :], start=(k == 0), stop=(k == 1))
                mm.then_inc(d_ready, 1)

                pe.wait_ge(x1_ready, 2 * b + 2)
                d_free("x1t")
                for j in range(TT):
                    for k in range(2):
                        mm = pe.transpose(d_bank("x1t")[:, k * T + j * P:k * T + (j + 1) * P],
                                          x1[:, j, k * P:(k + 1) * P], ident)
                mm.then_inc(d_ready, 1)
                pe.wait_ge(d_done, ud + (dn["x1t",] + 1 + RD))
                for n in range(4):
                    a_free("q", n)
                    for c in range(2):
                        for k in range(2):
                            mm = pe.matmul(a_bank("q", n)[:, c * T:(c + 1) * T],
                                           wq_s[:, k, (2 * n + c) * P:(2 * n + c + 1) * P], x1t[:, k, :],
                                           start=(k == 0), stop=(k == 1))
                    mm.then_inc(a_ready, 1)

                def scores2(h):
                    r, c = XD * (h % 2), h // 2
                    if c % 2 == 0 and h % 2 == 0:
                        pe.wait_ge(a_done, ua + (an["q", h // 4] + 1 + RA))
                    a_free("s", h)
                    for j in range(TT):
                        mm = pe.matmul(a_bank("s", h)[:, j * T:(j + 1) * T], qt[r:r + XD, c, j * P:(j + 1) * P],
                                       kt2[r:r + XD, c, :], start=True, stop=True)
                    mm.then_inc(a_ready, 1)

                def turn2(h):
                    pe.wait_ge(a_done, ua + (an["s", h] + 1 + RA))
                    d_free("pt2", h)
                    for j in range(TT):
                        for i in range(TT):
                            mm = pe.transpose(d_bank("pt2", h)[:, i * T + j * P:i * T + (j + 1) * P],
                                              pr[:, h % RING, j * T + i * P:j * T + (i + 1) * P], ident)
                    mm.then_inc(d_ready, 1)

                def values2(h):
                    pe.wait_ge(d_done, ud + (dn["pt2", h] + 1 + RD))
                    if h % 4 == 0:
                        o_free("o2", h // 4)
                    for j in range(TT):
                        o = o_bank("o2", h // 4)[:, j * T + (h % 4) * XD:j * T + (h % 4 + 1) * XD]
                        for i in range(TT):
                            mm = pe.matmul(o, pt[:, h % RING, i * T + j * P:i * T + (j + 1) * P],
                                           v2[:, i, h * XD:(h + 1) * XD], start=(i == 0), stop=(i == 1))
                    if h % 4 == 3:
                        mm.then_inc(o_ready, 1)

                for h in range(-LOOK, XH + 1):
                    if h + LOOK < XH:
                        scores2(h + LOOK)
                    if 0 <= h < XH:
                        turn2(h)
                    if h >= 1:
                        values2(h - 1)

                for n in range(4):
                    pe.wait_ge(o_done, uo + (on["o2", n] + 1 + RO))
                    a_free("o2t", n)
                    for c in range(2):
                        for j in range(TT):
                            mm = pe.transpose(a_bank("o2t", n)[:, c * T + j * P:c * T + (j + 1) * P],
                                              o2[:, j, (2 * n + c) * P:(2 * n + c + 1) * P], ident)
                    mm.then_inc(a_ready, 1)
                pe.wait_ge(a_done, ua + (an["o2t", 3] + 1 + RA))
                d_free("out2")
                for j in range(TT):
                    for k in range(8):
                        mm = pe.matmul(d_bank("out2")[:, j * D:(j + 1) * D], o2t[:, k, j * P:(j + 1) * P],
                                       wo_s[:, k, :], start=(k == 0), stop=(k == 7))
                mm.then_inc(d_ready, 1)

                pe.wait_ge(x2_ready, 2 * b + 2)
                d_free("x2t")
                for j in range(TT):
                    for k in range(2):
                        mm = pe.transpose(d_bank("x2t")[:, k * T + j * P:k * T + (j + 1) * P],
                                          x2[:, j, k * P:(k + 1) * P], ident)
                mm.then_inc(d_ready, 1)
                pe.wait_ge(d_done, ud + (dn["x2t",] + 1 + RD))
                d_free("lg")
                for j in range(TT):
                    for k in range(2):
                        mm = pe.matmul(d_bank("lg")[:, j * E:(j + 1) * E], x2t[:, k, j * P:(j + 1) * P],
                                       gate_s[:, k, :], start=(k == 0), stop=(k == 1))
                mm.then_inc(d_ready, 1)
                for c in range(2):
                    a_free("sg", c)
                    for k in range(2):
                        mm = pe.matmul(a_bank("sg", c)[:, 0:T], shgu_s[:, k, c * I:(c + 1) * I], x2t[:, k, :],
                                       start=(k == 0), stop=(k == 1))
                    mm.then_inc(a_ready, 1)
                pe.wait_ge(sgh_ready, b + 1)
                d_free("sh")
                for j in range(TT):
                    mm = pe.matmul(d_bank("sh")[:, j * D:(j + 1) * D], sgh[:, j * P:(j + 1) * P], shdn_s[:, :],
                                   start=True, stop=True)
                mm.then_inc(d_ready, 1)
                pe.wait_ge(chosen_ready, b + 1)
                d_free("pos")
                for j in range(TT):
                    o = d_bank("pos")[:, j * E:(j + 1) * E]
                    pe.matmul(o, ones_b[:, :], before[:, :], start=True, stop=False)
                    for i in range(j):
                        pe.matmul(o, ones_b[:, :], chosen[:, i, :], start=False, stop=False)
                    mm = pe.matmul(o, before_b[:, :], chosen[:, j, :], start=False, stop=True)
                mm.then_inc(d_ready, 1)

            pe.wait_ge(d_done, B * UD + RD)
            pe.wait_ge(a_done, B * UA + RA)
            pe.wait_ge(o_done, B * UO + RO)
            with pe.Fori(0, E // 4) as i:
                i4, i48 = pe.snap(4 * i), pe.snap(48 * i)

                def turn_slots(s):
                    pe.wait_ge(ex_loaded[s], i48 + 48)
                    pe.wait_ge(xet_done, i4 + (s + 1))
                    for k in range(2):
                        for c in range(2):
                            mm = pe.transpose(bank[s % 2][:, k * CAP + c * P:k * CAP + (c + 1) * P],
                                              xe[:, s, c, k * P:(k + 1) * P], ident)
                    mm.then_inc(xet_ready, 1)

                def gate_up(s):
                    pe.wait_ge(xet_done, i4 + (s + 3))
                    pe.wait_ge(he_ready, i4 + (s + 1))
                    for c in range(2):
                        for k in range(2):
                            mm = pe.matmul(bank[2 + s % 2][:, c * CAP:(c + 1) * CAP],
                                           we[:, s, k, c * I:(c + 1) * I], xet[:, s, k, :],
                                           start=(k == 0), stop=(k == 1))
                    mm.then_inc(gu_ready, 1)

                def down(s):
                    pe.wait_ge(he_ready, i4 + (s + 3))
                    pe.wait_ge(ye_done, i4 + (s + 1))
                    for c in range(2):
                        mm = pe.matmul(bank[4 + s % 2][:, c * D:(c + 1) * D], he[:, s, c * P:(c + 1) * P],
                                       wd[:, s, :], start=True, stop=True)
                    mm.then_inc(ye_ready, 1)

                for s in range(6):
                    if s < 4:
                        turn_slots(s)
                    if 1 <= s < 5:
                        gate_up(s - 1)
                    if s >= 2:
                        down(s - 2)

        @block.scalar
        def _(act):
            act.wait_ge(prepared, 12)
            for r in range(RA):
                nc.scalar.copy(turn_a[:, r:r + 1], ident[:, 0:1]).then_inc(a_done, 1)
            with act.Fori(0, B) as b:
                ua, ud = act.snap(b * UA), act.snap(b * UD)
                b16 = act.snap(b * 16)

                def ready(*u):
                    act.wait_ge(a_ready, ua + (an[u] + 1))

                for n in range(4):
                    ready("k", n)
                    nc.scalar.copy(kt2[:, 2 * n:2 * n + 2, :].rearrange("p c t -> p (c t)"), a_bank("k", n)[:, :]
                                   ).then_inc(a_done, 1)
                for n in range(4):
                    ready("v", n)
                    nc.scalar.copy(v2[:, n // 2, n % 2 * 512:(n % 2 + 1) * 512], a_bank("v", n)[:, :]
                                   ).then_inc(a_done, 1)
                for w in range(3):
                    for j in range(TT):
                        dst = qrt[:, :, :] if w == 0 else kt[:, w - 1, :, :]
                        ready("t", w, j)
                        nc.scalar.copy(dst[:, :, j * P:(j + 1) * P],
                                       a_bank("t", w, j)[:, :].rearrange("p (g t) -> p g t", g=GROUPS)
                                       ).then_inc(a_done, 1)

                def absolute(h):
                    ready("y", h)
                    nc.scalar.activation(ab[:, h % RING, :], a_bank("y", h)[:, 0:384], ACT.Abs
                                         ).then_inc(a_done, 1)

                def exps(h):
                    act.wait_ge(d_done, ud + (dn["x", h] + 1 + RD))
                    for j in range(TT):
                        cols = slice(0, P) if j == 0 else slice(P, 3 * P)
                        ins = nc.scalar.activation(pr[:, h % RING, cols], nl[:, h % RING, cols], ACT.Exp,
                                                   bias=nm[:, h % RING, j:j + 1], scale=-1.0,
                                                   accum_out=rs[:, j, h:h + 1])
                    ins.then_inc(probs_ready, 1)

                for h in range(-1, H):
                    if h + 1 < H:
                        absolute(h + 1)
                    if h >= 0:
                        exps(h)

                ready("ot")
                nc.scalar.copy(oht[:, :, :].rearrange("p k t -> p (k t)"), a_bank("ot")[:, :]
                               ).then_inc(a_done, 1)
                for n in range(4):
                    ready("q", n)
                    nc.scalar.copy(qt[:, 2 * n:2 * n + 2, :].rearrange("p c t -> p (c t)"), a_bank("q", n)[:, :]
                                   ).then_inc(a_done, 1)
                for h in range(XH):
                    act.wait_ge(rowmax_ready, b16 + (h + 1))
                    for j in range(TT):
                        ins = nc.scalar.activation(pr[:, h % RING, j * T:(j + 1) * T],
                                                   a_bank("s", h)[:, j * T:(j + 1) * T], ACT.Exp,
                                                   bias=nm2[:, h % RING, j:j + 1], scale=1.0,
                                                   accum_out=rs2[:, j, h:h + 1])
                    ins.then_inc(a_done, 1)
                for n in range(4):
                    ready("o2t", n)
                    nc.scalar.copy(o2t[:, 2 * n:2 * n + 2, :].rearrange("p c t -> p (c t)"),
                                   a_bank("o2t", n)[:, :]).then_inc(a_done, 1)
                ready("sg", 0)
                nc.scalar.activation(sge[:, :], a_bank("sg", 0)[:, 0:T], ACT.Exp, scale=-1.0
                                     ).then_inc(sge_ready, 1)
                nc.scalar.copy(sgg[:, :], a_bank("sg", 0)[:, 0:T]).then_inc(a_done, 1)
                ready("sg", 1)
                nc.scalar.copy(sgu[:, :], a_bank("sg", 1)[:, 0:T]).then_inc(a_done, 1)
                act.wait_ge(top_ready, b + 1)
                for j in range(TT):
                    ins = nc.scalar.activation(ew[:, j, :], m8[:, j, 0:K], ACT.Exp, bias=nmx[:, j:j + 1],
                                               scale=1.0, accum_out=ws[:, j:j + 1])
                ins.then_inc(ew_ready, 1)
                for n in range(UA - 1 - an["sg", 1]):
                    nc.scalar.copy(turn_a[:, n:n + 1], ident[:, 0:1]).then_inc(a_done, 1)

            act.sem_inc(ye_done, 2)
            act.sem_inc(ye_stored, 16)
            with act.Fori(0, E // 4) as i:
                i4, i64 = act.snap(4 * i), act.snap(64 * i)

                def silu(s):
                    act.wait_ge(gu_ready, i4 + (s + 1))
                    nc.scalar.activation(sl[:, s, :], bank[2 + s % 2][:, 0:CAP], ACT.Silu).then_inc(sl_ready, 1)

                def rows_out(s):
                    if s == 0:
                        act.wait_ge(ye_stored, i64 + 16)
                    act.wait_ge(ye_ready, i4 + (s + 1))
                    nc.scalar.copy(ye[:, s, :, :].rearrange("p c n -> p (c n)"), bank[4 + s % 2][:, :]
                                   ).then_inc(ye_done, 1)
                    act.wait_ge(ye_done, i4 + (s + 3))
                    act.dma_start(expert_rows[bass.ds((4 * i + s) * CAP, CAP), :].rearrange("(c p) n -> p c n", p=P),
                                  ye[:, s, :, :]).then_inc(ye_stored, 16)

                for s in range(5):
                    if s < 4:
                        silu(s)
                    if s >= 1:
                        rows_out(s - 1)

        @block.gpsimd
        def _(pool):
            pool.sem_inc(x2_free, 1)
            pool.memset(powers[:, :], -0.5).then_inc(pooled, 1)
            pool.wait_ge(pooled, 1)
            pool.wait_ge(zeroed, 16 * SLOTS * D // (P * 1024))
            with pool.Fori(0, B) as b:
                def power(n, dst, src, cols):
                    pool.wait_ge(norms_asked, 3 * b + (n + 1))
                    pool.tensor_tensor(dst, src, powers[:, 0:cols], ALU.pow).then_inc(norms_done, 1)

                power(0, rn[:, :], ss[:, :], 2 * TT * H)
                power(1, rv[:, :], va[:, :], TT)
                power(2, rv[:, :], va[:, :], TT)
                pool.wait_ge(slots_known, b + 1)
                pool.tensor_tensor(turn_p[:, 0:1], powers[:, 0:1], powers[:, 0:1], ALU.mult)
                for j in range(TT):
                    for k in range(K):
                        c = j * K + k
                        pool.indirect_dma_start(
                            out=slots[:, :], out_offset=bass.IndirectOffsetOnAxis(ap=slot_i[:, c:c + 1], axis=0),
                            in_=x2[:, j, :], in_offset=None).then_inc(scattered, 16)
                pool.wait_ge(scattered, 16 * TT * K * b + 16 * TT * K)
                pool.tensor_tensor(turn_p[:, 3:4], powers[:, 0:1], powers[:, 0:1], ALU.mult).then_inc(x2_free, 1)
            pool.wait_ge(ye_stored, 16 * E + 16)
            with pool.Fori(0, N // P // 2) as i:
                for s in range(2):
                    pool.wait_ge(picks_ready, 2 * i + (s + 1))
                    pool.tensor_tensor(turn_p[:, 1 + s:2 + s], powers[:, 0:1], powers[:, 0:1], ALU.mult)
                    for k in range(K):
                        pool.indirect_dma_start(
                            out=gr[:, s, k, :], out_offset=None, in_=expert_rows[:, :],
                            in_offset=bass.IndirectOffsetOnAxis(ap=rows_s[:, s, k:k + 1], axis=0),
                        ).then_inc(gathered[s], 16)
                for s in range(2):
                    pool.wait_ge(var_ready, 2 * i + (s + 1))
                    pool.tensor_tensor(rv3[:, s:s + 1], va3[:, s:s + 1], powers[:, 0:1], ALU.pow
                                       ).then_inc(rstd_ready, 1)

        @block.vector
        def _(dve):
            steps = [0]

            def after(ins, sem_, at):
                ins.then_inc(sem_, 1)
                dve.wait_ge(sem_, at)

            nc.vector.memset(zero[:, :], 0.0).then_inc(prepared, 1)
            for t in (qr, ka, kb):
                nc.vector.memset(t[:, :, :], 0.0)
            nc.vector.memset(xp[:, :, 0:1], 0.0).then_inc(vec_step, 1)
            nc.vector.memset(before[:, :], 0.0).then_inc(vec_step, 1)
            nc.vector.memset(ones[:, :], 1.0).then_inc(prepared, 1)
            nc.vector.memset(ones_b[:, :], 1.0).then_inc(prepared, 1)
            dve.wait_ge(loaded, 16 * 10)
            nc.vector.tensor_copy(ident_b[:, :], ident).then_inc(prepared, 1)
            nc.vector.tensor_tensor(before_b[:, :], tri, ident, ALU.subtract).then_inc(prepared, 1)
            nc.vector.tensor_copy(spare[:, :], spare0).then_inc(prepared, 1)
            nc.vector.tensor_scalar(sgn[:, :], bscale, 0.0, 2.0, ALU.is_ge, ALU.mult).then_inc(prepared, 1)
            dve.wait_ge(prepared, 7)
            after(nc.vector.tensor_scalar(sgn[:, :], sgn[:, :], -1.0, None, ALU.add), prepared, 8)
            nc.vector.tensor_scalar(nsgn[:, :], sgn[:, :], -1.0, None, ALU.mult)
            nc.vector.tensor_tensor(absb[:, :], bscale, sgn[:, :], ALU.mult)
            sg3 = sgn[:, :].unsqueeze(2).to_broadcast([P, H, DH])
            for w in (wall_s[:, 0, 0:D], wall_s[:, 1, 0:D], bqkv[:, 0:D]):
                w3 = w.rearrange("p (h d) -> p h d", d=DH)
                ins = nc.vector.scalar_tensor_tensor(out=w3, in0=w3, scalar=float(DH) ** -0.5, in1=sg3,
                                                     op0=ALU.mult, op1=ALU.mult)
            ins.then_inc(prepared, 1)
            nc.vector.tensor_scalar(wq_s[:, :, :], wq_s[:, :, :], float(XD) ** -0.5, None, ALU.mult
                                    ).then_inc(prepared, 1)
            for h in range(H):
                ins = nc.vector.tensor_scalar(mask_s[:, h, :], mask, sgn[:, h:h + 1], None, ALU.mult)
            ins.then_inc(prepared, 1)
            nc.vector.memset(nm[:, :, :], 0.0).then_inc(prepared, 1)
            dve.wait_ge(prepared, 12)
            for r in range(RD):
                nc.vector.memset(scratch[:, 3 + r:4 + r], 0.0).then_inc(d_done, 1)
            for r in range(RO):
                nc.vector.memset(scratch[:, 6 + r:7 + r], 0.0).then_inc(o_done, 1)

            with dve.Fori(0, B) as b:
                ud, ua, uo = dve.snap(b * UD), dve.snap(b * UA), dve.snap(b * UO)
                vs = dve.snap(b * VEC_STEPS)
                steps[0] = 2

                def step(ins, carry=False):
                    steps[0] += 1
                    ins.then_inc(vec_step, 1)
                    dve.wait_ge(vec_step, vs + steps[0])
                    if carry:
                        nc.vector.memset(scratch[:, 11:12], 0.0)

                def ready(*u):
                    dve.wait_ge(d_ready, ud + (dn[u] + 1))

                def tt(o, a, c, op):
                    return nc.vector.tensor_tensor(o, a, c, op)

                for j in range(TT):
                    hs = slice(j * H, (j + 1) * H)
                    ready("g1", j)
                    g1 = d_bank("g1", j)
                    tt(qr[:, hs, 0:DH], g1[:, 0:D].rearrange("p (h d) -> p h d", d=DH),
                       bqkv[:, 0:D].rearrange("p (h d) -> p h d", d=DH), ALU.add)
                    tt(ka[:, hs, 0:DH], g1[:, D:2 * D].rearrange("p (h d) -> p h d", d=DH),
                       bqkv[:, D:2 * D].rearrange("p (h d) -> p h d", d=DH), ALU.add).then_inc(d_done, 1)
                    ready("g2", j)
                    g2 = d_bank("g2", j)
                    tt(v[:, j, :], g2[:, 0:D], bqkv[:, 2 * D:3 * D], ALU.add)
                    nc.vector.tensor_copy(lw[:, :, j * 64:(j + 1) * 64],
                                          g2[:, D:2 * D].rearrange("p (c n) -> p c n", c=4)).then_inc(d_done, 1)
                dve.wait_ge(d_done, ud + (dn["g2", TT - 1] + 1 + RD))

                def points(c):
                    return lw[:, c, :].rearrange("p (h i) -> p h i", i=4)

                wide = [P, TT * H, 4, 4]
                for w, (p1, p2) in enumerate(((3, 0), (1, 2))):
                    tt(pp[:, w, :, :, :], points(p1).unsqueeze(3).to_broadcast(wide),
                       points(p2).unsqueeze(2).to_broadcast(wide), ALU.mult)
                    if w:
                        step(nc.vector.memset(scratch[:, 12:13], 0.0))
                for c, (i, k) in enumerate(((2, 3), (3, 1), (1, 2), (0, 3), (2, 0), (0, 1))):
                    tt(ll[:, 0, :, c:c + 1], pp[:, 0, :, i, k:k + 1], pp[:, 0, :, k, i:i + 1], ALU.subtract)
                for c, i, n in ((0, 0, 3), (3, 1, 2), (5, 2, 1)):
                    ins = tt(ll[:, 1, :, c:c + n], pp[:, 1, :, i, i + 1:i + 1 + n],
                             pp[:, 1, :, i + 1:i + 1 + n, i], ALU.subtract)
                step(ins)
                lf = ll[:, :, :, :].rearrange("p w h c -> p (w h) c")
                step(tt(sq[:, :, :], lf, lf, ALU.mult))
                step(nc.vector.tensor_reduce(ss[:, :], sq[:, :, :], X, ALU.add))
                nc.vector.tensor_scalar(ss[:, :], ss[:, :], 1e-24, None, ALU.max).then_inc(norms_asked, 1)
                dve.wait_ge(norms_done, 3 * b + 1)
                half = TT * H
                tt(kb[:, :, DH:DH + 6], ll[:, 0, :, :], rn[:, 0:half].unsqueeze(2).to_broadcast([P, half, 6]),
                   ALU.mult)
                step(tt(rd[:, :, :], ll[:, 1, :, :],
                        rn[:, half:2 * half].unsqueeze(2).to_broadcast([P, half, 6]), ALU.mult))
                for j in range(TT):
                    jw = kb[:, j * H:(j + 1) * H, DH:DH + 6]
                    tt(oo[:, j, :].rearrange("p (h a c) -> p h a c", a=6, c=6),
                       jw.unsqueeze(3).to_broadcast([P, H, 6, 6]), jw.unsqueeze(2).to_broadcast([P, H, 6, 6]),
                       ALU.mult).then_inc(outer_done, 1)
                for j in range(TT):
                    for f in range(2):
                        h0 = j * H + f * 8
                        ready("m", j, f)
                        tt(mr[:, 2 * j + f, :, :].rearrange("p (h a) c -> p h a c", a=6),
                           d_bank("m", j, f)[:, 0:288].rearrange("p (h a c) -> p h a c", a=6, c=6),
                           rd[:, h0:h0 + 8, :].unsqueeze(2).to_broadcast([P, 8, 6, 6]), ALU.mult
                           ).then_inc(d_done, 1)
                dve.wait_ge(d_done, ud + (dn["m", TT - 1, 1] + 1 + RD))
                step(nc.vector.tensor_reduce(rm[:, :, :].rearrange("p h c -> p (h c)"),
                                             mr[:, :, :, :].rearrange("p a n c -> p (a n) c"), X, ALU.add))
                for j in range(TT):
                    hs = slice(j * H, (j + 1) * H)
                    ins = tt(qr[:, hs, DH:DH + 6], rm[:, hs, :], absb[:, :].unsqueeze(2).to_broadcast([P, H, 6]),
                             ALU.mult)
                ins.then_inc(heads_ready, 1)

                def logits(h):
                    ready("x", h)
                    dve.wait_ge(a_done, ua + (an["y", h] + 1 + RA))
                    nc.vector.memset(scratch[:, 32 + h:33 + h], 0.0)
                    for j in range(TT):
                        cols = slice(0, P) if j == 0 else slice(P, 3 * P)
                        ins = nc.vector.tensor_tensor_reduce(
                            out=nl[:, h % RING, cols], in0=ab[:, h % RING, cols], in1=d_bank("x", h)[:, cols],
                            scale=nsgn[:, h:h + 1], scalar=3e38, op0=ALU.add, op1=ALU.min,
                            accum_out=nm[:, h % RING, j:j + 1])
                    ins.then_inc(d_done, 1)

                for h in range(-LOOK, H):
                    if h + LOOK < H:
                        logits(h + LOOK)
                    if h >= 0:
                        ready("pt", h)
                        nc.vector.tensor_copy(pt[:, h % RING, 0:384], d_bank("pt", h)[:, 0:384]
                                              ).then_inc(d_done, 1)
                step(nc.vector.reciprocal(ri[:, :, :], rs[:, :, :]))
                for f in range(2):
                    dve.wait_ge(o_ready, uo + (on["o", f] + 1))
                    ins = tt(oh[:, :, f * P:(f + 1) * P].rearrange("p j (h d) -> p j h d", d=DH),
                             o_bank("o", f)[:, 0:256].rearrange("p (j h d) -> p j h d", j=TT, d=DH),
                             ri[:, :, f * 8:(f + 1) * 8].unsqueeze(3).to_broadcast([P, TT, 8, DH]), ALU.mult)
                    ins.then_inc(o_done, 1)

                def norm(src, dst, asked, ready_sem):
                    for j in range(TT):
                        ins = nc.vector.bn_stats(st[:, j, :], src[:, j, :])
                    step(ins, carry=True)
                    for j in range(TT):
                        ins = nc.vector.bn_aggr(mv[:, j, :], st[:, j, :])
                    step(ins)
                    nc.vector.tensor_scalar(va[:, :], mv[:, :, 1], EPS, None, ALU.add).then_inc(norms_asked, 1)
                    dve.wait_ge(norms_done, 3 * b + (asked + 1))
                    for j in range(TT):
                        nc.vector.tensor_scalar(dst[:, j, :], src[:, j, :], mv[:, j, 0:1], rv[:, j:j + 1],
                                                ALU.subtract, ALU.mult).then_inc(ready_sem, 1)

                flat = "p j n -> p (j n)"
                ready("out")
                dve.wait_ge(xr_loaded, 16 * b + 16)
                ins = tt(y1[:, :, :].rearrange(flat), d_bank("out")[:, :], xr[:, :, :].rearrange(flat), ALU.add)
                ins.then_inc(d_done, 1)
                dve.wait_ge(d_done, ud + (dn["out",] + 1 + RD))
                step(tt(y1[:, :, :], y1[:, :, :], bout.unsqueeze(1).to_broadcast([P, TT, D]), ALU.add))
                norm(y1, x1, 1, x1_ready)
                ready("x1t")
                nc.vector.tensor_copy(x1t[:, :, :].rearrange("p k t -> p (k t)"), d_bank("x1t")[:, :]
                                      ).then_inc(d_done, 1)

                def rowmax(h):
                    dve.wait_ge(a_ready, ua + (an["s", h] + 1))
                    nc.vector.tensor_reduce(nm2[:, h % RING, :], a_bank("s", h)[:, :].rearrange(
                        "p (j t) -> p j t", j=TT), X, ALU.max, negate=True).then_inc(rowmax_ready, 1)

                def outputs2(n):
                    hs = slice(4 * n, 4 * n + 4)
                    step(nc.vector.reciprocal(ri2[:, :, hs], rs2[:, :, hs]))
                    dve.wait_ge(o_ready, uo + (on["o2", n] + 1))
                    tt(o2[:, :, n * T:(n + 1) * T].rearrange("p j (h d) -> p j h d", d=XD),
                       o_bank("o2", n)[:, :].rearrange("p (j h d) -> p j h d", j=TT, d=XD),
                       ri2[:, :, hs].unsqueeze(3).to_broadcast([P, TT, 4, XD]), ALU.mult).then_inc(o_done, 1)

                for h in range(-LOOK, XH):
                    if h + LOOK < XH:
                        rowmax(h + LOOK)
                    if h >= 0:
                        ready("pt2", h)
                        nc.vector.tensor_copy(pt[:, h % RING, :], d_bank("pt2", h)[:, :]).then_inc(d_done, 1)
                    if h >= 4 and h % 4 == 1:
                        outputs2(h // 4 - 1)
                outputs2(3)
                ready("out2")
                tt(y1[:, :, :].rearrange(flat), d_bank("out2")[:, :], x1[:, :, :].rearrange(flat), ALU.add
                   ).then_inc(d_done, 1)
                dve.wait_ge(d_done, ud + (dn["out2",] + 1 + RD))
                step(tt(y1[:, :, :], y1[:, :, :], bo.unsqueeze(1).to_broadcast([P, TT, D]), ALU.add))
                dve.wait_ge(x2_free, b + 1)
                norm(y1, x2, 2, x2_ready)
                ready("x2t")
                nc.vector.tensor_copy(x2t[:, :, :].rearrange("p k t -> p (k t)"), d_bank("x2t")[:, :]
                                      ).then_inc(d_done, 1)

                ready("lg")
                nc.vector.tensor_copy(lg[:, :, :].rearrange("p j e -> p (j e)"), d_bank("lg")[:, 0:TT * E]
                                      ).then_inc(d_done, 1)
                dve.wait_ge(d_done, ud + (dn["lg",] + 1 + RD))
                nc.vector.memset(scratch[:, 17:18], 0.0)
                for j in range(TT):
                    ins = nc.vector.max(m8[:, j, :], lg[:, j, :])
                step(ins)
                nc.vector.tensor_scalar(nmx[:, :], m8[:, :, 0], -1.0, None, ALU.mult).then_inc(top_ready, 1)
                for j in range(TT):
                    ins = nc.vector.max_index(i8[:, j, :], m8[:, j, :], lg[:, j, :])
                step(ins)
                step(nc.vector.tensor_copy(ix[:, :].rearrange("p (j k) -> p j k", k=K), i8[:, :, 0:K]))
                many = [P, TT * K, E]
                step(tt(hot[:, :, :], iota.unsqueeze(1).to_broadcast(many), ix[:, :].unsqueeze(2).to_broadcast(many),
                        ALU.is_equal))
                for j in range(TT):
                    ins = nc.vector.tensor_reduce(
                        chosen[:, j, :], hot[:, j * K:(j + 1) * K, :].rearrange("p k e -> p e k"), X, ALU.max)
                ins.then_inc(chosen_ready, 1)

                dve.wait_ge(sge_ready, b + 1)
                step(nc.vector.tensor_scalar(sge[:, :], sge[:, :], 1.0, None, ALU.add))
                step(nc.vector.reciprocal(sgr[:, :], sge[:, :]))
                dve.wait_ge(a_done, ua + (an["sg", 1] + 1 + RA))
                step(tt(sgr[:, :], sgr[:, :], sgg[:, :], ALU.mult))
                tt(sgh[:, :], sgr[:, :], sgu[:, :], ALU.mult).then_inc(sgh_ready, 1)
                ready("sh")
                tt(base_all[:, bass.ds(b, 1), :, :].rearrange("p o j n -> p (o j n)"), d_bank("sh")[:, :],
                   x2[:, :, :].rearrange(flat), ALU.add).then_inc(d_done, 1)

                ready("pos")
                for j in range(TT):
                    ks = slice(j * K, (j + 1) * K)
                    ins = tt(hp[:, ks, :], hot[:, ks, :], d_bank("pos")[:, j * E:(j + 1) * E].unsqueeze(1)
                             .to_broadcast([P, K, E]), ALU.mult)
                ins.then_inc(d_done, 1)
                dve.wait_ge(d_done, ud + (dn["pos",] + 1 + RD))
                step(tt(before[:, :], before[:, :], chosen[:, 0, :], ALU.add))
                tt(before[:, :], before[:, :], chosen[:, 1, :], ALU.add)
                step(nc.vector.tensor_reduce(ps[:, :], hp[:, :, :], X, ALU.add))
                nc.vector.tensor_scalar(vd[:, :], ps[:, :], float(CAP), None, ALU.is_lt)
                nc.vector.scalar_tensor_tensor(out=fl[:, :], in0=ix[:, :], scalar=float(CAP), in1=ps[:, :],
                                               op0=ALU.mult, op1=ALU.add)
                step(nc.vector.tensor_scalar(gi[:, :], ps[:, :], float(CAP - 1), None, ALU.min))
                nc.vector.scalar_tensor_tensor(out=gi[:, :], in0=ix[:, :], scalar=float(CAP), in1=gi[:, :],
                                               op0=ALU.mult, op1=ALU.add)
                step(tt(fd[:, :], fl[:, :], spare[:, :], ALU.subtract))
                step(tt(fd[:, :], fd[:, :], vd[:, :], ALU.mult))
                step(tt(fd[:, :], fd[:, :], spare[:, :], ALU.add))
                nc.vector.tensor_copy(slot_i[:, :], fd[:, :]).then_inc(slots_known, 1)
                nc.vector.tensor_copy(rows_all[:, bass.ds(b, 1), :].rearrange("p o c -> p (o c)"), gi[:, :])
                step(nc.vector.tensor_scalar(spare[:, :], spare[:, :], float(TT * P * K), None, ALU.add))
                dve.wait_ge(ew_ready, b + 1)
                step(nc.vector.reciprocal(wi[:, :], ws[:, :]))
                step(tt(vd[:, :].rearrange("p (j k) -> p j k", k=K), vd[:, :].rearrange("p (j k) -> p j k", k=K),
                        wi[:, :].unsqueeze(2).to_broadcast([P, TT, K]), ALU.mult))
                step(tt(gates_all[:, bass.ds(b, 1), :].rearrange("p o c -> p (o c)"), vd[:, :],
                        ew[:, :, :].rearrange("p j k -> p (j k)"), ALU.mult))
                for n in range(UD - 1 - dn["pos",]):
                    nc.vector.memset(scratch[:, 3 + n:4 + n], 0.0).then_inc(d_done, 1)
                assert steps[0] - 2 == VEC_STEPS, steps

            dve.sem_inc(xet_done, 2)
            dve.sem_inc(he_ready, 2)
            with dve.Fori(0, E // 4) as i:
                i4 = dve.snap(4 * i)

                def slots_turned(s):
                    dve.wait_ge(xet_ready, i4 + (s + 1))
                    nc.vector.tensor_copy(xet[:, s, :, :].rearrange("p k t -> p (k t)"), bank[s % 2][:, :]
                                          ).then_inc(xet_done, 1)

                def hidden(s):
                    dve.wait_ge(sl_ready, i4 + (s + 1))
                    tt(he[:, s, :], bank[2 + s % 2][:, CAP:2 * CAP], sl[:, s, :], ALU.mult).then_inc(he_ready, 1)

                slots_turned(0)
                for s in range(4):
                    if s < 3:
                        slots_turned(s + 1)
                    hidden(s)

            for s in range(2):
                dve.sem_inc(stored[s], 16)
            with dve.Fori(0, N // P // 2) as i:
                i2, i64 = dve.snap(2 * i), dve.snap(64 * i)
                FS = 12
                fs = dve.snap(FS * i)
                steps[0] = 0

                def fin(ins, carry=False):
                    steps[0] += 1
                    ins.then_inc(fin_step, 1)
                    dve.wait_ge(fin_step, fs + steps[0])
                    if carry:
                        nc.vector.memset(scratch[:, 18:19], 0.0)

                for s in range(2):
                    nc.vector.tensor_copy(gates_s[:, s, :],
                                          gates_all[:, bass.ds(i, 1), s * K:(s + 1) * K].rearrange("p o c -> p (o c)"))
                    nc.vector.tensor_copy(rows_s[:, s, :],
                                          rows_all[:, bass.ds(i, 1), s * K:(s + 1) * K].rearrange("p o c -> p (o c)")
                                          ).then_inc(picks_ready, 1)
                for s in range(2):
                    dve.wait_ge(gathered[s], i64 + 64)
                    prev = base_all[:, bass.ds(i, 1), s, :].rearrange("p o n -> p (o n)")
                    for k in range(K):
                        fin(nc.vector.scalar_tensor_tensor(out=acc[:, s, :], in0=gr[:, s, k, :],
                                                           scalar=gates_s[:, s, k:k + 1], in1=prev,
                                                           op0=ALU.mult, op1=ALU.add))
                        prev = acc[:, s, :]
                    fin(nc.vector.bn_stats(st3[:, s, :], acc[:, s, :]), carry=True)
                    fin(nc.vector.bn_aggr(mv3[:, s, :], st3[:, s, :]))
                    nc.vector.tensor_scalar(va3[:, s:s + 1], mv3[:, s, 1:2], EPS, None, ALU.add
                                            ).then_inc(var_ready, 1)
                for s in range(2):
                    dve.wait_ge(rstd_ready, i2 + (s + 1))
                    dve.wait_ge(stored[s], 16 * i + 16)
                    nc.vector.tensor_scalar(yo[:, s, :], acc[:, s, :], mv3[:, s, 0:1], rv3[:, s:s + 1],
                                            ALU.subtract, ALU.mult).then_inc(yo_ready, 1)
                assert steps[0] == FS, steps


def kernel(**a):
    import concourse.bacc as _bacc
    from concourse.bass_utils import run_bass_kernel_spmd as _run

    a = {k: np.asarray(v) for k, v in a.items()}

    def rows(v):
        return np.broadcast_to(v.reshape(1, -1), (P, v.size))

    r = np.arange(P)
    spare = SLOTS + (np.arange(TT)[None, :, None] * P + r[:, None, None]) * K + np.arange(K)
    const = np.concatenate([
        np.eye(P), r[:, None] <= r[None, :], np.where(r[None, :] > r[:, None], NEG, 0.0),
        np.broadcast_to(np.arange(E), (P, E)), spare.reshape(P, TT * K)], axis=1).astype(np.float32)
    x = a["x"]
    arrays = {
        "x": x,
        "xT": x.transpose(0, 2, 1),
        "ctxT": a["ctx_768"].transpose(0, 2, 1),
        "wall": np.concatenate([a["L0_attn_Wqkv"], a["L0_attn_W2w"], a["L0_attn_W1r"], a["L0_attn_W2r"],
                                a["L0_attn_W1w"]], axis=0).T,
        "bias": np.concatenate([rows(a["L0_attn_bqkv"]), rows(a["L0_attn_bout"]), rows(a["L0_xattn_b_out"]),
                                rows(a["L0_attn_bias_scale"])], axis=1),
        "wout": a["L0_attn_Wout"].T,
        "wq": a["L0_xattn_w_q"],
        "wkv": a["L0_xattn_w_kv"],
        "wo": a["L0_xattn_w_out"],
        "gate": a["L0_ffn_gate_w"].T,
        "wgu": a["L0_ffn_w_gate_up"],
        "wdn": a["L0_ffn_w_down"],
        "shgu": a["L0_ffn_shared_w_gate_up"],
        "shdn": a["L0_ffn_shared_w_down"],
        "const": const,
    }
    nc = _bacc.Bacc("TRN2", target_bir_lowering=False, num_devices=1)
    args = []
    for name, v in arrays.items():
        arrays[name] = v = np.ascontiguousarray(v)
        args.append(nc.dram_tensor(name, v.shape, mybir.dt.from_np(v.dtype), kind="ExternalInput").ap())
    args.append(nc.dram_tensor("out", (N, D), F32, kind="ExternalOutput").ap())
    build(nc, *args)
    got = _run(nc, [arrays], core_ids=[0])
    return got.results[0]["out"].reshape(B, T, D)
```

```python
from contextlib import ExitStack

import numpy as np

import concourse.bass as bass
from concourse import mybir

F32 = mybir.dt.float32
BF16 = mybir.dt.bfloat16
U32 = mybir.dt.uint32
ALU = mybir.AluOpType
ACT = mybir.ActivationFunctionType
X = mybir.AxisListType.X

P = 128
B, T, D = 8, 256, 256
TT = T // P
H, DH = 16, 16
XH, XD = 16, 64
C = 192
CP = C // 2
E, K, CAP, I = 32, 4, 256, 128
N = B * T
SLOTS = E * CAP
EPS = 1e-5
NEG = -1e30

RD, RA, RO = 3, 3, 2
PARTS = 6
SPLIT_STEPS = 8
RING = 4
S_STEPS, X_STEPS = 16, 23
CROSS_SLOTS, SELF_SLOTS = XH + 3, H + 4


def schedule(self_part, cross_part):
    steps = []
    beside_cross = {0: [("proj", 0)], 1: [("take_proj", 0), ("proj", 1)], 2: [("take_proj", 1)],
                    3: [("lines", 0)], 4: [("lines", 1)], 5: [("lines", 2), ("split", 0)],
                    10: [("outer", 0)], 12: [("outer", 1)], 13: [("moment", 0)], 14: [("take_moment", 0), ("moment", 1)],
                    16: [("take_moment", 1)], 17: [("split", 2)], 18: [("split", 1)]}
    beside_self = {1: [("out2", 0)], 2: [("norm2", 0)], 4: [("norm2", 1)], 5: [("x2t", 0)], 6: [("shared", 0)],
                   7: [("gate", 0)], 9: [("silu", 0)], 11: [("shared", 1)], 16: [("choose", 0)], 17: [("choose", 1)]}
    for n in range(CROSS_SLOTS):
        if cross_part:
            steps.append(("cross", n))
        if self_part:
            steps += beside_cross.get(n, [])
    steps += [("turn_heads", 0)] if self_part else []
    steps += [("turn_out2", 0)] if cross_part else []
    steps += [("turn_heads", w) for w in (1, 2, 3)] if self_part else []
    for n in range(SELF_SLOTS):
        if self_part:
            steps.append(("self", n))
        if cross_part:
            steps += beside_self.get(n, [])
        if self_part and n == H:
            steps += [("keys", 0), ("keys", 1)]
        if self_part and n == H + 1:
            steps += [("sums", 0)]
        if self_part and n == H + 2:
            steps += [("keys", 2), ("keys", 3)]
    tail = [("turn_out", 0), ("vals", 0), ("place", 0), ("out", 0), ("place", 1), ("vals", 1), ("norm1", 0),
            ("vals", 2), ("vals", 3), ("place", 2), ("queries", 0)]
    steps += [s for s in tail if (cross_part if s[0] == "place" else self_part)]
    return steps


def turned(w):
    return [("t", w, n) for n in range(2 * TT if w < 2 else TT)]


def plan(steps):
    d, a, o = [], [], []
    for name, n in steps:
        if name == "proj":
            d += [("g1", n), ("g2", n)]
        elif name == "moment":
            d += [("m", n, f) for f in range(2)]
        elif name == "turn_heads":
            a += turned(n)[0::2]
            d += turned(n)[1::2]
        elif name == "self":
            if n < H:
                d.append(("x", n))
                a.append(("y", n))
            if 0 <= n - 3 < H:
                (a if n % 2 else d).append(("pt", n - 3))
            if n == 4:
                o += [("o", 0), ("o", 1)]
        elif name == "cross":
            if n < XH:
                a.append(("s", n))
            if 0 <= n - 2 < XH:
                a.append(("pt2", n - 2))
            if n == 3:
                o += [("o2", g) for g in range(4)]
        elif name == "turn_out":
            a.append(("ot",))
        elif name == "out":
            d.append(("out",))
        elif name == "keys":
            a.append(("k", n))
        elif name == "vals":
            a.append(("v", n))
        elif name == "queries":
            d.append(("x1t",))
            a += [("q", c) for c in range(4)]
        elif name == "turn_out2":
            a += [("o2t", c) for c in range(4)]
        elif name == "out2":
            d.append(("out2",))
        elif name == "x2t":
            d.append(("x2t",))
        elif name == "gate":
            d.append(("lg",))
        elif name == "shared" and n == 0:
            a += [("sg", 0), ("sg", 1)]
        elif name == "shared":
            d.append(("sh",))
        elif name == "place" and n == 0:
            d.append(("pos",))
    d += [("pad", n) for n in range(-len(d) % RD)]
    a += [("pad", n) for n in range(-len(a) % RA)]
    assert len(o) % RO == 0
    return [{u: n for n, u in enumerate(r)} for r in (d, a, o)]


class Pass:

    def __init__(self, eng, steps, before, each, i, s, x):
        self.steps, (self.dn, self.an, self.on), self.s, self.x = steps, plan(steps), s, x
        snap = (lambda v: v) if i is None else eng.snap
        self.d, self.a, self.o = (snap(before[r] + (0 if i is None else (i - 1) * each[r])) for r in range(3))
        self.s16 = None if s is None else snap(s * 16)
        self.x16 = None if x is None else snap(x * 16)

    def d_bank(self, *u):
        return self.dn[u] % RD

    def a_bank(self, *u):
        return RD + self.an[u] % RA

    def o_bank(self, *u):
        return RD + RA + self.on[u] % RO


def passes(eng):
    first, mid, last = (schedule(*k) for k in ((True, False), (True, True), (False, True)))
    n_first, n_mid = ([len(r) for r in plan(k)] for k in (first, mid))
    yield Pass(eng, first, [0, 0, 0], None, None, 0, None)
    with eng.Fori(1, B) as i:
        yield Pass(eng, mid, n_first, n_mid, i, i, i - 1)
    yield Pass(eng, last, [f + (B - 1) * m for f, m in zip(n_first, n_mid)], None, None, None, B - 1)


def totals():
    counts = [[len(r) for r in plan(schedule(*k))] for k in ((True, False), (True, True), (False, True))]
    return [f + (B - 1) * m + t for f, m, t in zip(*counts)]


def build(nc, x, xT, ctxT, wall, bias, wout, wq, wkv, wo, gate, wgu, wdn, shgu, shdn, const, out):
    all_d, all_a, all_o = totals()
    ctx = ExitStack()
    with ctx:
        def sb(name, shape, dt=F32):
            return ctx.enter_context(nc.sbuf_tensor(name, shape, dt))

        def sem(name):
            return ctx.enter_context(nc.semaphore(name))

        bank = [ctx.enter_context(nc.psum_tensor(f"bank{i}", [P, 512], F32)) for i in range(8)]
        slots = nc.dram_tensor("slots", [SLOTS + N * K, D], F32, kind="Internal").ap()
        expert_rows = nc.dram_tensor("expert_rows", [SLOTS, D], F32, kind="Internal").ap()

        cst = sb("cst", [P, 3 * P + E + TT * K])
        ident, tri, mask = cst[:, 0:P], cst[:, P:2 * P], cst[:, 2 * P:3 * P]
        iota, spare0 = cst[:, 3 * P:3 * P + E], cst[:, 3 * P + E:]
        ident_b = sb("ident_b", [P, P], BF16)
        before_b = sb("before_b", [P, P], BF16)
        ones_b = sb("ones_b", [P, P], BF16)
        ones = sb("ones", [P, P])
        mask_s = sb("mask_s", [P, H, P], BF16)
        wall_s = sb("wall_s", [P, 2, 1024])
        bias_s = sb("bias_s", [P, 3 * D + 2 * D + H])
        bqkv, bout, bo = bias_s[:, 0:3 * D], bias_s[:, 3 * D:4 * D], bias_s[:, 4 * D:5 * D]
        bscale = bias_s[:, 5 * D:]
        sgn, nsgn, absb = sb("sgn", [P, H]), sb("nsgn", [P, H]), sb("absb", [P, H])
        wout_s = sb("wout_s", [P, 2, D])
        wq_s = sb("wq_s", [P, 2, XH * XD])
        wkv_s = sb("wkv_s", [CP, 2, 2 * XH * XD])
        wo_s = sb("wo_s", [P, 8, D])
        gate_s = sb("gate_s", [P, 2, E])
        shgu_s, shdn_s = sb("shgu_s", [P, 2, 2 * I]), sb("shdn_s", [P, D])
        powers = sb("powers", [P, 2 * TT * H])
        zero = sb("zero", [P, 1024])
        scratch, turn_p, turn_a = sb("scratch", [P, 64]), sb("turn_p", [P, 8]), sb("turn_a", [P, 4])

        xp = sb("xp", [P, 2, T + 1])
        xr = sb("xr", [P, TT, D])
        ct = sb("ct", [CP, 2, T])
        raw = sb("raw", [P, 2, TT * H, DH])
        lraw = sb("lraw", [P, 2, TT * H, 6])
        qks = sb("qks", [P, 2, TT * H, PARTS * DH], BF16)
        lqk = sb("lqk", [P, 2, TT * H, 64], BF16)
        v = sb("v", [P, TT, H, 2 * DH])
        lw = sb("lw", [P, 4, TT * 64])
        ll = sb("ll", [P, 2, TT * H, 6])
        ss = sb("ss", [P, 2 * TT * H])
        rn = sb("rn", [P, 2 * TT * H])
        rd = sb("rd", [P, TT * H, 6])
        oo = sb("oo", [P, TT, H * 36])
        sq = oo[:, :, :].rearrange("p j n -> p (j n)")[:, 0:2 * TT * H * 6].rearrange("p (h c) -> p h c", c=6)
        mr = sb("mr", [P, TT * 2, 8 * 6, 6])
        pp = mr[:, :, :, :].rearrange("p a n c -> p (a n c)")[:, 0:2 * TT * H * 16].rearrange(
            "p (w h i k) -> p w h i k", w=2, i=4, k=4)
        rm = sb("rm", [P, TT * H, 6])
        lqt, lkt = sb("lqt", [P, H // 2, T], BF16), sb("lkt", [P, H // 2, T], BF16)
        abnl = sb("abnl", [P, 2 * RING * 384])
        ab = abnl[:, 0:RING * 384].rearrange("p (r n) -> p r n", r=RING)
        nl = abnl[:, RING * 384:].rearrange("p (r n) -> p r n", r=RING)
        nm = sb("nm", [P, RING, TT])
        prpt = sb("prpt", [P, 2 * RING * 512])
        pr = prpt[:, 0:RING * 512].rearrange("p (r n) -> p r n", r=RING)
        pt = prpt[:, RING * 512:].rearrange("p (r n) -> p r n", r=RING)
        rs, ri = sb("rs", [P, TT, H]), sb("ri", [P, TT, H])
        oht = sb("oht", [P, 2, T])
        y1, y2 = sb("y1", [P, TT, D]), sb("y2", [P, TT, D])
        rib = y1
        rit = y2[:, :, :].rearrange("p f (j t) -> p f j t", j=TT)
        st, mv, va, rv = (sb(n, [P, 2, TT, w]) for n, w in (("st", 6), ("mv", 2), ("va", 1), ("rv", 1)))
        x1 = sb("x1", [P, TT, D])
        x1t = sb("x1t", [P, 2, T])
        kt2 = sb("kt2", [P, 8, T])
        qt = abnl[:, 0:8 * T].rearrange("p (c t) -> p c t", c=8)
        v2 = sb("v2", [P, TT, XH * XD])
        nm2 = sb("nm2", [P, RING, TT])
        rs2, ri2 = sb("rs2", [P, TT, XH]), sb("ri2", [P, TT, XH])
        o2 = sb("o2", [P, TT, XH * XD])
        o2t = kt2
        st_q, st_k = (w[:, :, :].rearrange("p j n -> p (j n)").bitcast(BF16).rearrange("p (h t) -> p h t", h=H)
                      for w in (v2, o2))
        x2 = sb("x2", [P, TT, D])
        x2t = sb("x2t", [P, 2, T])
        lg, m8 = sb("lg", [P, TT, E]), sb("m8", [P, TT, 8])
        i8 = sb("i8", [P, TT, 8], U32)
        ix = sb("ix", [P, TT * K])
        nmx, ew, ws, wi = sb("nmx", [P, TT]), sb("ew", [P, TT, K]), sb("ws", [P, TT]), sb("wi", [P, TT])
        hot = sb("hot", [P, TT * K, E])
        hp = sb("hp", [P, TT * K, E])
        chosen = sb("chosen", [P, TT, E], BF16)
        before = sb("before", [P, E], BF16)
        ps, vd, fl, fd, gi = (sb(n, [P, TT * K]) for n in ("ps", "vd", "fl", "fd", "gi"))
        spare = sb("spare", [P, TT * K])
        slot_i = sb("slot_i", [P, TT * K], U32)
        sge, sgg, sgu, sgr = (mr[:, n, :, :].rearrange("p a c -> p (a c)")[:, 0:T] for n in range(4))
        sgh = sb("sgh", [P, T])
        base_all = sb("base_all", [P, B, TT, D])
        gates_all = sb("gates_all", [P, B, TT * K])
        rows_all = sb("rows_all", [P, B, TT * K], U32)

        we = qks[:, :, :, :].rearrange("p w h n -> p (w h n)")[:, 0:4 * 2 * 2 * I * 2].bitcast(F32).rearrange(
            "p (s k n) -> p s k n", s=4, k=2)
        wd = zero[:, :].rearrange("p (s n) -> p s n", s=4)
        xe = qt[:, :, :].rearrange("p (s c) n -> p s c n", c=2)
        xet = o2[:, :, :].rearrange("p j (a n) -> p (j a) n", n=CAP).rearrange("p (s c) n -> p s c n", c=2)
        ye = o2t[:, :, :].rearrange("p (s c) n -> p s c n", c=2)
        sl = v2[:, 0, :].rearrange("p (s n) -> p s n", s=4)
        he = v2[:, 1, :].rearrange("p (s n) -> p s n", s=4)
        NC = 4
        gr = prpt[:, :].rearrange("p (s c n) -> p s c n", s=NC, c=K)
        rows_s, gates_s = sb("rows_s", [P, NC, K], U32), sb("gates_s", [P, NC, K])
        acc = v2[:, 0, :].rearrange("p (s n) -> p s n", s=NC)
        yo = v2[:, 1, :].rearrange("p (s n) -> p s n", s=NC)
        st3, mv3, va3, rv3 = sb("st3", [P, NC, 6]), sb("mv3", [P, NC, 2]), sb("va3", [P, NC]), sb("rv3", [P, NC])

        loaded, loaded2, zeroed = sem("loaded"), sem("loaded2"), sem("zeroed")
        prepared, prepared2, pooled = sem("prepared"), sem("prepared2"), sem("pooled")
        setup = sem("setup")
        xt_loaded, xr_loaded, ctx_loaded = sem("xt_loaded"), sem("xr_loaded"), sem("ctx_loaded")
        xt_used, ctx_used = sem("xt_used"), sem("ctx_used")
        d_ready, d_done = sem("d_ready"), sem("d_done")
        a_ready, a_done = sem("a_ready"), sem("a_done")
        o_ready, o_done = sem("o_ready"), sem("o_done")
        s_step, x_step = sem("s_step"), sem("x_step")
        lines_asked, lines_done = sem("lines_asked"), sem("lines_done")
        var1_asked, var1_done = sem("var1_asked"), sem("var1_done")
        var2_asked, var2_done = sem("var2_asked"), sem("var2_done")
        outer_done = sem("outer_done")
        raw_ready, lines_ready = sem("raw_ready"), sem("lines_ready")
        split_step, split_ready, heads_turned = sem("split_step"), sem("split_ready"), sem("heads_turned")
        probs_ready, sums_ready = sem("probs_ready"), sem("sums_ready")
        x1_ready, rowmax_ready = sem("x1_ready"), sem("rowmax_ready")
        x2_ready, top_ready, ew_ready, chosen_ready = (sem("x2_ready"), sem("top_ready"), sem("ew_ready"),
                                                       sem("chosen_ready"))
        queries_ready = sem("queries_ready")
        sgh_ready = sem("sgh_ready")
        slots_known, scattered, x2_free = sem("slots_known"), sem("scattered"), sem("x2_free")
        routed = sem("routed")
        ex_loaded = [sem(f"ex_loaded{s}") for s in range(4)]
        xet_ready, xet_done = sem("xet_ready"), sem("xet_done")
        gu_ready, sl_ready, he_ready = sem("gu_ready"), sem("sl_ready"), sem("he_ready")
        ye_ready, ye_done, ye_stored = sem("ye_ready"), sem("ye_done"), sem("ye_stored")
        picks_ready, wait_taken = sem("picks_ready"), sem("wait_taken")
        gathered = [sem(f"gathered{s}") for s in range(4)]
        var_ready, rstd_ready = sem("var_ready"), sem("rstd_ready")
        yo_ready, fin_step = sem("yo_ready"), sem("fin_step")
        stored = [sem(f"stored{s}") for s in range(4)]

        def split(tasks, tensor_tensor, then):
            one = ones[:, 0:1].unsqueeze(2).unsqueeze(3)
            for step in range(4):
                for x, p, w in tasks:
                    wide = p.rearrange("p h (a c) d -> p h a c d", c=2)
                    p1 = p[:, :, 3:6, :] if w == 0 else wide[:, :, :, 0, :]
                    p2 = p[:, :, 0:2, :] if w == 0 else wide[:, :, 0:2, 1, :]
                    p3 = p[:, :, 2, :] if w == 0 else p[:, :, 5, :]
                    if step == 0:
                        ins = tensor_tensor(p1, x.unsqueeze(2).to_broadcast(list(p1.shape)),
                                            one.to_broadcast(list(p1.shape)), ALU.mult)
                    elif step == 1:
                        ins = tensor_tensor(x, x, p1[:, :, 0, :], ALU.subtract)
                    elif step == 2:
                        ins = tensor_tensor(p2, x.unsqueeze(2).to_broadcast(list(p2.shape)),
                                            one.to_broadcast(list(p2.shape)), ALU.mult)
                    else:
                        ins = tensor_tensor(p3, x, p2[:, :, 0, :], ALU.subtract)
                if step < 3:
                    then(ins)
            return ins

        def line_parts(w):
            return lqk[:, w, :, 0:PARTS * 6].rearrange("p h (b d) -> p h b d", d=6)

        def turned_to(w, n, o):
            o = o[:, :].bitcast(BF16).rearrange("p (g t) -> p g t", g=8)
            if w < 2:
                j, f = n // 2, n % 2
                rows = slice(0, PARTS * DH)
                return (st_q, st_k)[w][rows, 8 * f:8 * f + 8, j * P:(j + 1) * P], o[rows, :, :]
            return (lqt, lkt)[w - 2][:, :, n * P:(n + 1) * P], o

        block = ctx.enter_context(nc.Block())

        @block.sync
        def _(sp):
            sp.dma_start(cst[:, :], const).then_inc(loaded, 16)
            sp.dma_start(bias_s[:, :], bias).then_inc(loaded, 16)
            sp.dma_start(wall_s[:, :, :], wall.rearrange("(k p) n -> p k n", p=P)).then_inc(loaded, 16)
            sp.dma_start(xp[:, :, 1:T + 1], xT[0, :, :].rearrange("(k p) t -> p k t", p=P)).then_inc(xt_loaded, 16)
            for dst, src in (
                (wkv_s[:, :, :], wkv.rearrange("(k p) n -> p k n", p=CP)),
                (wout_s[:, :, :], wout.rearrange("(k p) n -> p k n", p=P)),
                (wq_s[:, :, :], wq.rearrange("(k p) n -> p k n", p=P)),
                (wo_s[:, :, :], wo.rearrange("(k p) n -> p k n", p=P)),
                (gate_s[:, :, :], gate.rearrange("(k p) n -> p k n", p=P)),
                (shgu_s[:, :, :], shgu.rearrange("(k p) n -> p k n", p=P)),
                (shdn_s[:, :], shdn),
            ):
                sp.dma_start(dst, src).then_inc(loaded2, 16)
            sp.dma_start(ct[:, :, :], ctxT[0, :, :].rearrange("(k p) t -> p k t", p=CP)).then_inc(ctx_loaded, 16)
            sp.dma_start(xr[:, :, :], x[0, :, :].rearrange("(j p) n -> p j n", p=P)).then_inc(xr_loaded, 16)
            sp.wait_ge(prepared, 1)
            rows = 1024 // D
            for c in range(SLOTS // (P * rows)):
                sp.dma_start(slots[c * P * rows:(c + 1) * P * rows, :].rearrange("(p r) n -> p (r n)", p=P),
                             zero[:, :]).then_inc(zeroed, 16)
            with sp.Fori(1, B) as b:
                sp.wait_ge(xt_used, b)
                sp.dma_start(xp[:, :, 1:T + 1], xT[bass.ds(b, 1), :, :].rearrange("o (k p) t -> p (o k) t", p=P)
                             ).then_inc(xt_loaded, 16)
                sp.wait_ge(ctx_used, b)
                sp.dma_start(ct[:, :, :], ctxT[bass.ds(b, 1), :, :].rearrange("o (k p) t -> p (o k) t", p=CP)
                             ).then_inc(ctx_loaded, 16)
                sp.wait_ge(s_step, S_STEPS * b)
                sp.dma_start(xr[:, :, :], x[bass.ds(b, 1), :, :].rearrange("o (j p) n -> p (o j) n", p=P)
                             ).then_inc(xr_loaded, 16)

            def load_expert(e, s):
                sp.dma_start(we[:, s, :, :], wgu[e, :, :].rearrange("o (k p) n -> p (o k) n", p=P)
                             ).then_inc(ex_loaded[s], 16)
                sp.dma_start(wd[:, s, :], wdn[e, :, :].rearrange("o p n -> p (o n)")
                             ).then_inc(ex_loaded[s], 16)

            def load_slots(c, s):
                sp.dma_start(xe[:, s, :, :], slots[c, :].rearrange("(k p) n -> p k n", p=P)
                             ).then_inc(ex_loaded[s], 16)

            sp.wait_ge(zeroed, 16 * SLOTS * D // (P * 1024))
            sp.wait_ge(heads_turned, B)
            for s in range(4):
                load_expert(slice(s, s + 1), s)
            sp.wait_ge(scattered, 16 * N * K // P)
            for s in range(4):
                load_slots(slice(s * CAP, (s + 1) * CAP), s)
            with sp.Fori(1, E // 4) as i:
                for s in range(4):
                    sp.wait_ge(ye_ready, 4 * i + (s - 3))
                    load_expert(bass.ds(4 * i + s, 1), s)
                    load_slots(bass.ds((4 * i + s) * CAP, CAP), s)
            with sp.Fori(0, N // P // NC) as i:
                for s in range(NC):
                    sp.wait_ge(yo_ready, NC * i + (s + 1))
                    sp.dma_start(out[bass.ds((NC * i + s) * P, P), :], yo[:, s, :]).then_inc(stored[s], 16)
            for s in range(NC):
                sp.wait_ge(stored[s], 16 * (N // P // NC) + 16)

        @block.tensor
        def _(pe):
            pe.wait_ge(loaded, 16 * 3)
            pe.wait_ge(prepared, 5)

            def part_a(u):
                def d_free(*n):
                    pe.wait_ge(d_done, u.d + (u.dn[n] + 1))
                    return bank[u.d_bank(*n)]

                def a_free(*n):
                    pe.wait_ge(a_done, u.a + (u.an[n] + 1))
                    return bank[u.a_bank(*n)]

                def o_free(*n):
                    pe.wait_ge(o_done, u.o + (u.on[n] + 1))

                def o_bank(*n):
                    return bank[u.o_bank(*n)]

                def vec_took(*n):
                    pe.wait_ge(d_done, u.d + (u.dn[n] + 1 + RD))

                def act_took(*n):
                    pe.wait_ge(a_done, u.a + (u.an[n] + 1 + RA))

                def divided(*n):
                    pe.wait_ge(o_done, u.o + (u.on[n] + 1 + RO))

                def proj(j):
                    if j == 0:
                        pe.wait_ge(xt_loaded, 16 * u.s + 16)
                    o = d_free("g1", j)
                    for k in range(2):
                        mm = pe.matmul(o[:, :], xp[:, k, 1 + j * P:1 + (j + 1) * P],
                                       wall_s[:, k, 0:512], start=(k == 0), stop=(k == 1))
                    mm.then_inc(d_ready, 1)
                    o = d_free("g2", j)
                    for k in range(2):
                        pe.matmul(o[:, 0:448], xp[:, k, 1 + j * P:1 + (j + 1) * P],
                                  wall_s[:, k, 512:960], start=(k == 0), stop=(k == 1))
                    for k in range(2):
                        mm = pe.matmul(o[:, 448:512], xp[:, k, j * P:(j + 1) * P],
                                       wall_s[:, k, 960:1024], start=(k == 0), stop=(k == 1))
                    mm.then_inc(d_ready, 1)
                    if j == TT - 1:
                        pe.drain().then_inc(xt_used, 1)

                def moment(j):
                    pe.wait_ge(outer_done, 2 * u.s + (j + 1))
                    for f in range(2):
                        o, cols = d_free("m", j, f)[:, 0:288], slice(f * 288, (f + 1) * 288)
                        for i in range(j):
                            pe.matmul(o, ones[:, :], oo[:, i, cols], start=(i == 0), stop=False)
                        pe.matmul(o, tri, oo[:, j, cols], start=(j == 0), stop=True).then_inc(d_ready, 1)

                def turn_heads(w):
                    if w == 0:
                        pe.wait_ge(split_ready, u.s + 1)
                    if w == 2:
                        pe.wait_ge(lines_ready, 2 * u.s + 2)
                    for n, unit in enumerate(turned(w)):
                        o = (a_free if n % 2 == 0 else d_free)(*unit)[:, :].bitcast(BF16)
                        j, f = (n // 2, n % 2) if w < 2 else (n, 0)
                        for g in range(8):
                            if w < 2:
                                mm = pe.transpose(o[0:PARTS * DH, g * P:(g + 1) * P],
                                                  qks[:, w, j * H + 8 * f + g, :], ident_b[:, :])
                            else:
                                mm = pe.transpose(o[:, g * P:(g + 1) * P],
                                                  lqk[:, w - 2, j * H + 2 * g:j * H + 2 * g + 2, :].rearrange(
                                                      "p a c -> p (a c)"), ident_b[:, :])
                        mm.then_inc(a_ready if n % 2 == 0 else d_ready, 1)
                    if w == 1:
                        pe.drain().then_inc(heads_turned, 1)

                def scores(h):
                    if h == 0:
                        act_took(*turned(3)[0])
                        vec_took(*turned(3)[1])
                    o = d_free("x", h)
                    rows = slice(0, PARTS * DH)
                    for j in range(TT):
                        cols = slice(0, P) if j == 0 else slice(P, 3 * P)
                        pe.matmul(o[:, cols], st_q[rows, h, j * P:(j + 1) * P], st_k[rows, h, 0:(j + 1) * P],
                                  start=True, stop=False)
                        mm = pe.matmul(o[:, 2 * j * P:(2 * j + 1) * P], ident_b[:, :], mask_s[:, h, :],
                                       start=False, stop=True)
                    mm.then_inc(d_ready, 1)
                    o = a_free("y", h)
                    rows = slice(64 * (h % 2), 64 * (h % 2) + PARTS * 6)
                    for j in range(TT):
                        cols = slice(0, P) if j == 0 else slice(P, 3 * P)
                        mm = pe.matmul(o[:, cols], lqt[rows, h // 2, j * P:(j + 1) * P],
                                       lkt[rows, h // 2, 0:(j + 1) * P], start=True, stop=True)
                    mm.then_inc(a_ready, 1)

                def turn(h):
                    pe.wait_ge(probs_ready, u.s16 + (h + 1))
                    o = d_free("pt", h) if h % 2 else a_free("pt", h)
                    for c in range(3):
                        mm = pe.transpose(o[:, c * P:(c + 1) * P], pr[:, h % RING, c * P:(c + 1) * P], ident)
                    mm.then_inc(d_ready if h % 2 else a_ready, 1)

                def values(h):
                    (vec_took if h % 2 else act_took)("pt", h)
                    if h % 8 == 0:
                        o_free("o", h // 8)
                    rows = slice(h % 8 // 2 * 32, h % 8 // 2 * 32 + 32)
                    o = o_bank("o", h // 8)
                    pe.matmul(o[rows, 0:T], v[:, 0, h, :], pt[:, h % RING, 0:T], start=(h % 2 == 0), stop=False)
                    mm = pe.matmul(o[rows, P:T], v[:, 1, h, :], pt[:, h % RING, T:T + P],
                                   start=False, stop=(h % 2 == 1))
                    if h % 8 == 7:
                        mm.then_inc(o_ready, 1)

                def turn_out():
                    pe.wait_ge(sums_ready, u.s + 1)
                    o = a_free("ot")
                    for j in range(TT):
                        for f in range(2):
                            mm = pe.transpose(o[:, f * T + j * P:f * T + (j + 1) * P],
                                              rib[:, j, f * P:(f + 1) * P], ident)
                    mm.then_inc(a_ready, 1)

                def out():
                    divided("o", 1)
                    o = d_free("out")
                    for j in range(TT):
                        for k in range(2):
                            mm = pe.matmul(o[:, j * D:(j + 1) * D], oht[:, k, j * P:(j + 1) * P],
                                           wout_s[:, k, :], start=(k == 0), stop=(k == 1))
                    mm.then_inc(d_ready, 1)

                def keys(n):
                    if n == 0:
                        pe.wait_ge(ctx_loaded, 16 * u.s + 16)
                    o = a_free("k", n)
                    for c in range(2):
                        for k in range(2):
                            mm = pe.matmul(o[:, c * T:(c + 1) * T],
                                           wkv_s[:, k, (2 * n + c) * P:(2 * n + c + 1) * P], ct[:, k, :],
                                           start=(k == 0), stop=(k == 1))
                    mm.then_inc(a_ready, 1)

                def vals(n):
                    cols = slice(XH * XD + n % 2 * 512, XH * XD + (n % 2 + 1) * 512)
                    o = a_free("v", n)
                    for k in range(2):
                        mm = pe.matmul(o[:, :], ct[:, k, n // 2 * P:(n // 2 + 1) * P], wkv_s[:, k, cols],
                                       start=(k == 0), stop=(k == 1))
                    mm.then_inc(a_ready, 1)
                    if n == 3:
                        pe.drain().then_inc(ctx_used, 1)

                def queries():
                    pe.wait_ge(x1_ready, 2 * u.s + 2)
                    o = d_free("x1t")
                    for j in range(TT):
                        for k in range(2):
                            mm = pe.transpose(o[:, k * T + j * P:k * T + (j + 1) * P],
                                              x1[:, j, k * P:(k + 1) * P], ident)
                    mm.then_inc(d_ready, 1)
                    vec_took("x1t")
                    for n in range(4):
                        o = a_free("q", n)
                        for c in range(2):
                            for k in range(2):
                                mm = pe.matmul(o[:, c * T:(c + 1) * T],
                                               wq_s[:, k, (2 * n + c) * P:(2 * n + c + 1) * P], x1t[:, k, :],
                                               start=(k == 0), stop=(k == 1))
                        mm.then_inc(a_ready, 1)

                def scores2(h):
                    if h == 0:
                        pe.wait_ge(queries_ready, u.x + 1)
                    r, c = XD * (h % 2), h // 2
                    o = a_free("s", h)
                    for j in range(TT):
                        mm = pe.matmul(o[:, j * T:(j + 1) * T], qt[r:r + XD, c, j * P:(j + 1) * P],
                                       kt2[r:r + XD, c, :], start=True, stop=True)
                    mm.then_inc(a_ready, 1)

                def turn2(h):
                    act_took("s", h)
                    o = a_free("pt2", h)
                    for j in range(TT):
                        for i in range(TT):
                            mm = pe.transpose(o[:, i * T + j * P:i * T + (j + 1) * P],
                                              pr[:, h % RING, j * T + i * P:j * T + (i + 1) * P], ident)
                    mm.then_inc(a_ready, 1)

                def values2(h):
                    act_took("pt2", h)
                    if h % 4 == 0:
                        o_free("o2", h // 4)
                    for j in range(TT):
                        o = o_bank("o2", h // 4)[:, j * T + (h % 4) * XD:j * T + (h % 4 + 1) * XD]
                        for i in range(TT):
                            mm = pe.matmul(o, pt[:, h % RING, i * T + j * P:i * T + (j + 1) * P],
                                           v2[:, i, h * XD:(h + 1) * XD], start=(i == 0), stop=(i == 1))
                    if h % 4 == 3:
                        mm.then_inc(o_ready, 1)

                def turn_out2():
                    for n in range(4):
                        divided("o2", n)
                        o = a_free("o2t", n)
                        for c in range(2):
                            for j in range(TT):
                                mm = pe.transpose(o[:, c * T + j * P:c * T + (j + 1) * P],
                                                  o2[:, j, (2 * n + c) * P:(2 * n + c + 1) * P], ident)
                        mm.then_inc(a_ready, 1)

                def out2():
                    o = d_free("out2")
                    act_took("o2t", 3)
                    for j in range(TT):
                        for k in range(8):
                            mm = pe.matmul(o[:, j * D:(j + 1) * D], o2t[:, k, j * P:(j + 1) * P],
                                           wo_s[:, k, :], start=(k == 0), stop=(k == 7))
                    mm.then_inc(d_ready, 1)

                def turn_x2():
                    pe.wait_ge(x2_ready, 2 * u.x + 2)
                    o = d_free("x2t")
                    for j in range(TT):
                        for k in range(2):
                            mm = pe.transpose(o[:, k * T + j * P:k * T + (j + 1) * P],
                                              x2[:, j, k * P:(k + 1) * P], ident)
                    mm.then_inc(d_ready, 1)

                def gate_logits():
                    o = d_free("lg")
                    vec_took("x2t")
                    for j in range(TT):
                        for k in range(2):
                            mm = pe.matmul(o[:, j * E:(j + 1) * E], x2t[:, k, j * P:(j + 1) * P],
                                           gate_s[:, k, :], start=(k == 0), stop=(k == 1))
                    mm.then_inc(d_ready, 1)

                def shared_up():
                    vec_took("x2t")
                    for c in range(2):
                        o = a_free("sg", c)
                        for k in range(2):
                            mm = pe.matmul(o[:, 0:T], shgu_s[:, k, c * I:(c + 1) * I], x2t[:, k, :],
                                           start=(k == 0), stop=(k == 1))
                        mm.then_inc(a_ready, 1)

                def shared_down():
                    pe.wait_ge(sgh_ready, u.x + 1)
                    o = d_free("sh")
                    for j in range(TT):
                        mm = pe.matmul(o[:, j * D:(j + 1) * D], sgh[:, j * P:(j + 1) * P], shdn_s[:, :],
                                       start=True, stop=True)
                    mm.then_inc(d_ready, 1)

                def places():
                    pe.wait_ge(chosen_ready, u.x + 1)
                    bk = d_free("pos")
                    for j in range(TT):
                        o = bk[:, j * E:(j + 1) * E]
                        pe.matmul(o, ones_b[:, :], before[:, :], start=True, stop=False)
                        for i in range(j):
                            pe.matmul(o, ones_b[:, :], chosen[:, i, :], start=False, stop=False)
                        mm = pe.matmul(o, before_b[:, :], chosen[:, j, :], start=False, stop=True)
                    mm.then_inc(d_ready, 1)

                for name, n in u.steps:
                    if name == "proj":
                        proj(n)
                    elif name == "moment":
                        moment(n)
                    elif name == "turn_heads":
                        turn_heads(n)
                    elif name == "self":
                        if n < H:
                            scores(n)
                        if 0 <= n - 3 < H:
                            turn(n - 3)
                        if 0 <= n - 4 < H:
                            values(n - 4)
                    elif name == "turn_out":
                        turn_out()
                    elif name == "out":
                        out()
                    elif name == "keys":
                        if n == 0 and u.x is None:
                            pe.wait_ge(loaded2, 16 * 7)
                            pe.wait_ge(prepared2, 1)
                        keys(n)
                    elif name == "vals":
                        vals(n)
                    elif name == "queries":
                        queries()
                    elif name == "cross":
                        if n < XH:
                            scores2(n)
                        if 0 <= n - 2 < XH:
                            turn2(n - 2)
                        if 0 <= n - 3 < XH:
                            values2(n - 3)
                    elif name == "turn_out2":
                        turn_out2()
                    elif name == "out2":
                        out2()
                    elif name == "x2t":
                        turn_x2()
                    elif name == "shared":
                        (shared_down if n else shared_up)()
                    elif name == "gate":
                        gate_logits()
                    elif name == "place" and n == 0:
                        places()
                for units, ready_sem in ((u.dn, d_ready), (u.an, a_ready)):
                    pads = len([k for k in units if k[0] == "pad"])
                    if pads:
                        pe.drain().then_inc(ready_sem, pads)

            for u in passes(pe):
                part_a(u)

            pe.wait_ge(d_done, all_d + RD)
            pe.wait_ge(a_done, all_a + RA)
            pe.wait_ge(o_done, all_o + RO)

            def turn_slots(e, s, i48):
                pe.wait_ge(ex_loaded[s % 4], i48 + 48)
                pe.wait_ge(xet_done, e + 1)
                for k in range(2):
                    for c in range(2):
                        mm = pe.transpose(bank[s % 2][:, k * CAP + c * P:k * CAP + (c + 1) * P],
                                          xe[:, s % 4, c, k * P:(k + 1) * P], ident)
                mm.then_inc(xet_ready, 1)

            def gate_up(e, s):
                pe.wait_ge(xet_done, e + 3)
                pe.wait_ge(he_ready, e + 1)
                for c in range(2):
                    for k in range(2):
                        mm = pe.matmul(bank[2 + s % 2][:, c * CAP:(c + 1) * CAP],
                                       we[:, s % 4, k, c * I:(c + 1) * I], xet[:, s % 4, k, :],
                                       start=(k == 0), stop=(k == 1))
                mm.then_inc(gu_ready, 1)

            def down(e, s):
                pe.wait_ge(he_ready, e + 3)
                pe.wait_ge(ye_done, e + 1)
                for c in range(2):
                    mm = pe.matmul(bank[4 + s % 2][:, c * D:(c + 1) * D], he[:, s % 4, c * P:(c + 1) * P],
                                   wd[:, s % 4, :], start=True, stop=True)
                mm.then_inc(ye_ready, 1)

            turn_slots(0, 0, 0)
            turn_slots(1, 1, 0)
            gate_up(0, 0)
            with pe.Fori(0, E // 4 - 1) as i:
                i4, i48 = pe.snap(4 * i), pe.snap(48 * i)
                for s in range(4):
                    turn_slots(i4 + (s + 2), s + 2, i48 + (48 if s >= 2 else 0))
                    gate_up(i4 + (s + 1), s + 1)
                    down(i4 + s, s)
            for s in range(4):
                if s < 2:
                    turn_slots(E - 4 + s + 2, s + 2, 48 * (E // 4 - 1))
                if s < 3:
                    gate_up(E - 4 + s + 1, s + 1)
                down(E - 4 + s, s)

        @block.scalar
        def _(act):
            act.wait_ge(loaded, 16 * 3)
            for r in range(RA):
                nc.scalar.copy(turn_a[:, r:r + 1], ident[:, 0:1]).then_inc(a_done, 1)

            def part_a(u):
                def ready(*n):
                    act.wait_ge(a_ready, u.a + (u.an[n] + 1))
                    return bank[u.a_bank(*n)]

                def exps(h):
                    act.wait_ge(d_done, u.d + (u.dn["x", h] + 1 + RD))
                    for j in range(TT):
                        cols = slice(0, P) if j == 0 else slice(P, 3 * P)
                        ins = nc.scalar.activation(pr[:, h % RING, cols], nl[:, h % RING, cols], ACT.Exp,
                                                   bias=nm[:, h % RING, j:j + 1], scale=-1.0,
                                                   accum_out=rs[:, j, h:h + 1])
                    ins.then_inc(probs_ready, 1)

                def exps2(h):
                    o = bank[u.a_bank("s", h)]
                    act.wait_ge(rowmax_ready, u.x16 + (h + 1))
                    for j in range(TT):
                        ins = nc.scalar.activation(pr[:, h % RING, j * T:(j + 1) * T], o[:, j * T:(j + 1) * T],
                                                   ACT.Exp, bias=nm2[:, h % RING, j:j + 1], scale=1.0,
                                                   accum_out=rs2[:, j, h:h + 1])
                    ins.then_inc(a_done, 1)

                for name, n in u.steps:
                    if name == "turn_heads":
                        for m, unit in enumerate(turned(n)):
                            if m % 2 == 0:
                                dst, src = turned_to(n, m, ready(*unit))
                                nc.scalar.copy(dst, src).then_inc(a_done, 1)
                    elif name == "self":
                        for h in {H: [H - 2, H - 1], H + 1: []}.get(n, [n - 2]):
                            if 0 <= h < H:
                                exps(h)
                        if 0 <= n - 4 < H and n % 2 == 0:
                            nc.scalar.copy(pt[:, n % RING, 0:384], ready("pt", n - 4)[:, 0:384]
                                           ).then_inc(a_done, 1)
                        if n < H:
                            nc.scalar.activation(ab[:, n % RING, :], ready("y", n)[:, 0:384], ACT.Abs
                                                 ).then_inc(a_done, 1)
                    elif name == "turn_out":
                        nc.scalar.copy(rit[:, :, :, :].rearrange("p f j t -> p (f j t)"), ready("ot")[:, :]
                                       ).then_inc(a_done, 1)
                    elif name == "keys":
                        nc.scalar.copy(kt2[:, 2 * n:2 * n + 2, :].rearrange("p c t -> p (c t)"),
                                       ready("k", n)[:, :]).then_inc(a_done, 1)
                    elif name == "vals":
                        nc.scalar.copy(v2[:, n // 2, n % 2 * 512:(n % 2 + 1) * 512], ready("v", n)[:, :]
                                       ).then_inc(a_done, 1)
                    elif name == "queries":
                        for c in range(4):
                            nc.scalar.copy(qt[:, 2 * c:2 * c + 2, :].rearrange("p c t -> p (c t)"),
                                           ready("q", c)[:, :]).then_inc(a_done, 1)
                        for p in range(len([k for k in u.an if k[0] == "pad"])):
                            nc.scalar.copy(turn_a[:, p:p + 1], ident[:, 0:1]).then_inc(a_done, 1)
                        act.drain().then_inc(queries_ready, 1)
                    elif name == "cross":
                        if 0 <= n - 3 < XH:
                            nc.scalar.copy(pt[:, (n - 3) % RING, :], ready("pt2", n - 3)[:, :]
                                           ).then_inc(a_done, 1)
                        if n < XH:
                            exps2(n)
                    elif name == "turn_out2":
                        for c in range(4):
                            nc.scalar.copy(o2t[:, 2 * c:2 * c + 2, :].rearrange("p c t -> p (c t)"),
                                           ready("o2t", c)[:, :]).then_inc(a_done, 1)
                    elif name == "shared" and n == 0:
                        o = ready("sg", 0)
                        nc.scalar.activation(sge[:, :], o[:, 0:T], ACT.Exp, scale=-1.0)
                        nc.scalar.copy(sgg[:, :], o[:, 0:T]).then_inc(a_done, 1)
                        nc.scalar.copy(sgu[:, :], ready("sg", 1)[:, 0:T]).then_inc(a_done, 1)
                    elif name == "choose" and n:
                        act.wait_ge(top_ready, u.x + 1)
                        for j in range(TT):
                            ins = nc.scalar.activation(ew[:, j, :], m8[:, j, 0:K], ACT.Exp, bias=nmx[:, j:j + 1],
                                                       scale=1.0, accum_out=ws[:, j:j + 1])
                        ins.then_inc(ew_ready, 1)
                if u.s is None:
                    for p in range(len([k for k in u.an if k[0] == "pad"])):
                        nc.scalar.copy(turn_a[:, p:p + 1], ident[:, 0:1]).then_inc(a_done, 1)

            for u in passes(act):
                part_a(u)

            act.sem_inc(ye_done, 2)
            act.sem_inc(ye_stored, 16)
            with act.Fori(0, E // 4) as i:
                i4, i64 = act.snap(4 * i), act.snap(64 * i)

                def silu(s):
                    act.wait_ge(gu_ready, i4 + (s + 1))
                    nc.scalar.activation(sl[:, s, :], bank[2 + s % 2][:, 0:CAP], ACT.Silu).then_inc(sl_ready, 1)

                def rows_out(s):
                    if s == 0:
                        act.wait_ge(ye_stored, i64 + 16)
                    act.wait_ge(ye_ready, i4 + (s + 1))
                    nc.scalar.copy(ye[:, s, :, :].rearrange("p c n -> p (c n)"), bank[4 + s % 2][:, :]
                                   ).then_inc(ye_done, 1)
                    act.wait_ge(ye_done, i4 + (s + 3))
                    act.dma_start(expert_rows[bass.ds((4 * i + s) * CAP, CAP), :].rearrange("(c p) n -> p c n", p=P),
                                  ye[:, s, :, :]).then_inc(ye_stored, 16)

                for s in range(5):
                    if s < 4:
                        silu(s)
                    if s >= 1:
                        rows_out(s - 1)

        @block.gpsimd
        def _(pool):
            pool.sem_inc(x2_free, 1)
            pool.memset(powers[:, :], -0.5).then_inc(pooled, 1)
            pool.wait_ge(pooled, 1)

            def part_a(u):
                base, count = None if u.s is None else (
                    u.s * SPLIT_STEPS if isinstance(u.s, int) else pool.snap(u.s * SPLIT_STEPS)), [0]

                def split_next(ins):
                    count[0] += 1
                    ins.then_inc(split_step, 1)
                    pool.wait_ge(split_step, base + count[0])

                for name, n in u.steps:
                    if name == "split" and n == 0:
                        pool.wait_ge(lines_asked, u.s + 1)
                        pool.tensor_tensor(rn[:, :], ss[:, :], powers[:, :], ALU.pow).then_inc(lines_done, 1)
                        pool.wait_ge(raw_ready, u.s + 1)
                        pool.tensor_tensor(turn_p[:, 2:3], powers[:, 0:1], powers[:, 0:1], ALU.mult
                                           ).then_inc(split_step, 1)
                        count[0] += 1
                        pool.wait_ge(split_step, base + count[0])
                        split([(raw[:, w, :, :], qks[:, w, :, :].rearrange("p h (b d) -> p h b d", d=DH), w)
                               for w in range(2)], pool.tensor_tensor, split_next
                              ).then_inc(split_ready, 1)
                    elif name == "split" and n == 1:
                        pool.wait_ge(outer_done, 2 * u.s + 2)
                        pool.tensor_tensor(turn_p[:, 5:6], powers[:, 0:1], powers[:, 0:1], ALU.mult
                                           ).then_inc(split_step, 1)
                        count[0] += 1
                        pool.wait_ge(split_step, base + count[0])
                        split([(lraw[:, 1, :, :], line_parts(1), 1)], pool.tensor_tensor, split_next
                              ).then_inc(lines_ready, 1)
                    elif name == "out":
                        pool.wait_ge(var1_asked, u.s + 1)
                        pool.tensor_tensor(rv[:, 0, :, 0], va[:, 0, :, 0], powers[:, 0:TT], ALU.pow
                                           ).then_inc(var1_done, 1)
                    elif name == "norm2" and n:
                        pool.wait_ge(var2_asked, u.x + 1)
                        pool.tensor_tensor(rv[:, 1, :, 0], va[:, 1, :, 0], powers[:, 0:TT], ALU.pow
                                           ).then_inc(var2_done, 1)
                    elif name == "place" and n == 1:
                        pool.wait_ge(zeroed, 16 * SLOTS * D // (P * 1024))
                        pool.wait_ge(slots_known, u.x + 1)
                        pool.tensor_tensor(turn_p[:, 0:1], powers[:, 0:1], powers[:, 0:1], ALU.mult)
                        for j in range(TT):
                            for k in range(K):
                                c = j * K + k
                                pool.indirect_dma_start(
                                    out=slots[:, :],
                                    out_offset=bass.IndirectOffsetOnAxis(ap=slot_i[:, c:c + 1], axis=0),
                                    in_=x2[:, j, :], in_offset=None).then_inc(scattered, 16)
                        pool.wait_ge(scattered, 16 * TT * K * u.x + 16 * TT * K)
                        pool.tensor_tensor(turn_p[:, 3:4], powers[:, 0:1], powers[:, 0:1], ALU.mult
                                           ).then_inc(x2_free, 1)

            for u in passes(pool):
                part_a(u)
            pool.wait_ge(ye_stored, 16 * E + 16)

            def gather(t, s):
                if not (isinstance(t, int) and t == 0):
                    pool.wait_ge(wait_taken, t)
                pool.wait_ge(picks_ready, t + 1)
                pool.tensor_tensor(turn_p[:, 1:2], powers[:, 0:1], powers[:, 0:1], ALU.mult
                                   ).then_inc(wait_taken, 1)
                for k in range(K):
                    pool.indirect_dma_start(
                        out=gr[:, s, k, :], out_offset=None, in_=expert_rows[:, :],
                        in_offset=bass.IndirectOffsetOnAxis(ap=rows_s[:, s, k:k + 1], axis=0),
                    ).then_inc(gathered[s], 16)

            def power3(i):
                pool.wait_ge(var_ready, i)
                pool.tensor_tensor(rv3[:, :], va3[:, :], powers[:, 0:NC], ALU.pow).then_inc(rstd_ready, 1)

            for s in range(NC):
                gather(s, s)
            with pool.Fori(1, N // P // NC) as i:
                t = pool.snap(NC * i)
                for s in range(NC):
                    gather(t + s, s)
                    if s == 1:
                        power3(i)
            power3(N // P // NC)

        @block.vector
        def _(dve):
            def tt(o, a, c, op):
                return nc.vector.tensor_tensor(o, a, c, op)

            nc.vector.memset(zero[:, :], 0.0).then_inc(prepared, 1)
            nc.vector.memset(lqk[:, :, :, :], 0.0)
            nc.vector.memset(v[:, :, :, :], 0.0)
            nc.vector.memset(nm[:, :, :], 0.0)
            nc.vector.memset(before[:, :], 0.0)
            nc.vector.memset(xp[:, :, 0:1], 0.0)
            nc.vector.memset(ones_b[:, :], 1.0)
            nc.vector.memset(ones[:, :], 1.0).then_inc(setup, 1)
            dve.wait_ge(loaded, 16 * 3)
            dve.wait_ge(setup, 1)
            nc.vector.tensor_scalar(sgn[:, :], bscale, 0.0, 2.0, ALU.is_ge, ALU.mult).then_inc(setup, 1)
            dve.wait_ge(setup, 2)
            nc.vector.tensor_scalar(sgn[:, :], sgn[:, :], -1.0, None, ALU.add).then_inc(setup, 1)
            dve.wait_ge(setup, 3)
            sg3 = sgn[:, :].unsqueeze(2).to_broadcast([P, H, DH])
            for w in (bqkv[:, 0:D], wall_s[:, 0, 0:D], wall_s[:, 1, 0:D]):
                w3 = w.rearrange("p (h d) -> p h d", d=DH)
                nc.vector.scalar_tensor_tensor(out=w3, in0=w3, scalar=float(DH) ** -0.5, in1=sg3,
                                               op0=ALU.mult, op1=ALU.mult).then_inc(prepared, 1)
            for h in range(H):
                nc.vector.tensor_scalar(mask_s[:, h, :], mask, sgn[:, h:h + 1], None, ALU.mult)
            nc.vector.tensor_scalar(nsgn[:, :], sgn[:, :], -1.0, None, ALU.mult)
            tt(absb[:, :], bscale, sgn[:, :], ALU.mult)
            nc.vector.tensor_copy(ident_b[:, :], ident)
            tt(before_b[:, :], tri, ident, ALU.subtract)
            nc.vector.tensor_copy(spare[:, :], spare0).then_inc(prepared, 1)
            dve.wait_ge(prepared, 5)
            for r in range(RD):
                nc.vector.memset(scratch[:, 3 + r:4 + r], 0.0).then_inc(d_done, 1)
            for r in range(RO):
                nc.vector.memset(scratch[:, 6 + r:7 + r], 0.0).then_inc(o_done, 1)

            def part_a(u):
                count = {"s": 0, "x": 0}
                s_base = None if u.s is None else (u.s * S_STEPS if isinstance(u.s, int) else dve.snap(u.s * S_STEPS))
                x_base = None if u.x is None else (u.x * X_STEPS if isinstance(u.x, int) else dve.snap(u.x * X_STEPS))

                def s_next(ins, carry=False):
                    count["s"] += 1
                    ins.then_inc(s_step, 1)
                    dve.wait_ge(s_step, s_base + count["s"])
                    if carry:
                        nc.vector.memset(scratch[:, 11:12], 0.0)

                def x_next(ins, carry=False):
                    count["x"] += 1
                    ins.then_inc(x_step, 1)
                    dve.wait_ge(x_step, x_base + count["x"])
                    if carry:
                        nc.vector.memset(scratch[:, 12:13], 0.0)

                def ready(*n):
                    dve.wait_ge(d_ready, u.d + (u.dn[n] + 1))
                    return bank[u.d_bank(*n)]

                def took(*n):
                    dve.wait_ge(d_done, u.d + (u.dn[n] + 1 + RD))

                half = TT * H

                def proj(j):
                    hs = slice(j * H, (j + 1) * H)
                    g1 = ready("g1", j)
                    tt(raw[:, :, hs, :], g1[:, :].rearrange("p (w h d) -> p w h d", w=2, d=DH),
                       bqkv[:, 0:2 * D].rearrange("p (w h d) -> p w h d", w=2, d=DH), ALU.add).then_inc(d_done, 1)
                    g2 = ready("g2", j)
                    for b in range(2):
                        def of(w):
                            return w.rearrange("p (a b d) -> p a b d", b=2, d=DH)[:, :, b, :]
                        tt(v[:, j, :, b * DH:(b + 1) * DH].rearrange("p (a b) d -> p a b d", b=2)[:, :, b, :],
                           of(g2[:, 0:D]), of(bqkv[:, 2 * D:3 * D]), ALU.add)
                    nc.vector.tensor_copy(lw[:, :, j * 64:(j + 1) * 64],
                                          g2[:, D:2 * D].rearrange("p (c n) -> p c n", c=4)).then_inc(d_done, 1)

                def points(c):
                    return lw[:, c, :].rearrange("p (h i) -> p h i", i=4)

                def lines0():
                    wide = [P, half, 4, 4]
                    took("g2", TT - 1)
                    nc.vector.memset(scratch[:, 15:16], 0.0).then_inc(raw_ready, 1)
                    for w, (p1, p2) in enumerate(((3, 0), (1, 2))):
                        ins = tt(pp[:, w, :, :, :], points(p1).unsqueeze(3).to_broadcast(wide),
                                 points(p2).unsqueeze(2).to_broadcast(wide), ALU.mult)
                    s_next(ins)

                def lines1():
                    for c, (i, k) in enumerate(((2, 3), (3, 1), (1, 2), (0, 3), (2, 0), (0, 1))):
                        tt(ll[:, 0, :, c:c + 1], pp[:, 0, :, i, k:k + 1], pp[:, 0, :, k, i:i + 1], ALU.subtract)
                    for c, i, n in ((0, 0, 3), (3, 1, 2), (5, 2, 1)):
                        ins = tt(ll[:, 1, :, c:c + n], pp[:, 1, :, i, i + 1:i + 1 + n],
                                 pp[:, 1, :, i + 1:i + 1 + n, i], ALU.subtract)
                    s_next(ins)

                def lines2():
                    lf = ll[:, :, :, :].rearrange("p w h c -> p (w h) c")
                    s_next(tt(sq[:, :, :], lf, lf, ALU.mult))
                    s_next(nc.vector.tensor_reduce(ss[:, :], sq[:, :, :], X, ALU.add))
                    nc.vector.tensor_scalar(ss[:, :], ss[:, :], 1e-24, None, ALU.max).then_inc(lines_asked, 1)

                def outer0():
                    dve.wait_ge(lines_done, u.s + 1)
                    tt(rd[:, :, :], ll[:, 1, :, :],
                       rn[:, half:2 * half].unsqueeze(2).to_broadcast([P, half, 6]), ALU.mult)
                    s_next(tt(lraw[:, 1, :, :], ll[:, 0, :, :],
                              rn[:, 0:half].unsqueeze(2).to_broadcast([P, half, 6]), ALU.mult))

                def outer1():
                    for j in range(TT):
                        jw = lraw[:, 1, j * H:(j + 1) * H, :]
                        tt(oo[:, j, :].rearrange("p (h a c) -> p h a c", a=6, c=6),
                           jw.unsqueeze(3).to_broadcast([P, H, 6, 6]), jw.unsqueeze(2).to_broadcast([P, H, 6, 6]),
                           ALU.mult).then_inc(outer_done, 1)

                def moment(j):
                    for f in range(2):
                        h0 = j * H + f * 8
                        tt(mr[:, 2 * j + f, :, :].rearrange("p (h a) c -> p h a c", a=6),
                           ready("m", j, f)[:, 0:288].rearrange("p (h a c) -> p h a c", a=6, c=6),
                           rd[:, h0:h0 + 8, :].unsqueeze(2).to_broadcast([P, 8, 6, 6]), ALU.mult
                           ).then_inc(d_done, 1)
                    took("m", j, 1)
                    hs = slice(j * H, (j + 1) * H)
                    s_next(nc.vector.tensor_reduce(
                        rm[:, hs, :].rearrange("p h c -> p (h c)"),
                        mr[:, 2 * j:2 * j + 2, :, :].rearrange("p a n c -> p (a n) c"), X, ALU.add))
                    s_next(tt(lraw[:, 0, hs, :], rm[:, hs, :], absb[:, :].unsqueeze(2).to_broadcast([P, H, 6]),
                              ALU.mult))

                def logits(h):
                    o = ready("x", h)
                    dve.wait_ge(a_done, u.a + (u.an["y", h] + 1 + RA))
                    nc.vector.memset(scratch[:, 32 + h:33 + h], 0.0)
                    for j in range(TT):
                        cols = slice(0, P) if j == 0 else slice(P, 3 * P)
                        ins = nc.vector.tensor_tensor_reduce(
                            out=nl[:, h % RING, cols], in0=ab[:, h % RING, cols], in1=o[:, cols],
                            scale=nsgn[:, h:h + 1], scalar=3e38, op0=ALU.add, op1=ALU.min,
                            accum_out=nm[:, h % RING, j:j + 1])
                    ins.then_inc(d_done, 1)

                def sums():
                    dve.wait_ge(probs_ready, u.s16 + H)
                    nc.vector.memset(scratch[:, 16:17], 0.0)
                    s_next(nc.vector.reciprocal(ri[:, :, :], rs[:, :, :]))
                    nc.vector.tensor_copy(rib[:, :, :].rearrange("p j (h d) -> p (j h) d", d=DH),
                                          ri[:, :, :].rearrange("p j h -> p (j h)").unsqueeze(2).to_broadcast(
                                              [P, TT * H, DH])).then_inc(sums_ready, 1)

                def outputs():
                    dve.wait_ge(a_done, u.a + (u.an["ot",] + 1 + RA))
                    nc.vector.memset(scratch[:, 17:18], 0.0)
                    for f in range(2):
                        dve.wait_ge(o_ready, u.o + (u.on["o", f] + 1))
                        tt(oht[:, f, :], bank[u.o_bank("o", f)][:, 0:T], rit[:, f, :, :].rearrange(
                            "p j t -> p (j t)"), ALU.mult).then_inc(o_done, 1)

                flat = "p j n -> p (j n)"

                def moments(w, src, nxt, asked):
                    for j in range(TT):
                        ins = nc.vector.bn_stats(st[:, w, j, :], src[:, j, :])
                    nxt(ins, carry=True)
                    for j in range(TT):
                        ins = nc.vector.bn_aggr(mv[:, w, j, :], st[:, w, j, :])
                    nxt(ins)
                    nc.vector.tensor_scalar(va[:, w, :, 0], mv[:, w, :, 1], EPS, None, ALU.add).then_inc(asked, 1)

                def apply(w, src, dst, done, at, ready_sem):
                    dve.wait_ge(done, at + 1)
                    for j in range(TT):
                        nc.vector.tensor_scalar(dst[:, j, :], src[:, j, :], mv[:, w, j, 0:1], rv[:, w, j, :],
                                                ALU.subtract, ALU.mult).then_inc(ready_sem, 1)

                def out():
                    dve.wait_ge(xr_loaded, 16 * u.s + 16)
                    s_next(tt(xr[:, :, :], xr[:, :, :], bout.unsqueeze(1).to_broadcast([P, TT, D]), ALU.add))
                    o = ready("out")
                    tt(y1[:, :, :].rearrange(flat), o[:, :], xr[:, :, :].rearrange(flat), ALU.add
                       ).then_inc(d_done, 1)
                    took("out")
                    moments(0, y1, s_next, var1_asked)

                def queries():
                    nc.vector.tensor_copy(x1t[:, :, :].rearrange("p k t -> p (k t)"), ready("x1t")[:, :]
                                          ).then_inc(d_done, 1)

                def rowmax(h):
                    dve.wait_ge(a_ready, u.a + (u.an["s", h] + 1))
                    nc.vector.tensor_reduce(nm2[:, h % RING, :], bank[u.a_bank("s", h)][:, :].rearrange(
                        "p (j t) -> p j t", j=TT), X, ALU.max, negate=True).then_inc(rowmax_ready, 1)

                def outputs2(n):
                    hs = slice(4 * n, 4 * n + 4)
                    dve.wait_ge(o_ready, u.o + (u.on["o2", n] + 1))
                    x_next(nc.vector.reciprocal(ri2[:, :, hs], rs2[:, :, hs]))
                    tt(o2[:, :, n * T:(n + 1) * T].rearrange("p j (h d) -> p j h d", d=XD),
                       bank[u.o_bank("o2", n)][:, :].rearrange("p (j h d) -> p j h d", j=TT, d=XD),
                       ri2[:, :, hs].unsqueeze(3).to_broadcast([P, TT, 4, XD]), ALU.mult).then_inc(o_done, 1)

                def out2():
                    x_next(tt(x1[:, :, :], x1[:, :, :], bo.unsqueeze(1).to_broadcast([P, TT, D]), ALU.add))
                    tt(y2[:, :, :].rearrange(flat), ready("out2")[:, :], x1[:, :, :].rearrange(flat), ALU.add
                       ).then_inc(d_done, 1)

                def norm2(half):
                    if half == 0:
                        took("out2")
                        moments(1, y2, x_next, var2_asked)
                    else:
                        dve.wait_ge(x2_free, u.x + 1)
                        apply(1, y2, x2, var2_done, u.x, x2_ready)

                def turn_x2():
                    nc.vector.tensor_copy(x2t[:, :, :].rearrange("p k t -> p (k t)"), ready("x2t")[:, :]
                                          ).then_inc(d_done, 1)

                def gate_logits():
                    nc.vector.tensor_copy(lg[:, :, :].rearrange("p j e -> p (j e)"), ready("lg")[:, 0:TT * E]
                                          ).then_inc(d_done, 1)
                    took("lg")
                    nc.vector.memset(scratch[:, 13:14], 0.0)

                def choose():
                    for j in range(TT):
                        ins = nc.vector.max(m8[:, j, :], lg[:, j, :])
                    x_next(ins)
                    nc.vector.tensor_scalar(nmx[:, :], m8[:, :, 0], -1.0, None, ALU.mult).then_inc(top_ready, 1)

                def choose_index():
                    for j in range(TT):
                        ins = nc.vector.max_index(i8[:, j, :], m8[:, j, :], lg[:, j, :])
                    x_next(ins)
                    x_next(nc.vector.tensor_copy(ix[:, :].rearrange("p (j k) -> p j k", k=K), i8[:, :, 0:K]))
                    many = [P, TT * K, E]
                    x_next(tt(hot[:, :, :], iota.unsqueeze(1).to_broadcast(many),
                              ix[:, :].unsqueeze(2).to_broadcast(many), ALU.is_equal))
                    for j in range(TT):
                        ins = nc.vector.tensor_reduce(
                            chosen[:, j, :], hot[:, j * K:(j + 1) * K, :].rearrange("p k e -> p e k"), X, ALU.max)
                    ins.then_inc(chosen_ready, 1)

                def shared_up():
                    dve.wait_ge(a_done, u.a + (u.an["sg", 1] + 1 + RA))
                    tt(sgr[:, :], sgg[:, :], sgu[:, :], ALU.mult)
                    x_next(nc.vector.tensor_scalar(sge[:, :], sge[:, :], 1.0, None, ALU.add))
                    x_next(nc.vector.reciprocal(sge[:, :], sge[:, :]))
                    tt(sgh[:, :], sgr[:, :], sge[:, :], ALU.mult).then_inc(sgh_ready, 1)

                def shared_down():
                    o = ready("sh")
                    b = slice(u.x, u.x + 1) if isinstance(u.x, int) else bass.ds(u.x, 1)
                    tt(base_all[:, b, :, :].rearrange("p o j n -> p (o j n)"), o[:, :],
                       x2[:, :, :].rearrange(flat), ALU.add).then_inc(d_done, 1)

                def places():
                    o = ready("pos")
                    for j in range(TT):
                        ks = slice(j * K, (j + 1) * K)
                        ins = tt(hp[:, ks, :], hot[:, ks, :], o[:, j * E:(j + 1) * E].unsqueeze(1)
                                 .to_broadcast([P, K, E]), ALU.mult)
                    ins.then_inc(d_done, 1)

                def places_found():
                    took("pos")
                    x_next(tt(before[:, :], before[:, :], chosen[:, 0, :], ALU.add))
                    tt(before[:, :], before[:, :], chosen[:, 1, :], ALU.add)
                    x_next(nc.vector.tensor_reduce(ps[:, :], hp[:, :, :], X, ALU.add))
                    nc.vector.tensor_scalar(vd[:, :], ps[:, :], float(CAP), None, ALU.is_lt)
                    nc.vector.scalar_tensor_tensor(out=fl[:, :], in0=ix[:, :], scalar=float(CAP), in1=ps[:, :],
                                                   op0=ALU.mult, op1=ALU.add)
                    x_next(nc.vector.tensor_scalar(gi[:, :], ps[:, :], float(CAP - 1), None, ALU.min))
                    nc.vector.scalar_tensor_tensor(out=gi[:, :], in0=ix[:, :], scalar=float(CAP), in1=gi[:, :],
                                                   op0=ALU.mult, op1=ALU.add)
                    x_next(tt(fd[:, :], fl[:, :], spare[:, :], ALU.subtract))
                    x_next(tt(fd[:, :], fd[:, :], vd[:, :], ALU.mult))
                    x_next(tt(fd[:, :], fd[:, :], spare[:, :], ALU.add))
                    nc.vector.tensor_copy(slot_i[:, :], fd[:, :]).then_inc(slots_known, 1)
                def weigh():
                    b = slice(u.x, u.x + 1) if isinstance(u.x, int) else bass.ds(u.x, 1)
                    nc.vector.tensor_copy(rows_all[:, b, :].rearrange("p o c -> p (o c)"), gi[:, :])
                    x_next(nc.vector.tensor_scalar(spare[:, :], spare[:, :], float(TT * P * K), None, ALU.add))
                    dve.wait_ge(ew_ready, u.x + 1)
                    x_next(nc.vector.reciprocal(wi[:, :], ws[:, :]))
                    x_next(tt(vd[:, :].rearrange("p (j k) -> p j k", k=K),
                              vd[:, :].rearrange("p (j k) -> p j k", k=K),
                              wi[:, :].unsqueeze(2).to_broadcast([P, TT, K]), ALU.mult))
                    x_next(tt(gates_all[:, b, :].rearrange("p o c -> p (o c)"), vd[:, :],
                              ew[:, :, :].rearrange("p j k -> p (j k)"), ALU.mult))

                for name, n in u.steps:
                    if name == "take_proj":
                        proj(n)
                    elif name == "lines":
                        (lines0, lines1, lines2)[n]()
                    elif name == "outer":
                        (outer1 if n else outer0)()
                    elif name == "take_moment":
                        moment(n)
                    elif name == "turn_heads":
                        for m, unit in enumerate(turned(n)):
                            if m % 2:
                                dst, src = turned_to(n, m, ready(*unit))
                                nc.vector.tensor_copy(dst, src).then_inc(d_done, 1)
                    elif name == "self":
                        if 0 <= n - 4 < H and n % 2:
                            nc.vector.tensor_copy(pt[:, n % RING, 0:384], ready("pt", n - 4)[:, 0:384]
                                                  ).then_inc(d_done, 1)
                        if n < H:
                            logits(n)
                    elif name == "sums":
                        sums()
                    elif name == "turn_out":
                        outputs()
                    elif name == "out":
                        out()
                    elif name == "queries":
                        queries()
                    elif name == "keys" and n == 0 and u.x is None:
                        dve.wait_ge(loaded2, 16 * 7)
                        nc.vector.tensor_scalar(wq_s[:, :, :], wq_s[:, :, :], float(XD) ** -0.5, None, ALU.mult
                                                ).then_inc(prepared2, 1)
                    elif name == "cross":
                        if n < XH:
                            rowmax(n)
                        if n in (7, 11, 15):
                            outputs2((n - 7) // 4)
                        if n == CROSS_SLOTS - 1:
                            outputs2(3)
                    elif name == "out2":
                        out2()
                    elif name == "norm1":
                        apply(0, y1, x1, var1_done, u.s, x1_ready)
                    elif name == "norm2":
                        norm2(n)
                    elif name == "x2t":
                        turn_x2()
                    elif name == "gate":
                        gate_logits()
                    elif name == "silu":
                        shared_up()
                    elif name == "shared" and n:
                        shared_down()
                    elif name == "choose":
                        (choose_index if n else choose)()
                    elif name == "place":
                        (places, places_found, weigh)[n]()
                    elif name == "split" and n == 2:
                        split([(lraw[:, 0, :, :], line_parts(0), 0)], tt, s_next).then_inc(lines_ready, 1)
                for p in range(len([k for k in u.dn if k[0] == "pad"])):
                    nc.vector.memset(scratch[:, 8 + p:9 + p], 0.0).then_inc(d_done, 1)
                assert count["s"] == (0 if u.s is None else S_STEPS), count
                assert count["x"] == (0 if u.x is None else X_STEPS), count

            for u in passes(dve):
                part_a(u)

            dve.sem_inc(xet_done, 2)
            dve.sem_inc(he_ready, 2)
            with dve.Fori(0, E // 4) as i:
                i4 = dve.snap(4 * i)

                def slots_turned(s):
                    dve.wait_ge(xet_ready, i4 + (s + 1))
                    nc.vector.tensor_copy(xet[:, s, :, :].rearrange("p k t -> p (k t)"), bank[s % 2][:, :]
                                          ).then_inc(xet_done, 1)

                def hidden(s):
                    dve.wait_ge(sl_ready, i4 + (s + 1))
                    tt(he[:, s, :], bank[2 + s % 2][:, CAP:2 * CAP], sl[:, s, :], ALU.mult).then_inc(he_ready, 1)

                slots_turned(0)
                for s in range(4):
                    if s < 3:
                        slots_turned(s + 1)
                    hidden(s)

            for s in range(NC):
                dve.sem_inc(stored[s], 16)
            FS = 6 * NC
            rows_flat = rows_all[:, :, :].rearrange("p b c -> p (b c)")
            gates_flat = gates_all[:, :, :].rearrange("p b c -> p (b c)")
            base_flat = base_all[:, :, :, :].rearrange("p b j n -> p (b j n)")

            def window(t, n):
                return slice(t * n, (t + 1) * n) if isinstance(t, int) else bass.ds(t * n, n)

            def pick(t, s):
                nc.vector.tensor_copy(gates_s[:, s, :], gates_flat[:, window(t, K)])
                nc.vector.tensor_copy(rows_s[:, s, :], rows_flat[:, window(t, K)]).then_inc(picks_ready, 1)

            def combine(i, last):
                fs, count = (i * FS if last else dve.snap(i * FS)), [0]

                def fin(ins, carry=False):
                    count[0] += 1
                    ins.then_inc(fin_step, 1)
                    dve.wait_ge(fin_step, fs + count[0])
                    if carry:
                        nc.vector.memset(scratch[:, 14:15], 0.0)

                for s in range(NC):
                    dve.wait_ge(gathered[s], 64 * i + 64)
                    prev = base_flat[:, window(NC * i + s, D)]
                    for k in range(K):
                        fin(nc.vector.scalar_tensor_tensor(out=acc[:, s, :], in0=gr[:, s, k, :],
                                                           scalar=gates_s[:, s, k:k + 1], in1=prev,
                                                           op0=ALU.mult, op1=ALU.add))
                        prev = acc[:, s, :]
                    if not last:
                        pick(NC * i + (NC + s), s)
                    fin(nc.vector.bn_stats(st3[:, s, :], acc[:, s, :]), carry=True)
                    fin(nc.vector.bn_aggr(mv3[:, s, :], st3[:, s, :]))
                nc.vector.tensor_scalar(va3[:, :], mv3[:, :, 1], EPS, None, ALU.add).then_inc(var_ready, 1)
                dve.wait_ge(rstd_ready, i + 1)
                for s in range(NC):
                    dve.wait_ge(stored[s], 16 * i + 16)
                    nc.vector.tensor_scalar(yo[:, s, :], acc[:, s, :], mv3[:, s, 0:1], rv3[:, s:s + 1],
                                            ALU.subtract, ALU.mult).then_inc(yo_ready, 1)
                if not last:
                    dve.wait_ge(yo_ready, dve.snap(NC * i) + NC)
                assert count[0] == FS, count

            for s in range(NC):
                pick(s, s)
            with dve.Fori(0, N // P // NC - 1) as i:
                combine(i, False)
            combine(N // P // NC - 1, True)


def kernel(**a):
    import concourse.bacc as _bacc
    from concourse.bass_utils import run_bass_kernel_spmd as _run

    a = {k: np.asarray(v) for k, v in a.items()}

    def rows(v):
        return np.broadcast_to(v.reshape(1, -1), (P, v.size))

    r = np.arange(P)
    spare = SLOTS + (np.arange(TT)[None, :, None] * P + r[:, None, None]) * K + np.arange(K)
    const = np.concatenate([
        np.eye(P), r[:, None] <= r[None, :], np.where(r[None, :] > r[:, None], NEG, 0.0),
        np.broadcast_to(np.arange(E), (P, E)), spare.reshape(P, TT * K)], axis=1).astype(np.float32)
    x = a["x"]
    arrays = {
        "x": x,
        "xT": x.transpose(0, 2, 1),
        "ctxT": a["ctx_768"].transpose(0, 2, 1),
        "wall": np.concatenate([a["L0_attn_Wqkv"], a["L0_attn_W2w"], a["L0_attn_W1r"], a["L0_attn_W2r"],
                                a["L0_attn_W1w"]], axis=0).T,
        "bias": np.concatenate([rows(a["L0_attn_bqkv"]), rows(a["L0_attn_bout"]), rows(a["L0_xattn_b_out"]),
                                rows(a["L0_attn_bias_scale"])], axis=1),
        "wout": a["L0_attn_Wout"].T,
        "wq": a["L0_xattn_w_q"],
        "wkv": a["L0_xattn_w_kv"],
        "wo": a["L0_xattn_w_out"],
        "gate": a["L0_ffn_gate_w"].T,
        "wgu": a["L0_ffn_w_gate_up"],
        "wdn": a["L0_ffn_w_down"],
        "shgu": a["L0_ffn_shared_w_gate_up"],
        "shdn": a["L0_ffn_shared_w_down"],
        "const": const,
    }
    nc = _bacc.Bacc("TRN2", target_bir_lowering=False, num_devices=1)
    args = []
    for name, v in arrays.items():
        arrays[name] = v = np.ascontiguousarray(v)
        args.append(nc.dram_tensor(name, v.shape, mybir.dt.from_np(v.dtype), kind="ExternalInput").ap())
    args.append(nc.dram_tensor("out", (N, D), F32, kind="ExternalOutput").ap())
    build(nc, *args)
    got = _run(nc, [arrays], core_ids=[0])
    return got.results[0]["out"].reshape(B, T, D)
```

```python
from contextlib import ExitStack

import numpy as np

import concourse.bass as bass
from concourse import mybir

F32 = mybir.dt.float32
BF16 = mybir.dt.bfloat16
U32 = mybir.dt.uint32
ALU = mybir.AluOpType
ACT = mybir.ActivationFunctionType
X = mybir.AxisListType.X

P = 128
B, T, D = 8, 256, 256
TT = T // P
H, DH = 16, 16
XH, XD = 16, 64
C = 192
CP = C // 2
E, K, CAP, I = 32, 4, 256, 128
N = B * T
SLOTS = E * CAP
EPS = 1e-5
NEG = -1e30

RD, RA, RO = 3, 3, 2
PARTS = 6
FIRST_STEPS = 3
SPLIT_STEPS = 8
RING = 4
S_STEPS, X_STEPS = 16, 23
CROSS_SLOTS, SELF_SLOTS = XH + 3, H + 5


def schedule(self_part, cross_part):
    steps = []
    beside_cross = {0: [("proj", 0)], 1: [("take_proj", 0), ("proj", 1)], 2: [("take_proj", 1)],
                    3: [("lines", 0)], 4: [("lines", 1)], 5: [("lines", 2), ("split", 0)],
                    10: [("outer", 0)], 12: [("outer", 1)], 13: [("moment", 0)],
                    14: [("take_moment", 0), ("moment", 1)], 16: [("take_moment", 1)], 17: [("split", 2)], 18: [("split", 1)]}
    beside_self = {1: [("out2", 0)], 3: [("norm2", 0)], 5: [("norm2", 1)], 7: [("x2t", 0)], 14: [("shared", 0)],
                   9: [("gate", 0)], 16: [("choose", 0)]}
    for n in range(CROSS_SLOTS):
        if cross_part:
            steps.append(("cross", n))
        if self_part:
            steps += beside_cross.get(n, [])
            if not cross_part and n == 4:
                steps += [("keys", c) for c in range(4)]
    steps += [("turn_heads", 0)] if self_part else []
    steps += [("turn_out2", 0)] if cross_part else []
    steps += [("turn_heads", w) for w in (1, 2, 3)] if self_part else []
    if not self_part:
        return steps + [("out2", 0), ("norm2", 0), ("norm2", 1), ("x2t", 0), ("gate", 0), ("choose", 0), ("choose", 1),
                        ("place", 0), ("shared", 0), ("place", 1), ("silu", 0), ("shared", 1), ("place", 2)]
    for n in range(SELF_SLOTS):
        if self_part:
            steps.append(("self", n))
        if cross_part:
            steps += beside_self.get(n, [])
        if self_part and cross_part and n == H:
            steps += [("keys", 0), ("keys", 1)]
        if self_part and n == H + 1:
            steps += [("sums", 0)]
        if self_part and cross_part and n == H + 2:
            steps += [("keys", 2), ("keys", 3)]
    tail = [("turn_out", 0), ("choose", 1), ("vals", 0), ("out", 0), ("vals", 1), ("norm1", 0), ("vals", 2),
            ("place", 0), ("vals", 3), ("queries", 0), ("place", 1), ("silu", 0), ("shared", 1), ("place", 2)]
    steps += [s for s in tail if (cross_part if s[0] in ("choose", "place", "silu", "shared") else self_part)]
    return steps


def turned(w):
    return [("t", w, n) for n in range(2 * TT if w < 2 else TT)]


def plan(steps):
    d, a, o = [], [], []
    for name, n in steps:
        if name == "proj":
            d += [("g1", n), ("g2", n)]
        elif name == "moment":
            d += [("m", n, f) for f in range(2)]
        elif name == "turn_heads":
            a += turned(n)[0::2]
            d += turned(n)[1::2]
        elif name == "self":
            if n < H:
                d.append(("x", n))
                a.append(("y", n))
            if 0 <= n - 3 < H:
                (a if n % 2 else d).append(("pt", n - 3))
            if n == 5:
                o += [("o", 0), ("o", 1)]
        elif name == "cross":
            if n < XH:
                a.append(("s", n))
            if 0 <= n - 2 < XH:
                a.append(("pt2", n - 2))
            if n == 3:
                o += [("o2", g) for g in range(4)]
        elif name == "turn_out":
            a.append(("ot",))
        elif name == "out":
            d.append(("out",))
        elif name == "keys":
            a.append(("k", n))
        elif name == "vals":
            a.append(("v", n))
        elif name == "queries":
            d.append(("x1t",))
            a += [("q", c) for c in range(4)]
        elif name == "turn_out2":
            a += [("o2t", c) for c in range(4)]
        elif name == "out2":
            d.append(("out2",))
        elif name == "x2t":
            d.append(("x2t",))
        elif name == "gate":
            d.append(("lg",))
        elif name == "shared" and n == 0:
            a += [("sg", 0), ("sg", 1)]
        elif name == "shared":
            d.append(("sh",))
        elif name == "place" and n == 0:
            d.append(("pos",))
    d += [("pad", n) for n in range(-len(d) % RD)]
    a += [("pad", n) for n in range(-len(a) % RA)]
    assert len(o) % RO == 0
    return [{u: n for n, u in enumerate(r)} for r in (d, a, o)]


class Pass:

    def __init__(self, eng, steps, before, each, i, s, x):
        self.steps, (self.dn, self.an, self.on), self.s, self.x = steps, plan(steps), s, x
        snap = (lambda v: v) if i is None else eng.snap
        self.d, self.a, self.o = (snap(before[r] + (0 if i is None else (i - 1) * each[r])) for r in range(3))
        self.s16 = None if s is None else snap(s * 16)
        self.x16 = None if x is None else snap(x * 16)

    def d_bank(self, *u):
        return self.dn[u] % RD

    def a_bank(self, *u):
        return RD + self.an[u] % RA

    def o_bank(self, *u):
        return RD + RA + self.on[u] % RO


def passes(eng):
    first, mid, last = (schedule(*k) for k in ((True, False), (True, True), (False, True)))
    n_first, n_mid = ([len(r) for r in plan(k)] for k in (first, mid))
    yield Pass(eng, first, [0, 0, 0], None, None, 0, None)
    with eng.Fori(1, B) as i:
        yield Pass(eng, mid, n_first, n_mid, i, i, i - 1)
    yield Pass(eng, last, [f + (B - 1) * m for f, m in zip(n_first, n_mid)], None, None, None, B - 1)


def totals():
    counts = [[len(r) for r in plan(schedule(*k))] for k in ((True, False), (True, True), (False, True))]
    return [f + (B - 1) * m + t for f, m, t in zip(*counts)]


def build(nc, x, xT, ctxT, wall, bias, wout, wq, wkv, wo, gate, wgu, wdn, shgu, shdn, const, own, out):
    all_d, all_a, all_o = totals()
    ctx = ExitStack()
    with ctx:
        def sb(name, shape, dt=F32):
            return ctx.enter_context(nc.sbuf_tensor(name, shape, dt))

        def sem(name):
            return ctx.enter_context(nc.semaphore(name))

        bank = [ctx.enter_context(nc.psum_tensor(f"bank{i}", [P, 512], F32)) for i in range(8)]
        slots = nc.dram_tensor("slots", [SLOTS + N * K, D], F32, kind="Internal").ap()
        owners = nc.dram_tensor("owners", [SLOTS + N * K, 1], F32, kind="Internal").ap()
        by_token = nc.dram_tensor("by_token", [SLOTS + N * K, D], F32, kind="Internal").ap()

        cst = sb("cst", [P, 3 * P + E + TT * K])
        ident, tri, mask = cst[:, 0:P], cst[:, P:2 * P], cst[:, 2 * P:3 * P]
        iota, spare0 = cst[:, 3 * P:3 * P + E], cst[:, 3 * P + E:]
        ident_b = sb("ident_b", [P, P], BF16)
        before_b = sb("before_b", [P, P], BF16)
        ones_b = sb("ones_b", [P, P], BF16)
        ones = sb("ones", [P, P])
        mask_s = sb("mask_s", [P, H, P], BF16)
        wall_s = sb("wall_s", [P, 2, 1024])
        bias_s = sb("bias_s", [P, 3 * D + 2 * D + H])
        bqkv, bout, bo = bias_s[:, 0:3 * D], bias_s[:, 3 * D:4 * D], bias_s[:, 4 * D:5 * D]
        bscale = bias_s[:, 5 * D:]
        sgn, nsgn, absb = sb("sgn", [P, H]), sb("nsgn", [P, H]), sb("absb", [P, H])
        wout_s = sb("wout_s", [P, 2, D])
        wq_s = sb("wq_s", [P, 2, XH * XD])
        wkv_s = sb("wkv_s", [CP, 2, 2 * XH * XD])
        wo_s = sb("wo_s", [P, 8, D])
        gate_s = sb("gate_s", [P, 2, E])
        shgu_s, shdn_s = sb("shgu_s", [P, 2, 2 * I]), sb("shdn_s", [P, D])
        powers = sb("powers", [P, 2 * TT * H])
        zero = sb("zero", [P, 1024])
        scratch, turn_p, turn_a = sb("scratch", [P, 64]), sb("turn_p", [P, 16]), sb("turn_a", [P, 4])

        xp = sb("xp", [P, 2, T + 1])
        xr = sb("xr", [P, TT, D])
        ct = sb("ct", [CP, 2, T])
        raw = sb("raw", [P, 2, TT * H, DH])
        lraw = sb("lraw", [P, 2, TT * H, 6])
        qks = sb("qks", [P, 2, TT * H, PARTS * DH], BF16)
        lqk = sb("lqk", [P, 2, TT * H, 64], BF16)
        v = sb("v", [P, TT, H, 2 * DH])
        lw = sb("lw", [P, 4, TT * 64])
        ll = sb("ll", [P, 2, TT * H, 6])
        ss = sb("ss", [P, 2 * TT * H])
        rn = sb("rn", [P, 2 * TT * H])
        rd = sb("rd", [P, TT * H, 6])
        oo = sb("oo", [P, TT, H * 36])
        sq = oo[:, :, :].rearrange("p j n -> p (j n)")[:, 0:2 * TT * H * 6].rearrange("p (h c) -> p h c", c=6)
        mr = sb("mr", [P, TT * 2, 8 * 6, 6])
        pp = mr[:, :, :, :].rearrange("p a n c -> p (a n c)")[:, 0:2 * TT * H * 16].rearrange(
            "p (w h i k) -> p w h i k", w=2, i=4, k=4)
        rm = sb("rm", [P, TT * H, 6])
        lqt, lkt = sb("lqt", [P, H // 2, T], BF16), sb("lkt", [P, H // 2, T], BF16)
        abnl = sb("abnl", [P, 2 * RING * 384])
        ab = abnl[:, 0:RING * 384].rearrange("p (r n) -> p r n", r=RING)
        nl = abnl[:, RING * 384:].rearrange("p (r n) -> p r n", r=RING)
        nm = sb("nm", [P, RING, TT])
        prpt = sb("prpt", [P, 2 * RING * 512])
        pr = prpt[:, 0:RING * 512].rearrange("p (r n) -> p r n", r=RING)
        pt = prpt[:, RING * 512:].rearrange("p (r n) -> p r n", r=RING)
        rs, ri = sb("rs", [P, TT, H]), sb("ri", [P, TT, H])
        oht = sb("oht", [P, 2, T])
        y1, y2 = sb("y1", [P, TT, D]), sb("y2", [P, TT, D])
        rib = y1
        rit = y2[:, :, :].rearrange("p f (j t) -> p f j t", j=TT)
        st, mv, va, rv = (sb(n, [P, 2, TT, w]) for n, w in (("st", 6), ("mv", 2), ("va", 1), ("rv", 1)))
        x1 = sb("x1", [P, TT, D])
        x1t = sb("x1t", [P, 2, T])
        kt2 = sb("kt2", [P, 8, T])
        qt = abnl[:, 0:8 * T].rearrange("p (c t) -> p c t", c=8)
        v2 = sb("v2", [P, TT, XH * XD])
        nm2 = sb("nm2", [P, RING, TT])
        rs2, ri2 = sb("rs2", [P, TT, XH]), sb("ri2", [P, TT, XH])
        o2 = sb("o2", [P, TT, XH * XD])
        o2t = kt2
        st_q, st_k = (w[:, :, :].rearrange("p j n -> p (j n)").bitcast(BF16).rearrange("p (h t) -> p h t", h=H)
                      for w in (v2, o2))
        x2 = sb("x2", [P, TT, D])
        x2t = sb("x2t", [P, 2, T])
        lg, m8 = sb("lg", [P, TT, E]), sb("m8", [P, TT, 8])
        i8 = sb("i8", [P, TT, 8], U32)
        ix = sb("ix", [P, TT * K])
        nmx, ew, ws, wi = sb("nmx", [P, TT]), sb("ew", [P, TT, K]), sb("ws", [P, TT]), sb("wi", [P, TT])
        hot = sb("hot", [P, TT * K, E])
        hp = sb("hp", [P, TT * K, E])
        chosen = sb("chosen", [P, TT, E], BF16)
        before = sb("before", [P, E], BF16)
        ps, vd, fl, fd, ids = (sb(n, [P, TT * K]) for n in ("ps", "vd", "fl", "fd", "ids"))
        spare = sb("spare", [P, TT * K])
        slot_i = sb("slot_i", [P, TT * K], U32)
        sge, sgg, sgu, sgr = (mr[:, n, :, :].rearrange("p a c -> p (a c)")[:, 0:T] for n in range(4))
        sgh = sb("sgh", [P, T])
        base_all = sb("base_all", [P, B, TT, D])
        gates_all = sb("gates_all", [P, B, TT * K])
        NS = SLOTS // P
        own_s = ones[0:NS, :]
        own_i, own_now = (hp[:, :, :].rearrange("p k e -> p (k e)")[:, w].bitcast(U32)
                          for w in (slice(0, NS), slice(NS, NS + 2 * 8)))

        NE = 8
        we = prpt[:, :].rearrange("p (s k n) -> p s k n", s=NE, k=2)
        wd = qks[:, :, :, :].rearrange("p w h n -> p (w h n)")[:, 0:NE * D * 2].bitcast(F32).rearrange(
            "p (s n) -> p s n", s=NE)
        xe = [w.rearrange("p (s c n) -> p s c n", c=2, n=D)[:, s, :, :] for w in (
            abnl[:, 0:NE // 2 * 2 * D], wall_s[:, :, :].rearrange("p k n -> p (k n)")) for s in range(NE // 2)]
        xet = o2[:, :, :].rearrange("p j (a n) -> p (j a) n", n=CAP).rearrange("p (s c) n -> p s c n", c=2)
        ye = o2t[:, :, :].rearrange("p (s c) n -> p s c n", c=2)
        sl = v2[:, 0, :].rearrange("p (s n) -> p s n", s=4)
        he = v2[:, 1, :].rearrange("p (s n) -> p s n", s=4)
        NC = 4
        ROUNDS, COMBINE_STEPS = N // P // NC, NC * (K + 2)
        gr = [w.rearrange("p (s c n) -> p s c n", c=K, n=D)[:, s, :, :] for w, n in (
            (prpt[:, :], NC), (abnl[:, 0:NC // 2 * K * D], NC // 2),
            (wall_s[:, :, :].rearrange("p k n -> p (k n)"), NC // 2)) for s in range(n)]
        acc, yo = (w[:, :, :].rearrange("p j (s n) -> p j s n", s=NC) for w in (v2, o2))
        st3, mv3, va3, rv3 = (sb("st3", [P, N // P, 6]), sb("mv3", [P, N // P, 2]), sb("va3", [P, N // P]),
                              sb("rv3", [P, N // P]))

        loaded, loaded2, zeroed = sem("loaded"), sem("loaded2"), sem("zeroed")
        prepared, prepared2, pooled = sem("prepared"), sem("prepared2"), sem("pooled")
        setup = sem("setup")
        xt_loaded, xr_loaded, ctx_loaded = sem("xt_loaded"), sem("xr_loaded"), sem("ctx_loaded")
        xt_used, ctx_used = sem("xt_used"), sem("ctx_used")
        d_ready, d_done = sem("d_ready"), sem("d_done")
        a_ready, a_done = sem("a_ready"), sem("a_done")
        o_ready, o_done = sem("o_ready"), sem("o_done")
        s_step, x_step = sem("s_step"), sem("x_step")
        lines_asked, lines_done = sem("lines_asked"), sem("lines_done")
        var1_asked, var1_done = sem("var1_asked"), sem("var1_done")
        var2_asked, var2_done = sem("var2_asked"), sem("var2_done")
        outer_done = sem("outer_done")
        raw_ready, lines_ready = sem("raw_ready"), sem("lines_ready")
        split_step, split_ready, heads_turned = sem("split_step"), sem("split_ready"), sem("heads_turned")
        probs_ready, sums_ready = sem("probs_ready"), sem("sums_ready")
        x1_ready, rowmax_ready = sem("x1_ready"), sem("rowmax_ready")
        x2_ready, top_ready, ew_ready, chosen_ready = (sem("x2_ready"), sem("top_ready"), sem("ew_ready"),
                                                       sem("chosen_ready"))
        queries_ready = sem("queries_ready")
        sgh_ready = sem("sgh_ready")
        slots_known, scattered, x2_free = sem("slots_known"), sem("scattered"), sem("x2_free")
        owned = sem("owned")
        routed = sem("routed")
        ex_loaded = [sem(f"ex_loaded{s}") for s in range(NE)]
        xet_ready, xet_done = sem("xet_ready"), sem("xet_done")
        gu_ready, sl_ready, he_ready = sem("gu_ready"), sem("sl_ready"), sem("he_ready")
        ye_ready, ye_done, ye_stored = sem("ye_ready"), sem("ye_done"), [sem(f"ye_stored{s}") for s in range(4)]
        own_loaded, own_turned, own_ready, own_step = (sem("own_loaded"), sem("own_turned"), sem("own_ready"),
                                                       sem("own_step"))
        gathered = [sem(f"gathered{s}") for s in range(2 * NC)]
        var_ready, rstd_ready = sem("var_ready"), sem("rstd_ready")
        yo_ready, fin_step = sem("yo_ready"), sem("fin_step")
        stored = [sem(f"stored{s}") for s in range(2 * NC)]

        def split(tasks, tensor_tensor, then):
            one = ones[:, 0:1].unsqueeze(2).unsqueeze(3)
            for step in range(4):
                for x, p, w in tasks:
                    wide = p.rearrange("p h (a c) d -> p h a c d", c=2)
                    p1 = p[:, :, 3:6, :] if w == 0 else wide[:, :, :, 0, :]
                    p2 = p[:, :, 0:2, :] if w == 0 else wide[:, :, 0:2, 1, :]
                    p3 = p[:, :, 2, :] if w == 0 else p[:, :, 5, :]
                    if step == 0:
                        ins = tensor_tensor(p1, x.unsqueeze(2).to_broadcast(list(p1.shape)),
                                            one.to_broadcast(list(p1.shape)), ALU.mult)
                    elif step == 1:
                        ins = tensor_tensor(x, x, p1[:, :, 0, :], ALU.subtract)
                    elif step == 2:
                        ins = tensor_tensor(p2, x.unsqueeze(2).to_broadcast(list(p2.shape)),
                                            one.to_broadcast(list(p2.shape)), ALU.mult)
                    else:
                        ins = tensor_tensor(p3, x, p2[:, :, 0, :], ALU.subtract)
                if step < 3:
                    then(ins)
            return ins

        def line_parts(w):
            return lqk[:, w, :, 0:PARTS * 6].rearrange("p h (b d) -> p h b d", d=6)

        heads = [(raw[:, w, :, :], qks[:, w, :, :].rearrange("p h (b d) -> p h b d", d=DH), w) for w in range(2)]

        def turned_to(w, n, o):
            o = o[:, :].bitcast(BF16).rearrange("p (g t) -> p g t", g=8)
            if w < 2:
                j, f = n // 2, n % 2
                rows = slice(0, PARTS * DH)
                return (st_q, st_k)[w][rows, 8 * f:8 * f + 8, j * P:(j + 1) * P], o[rows, :, :]
            return (lqt, lkt)[w - 2][:, :, n * P:(n + 1) * P], o

        WARM = (2, 2, 1)
        OWN_AT = 3
        ZEROED = 16 * (2 * SLOTS * D // (P * 1024) + 1)
        block = ctx.enter_context(nc.Block())

        @block.sync
        def _(sp):
            sp.dma_start(cst[:, :], const).then_inc(loaded, 16)
            sp.dma_start(bias_s[:, :], bias).then_inc(loaded, 16)
            sp.dma_start(wall_s[:, :, :], wall.rearrange("(k p) n -> p k n", p=P)).then_inc(loaded, 16)
            sp.dma_start(xp[:, :, 1:T + 1], xT[0, :, :].rearrange("(k p) t -> p k t", p=P)).then_inc(xt_loaded, 16)
            for dst, src in (
                (wkv_s[:, :, :], wkv.rearrange("(k p) n -> p k n", p=CP)),
                (wout_s[:, :, :], wout.rearrange("(k p) n -> p k n", p=P)),
                (wq_s[:, :, :], wq.rearrange("(k p) n -> p k n", p=P)),
                (wo_s[:, :, :], wo.rearrange("(k p) n -> p k n", p=P)),
                (gate_s[:, :, :], gate.rearrange("(k p) n -> p k n", p=P)),
                (shgu_s[:, :, :], shgu.rearrange("(k p) n -> p k n", p=P)),
                (shdn_s[:, :], shdn),
            ):
                sp.dma_start(dst, src).then_inc(loaded2, 16)
            sp.dma_start(ct[:, :, :], ctxT[0, :, :].rearrange("(k p) t -> p k t", p=CP)).then_inc(ctx_loaded, 16)
            sp.dma_start(xr[:, :, :], x[0, :, :].rearrange("(j p) n -> p j n", p=P)).then_inc(xr_loaded, 16)
            sp.wait_ge(prepared, 1)
            rows = 1024 // D
            for c in range(SLOTS // (P * rows)):
                sp.dma_start(slots[c * P * rows:(c + 1) * P * rows, :].rearrange("(p r) n -> p (r n)", p=P),
                             zero[:, :]).then_inc(zeroed, 16)
                sp.dma_start(by_token[SLOTS + c * P * rows:SLOTS + (c + 1) * P * rows, :].rearrange(
                    "(p r) n -> p (r n)", p=P), zero[:, :]).then_inc(zeroed, 16)
            sp.dma_start(owners[0:SLOTS, :].rearrange("(a b) o -> a (b o)", b=P),
                         own.rearrange("(a b) o -> a (b o)", b=P)).then_inc(zeroed, 16)
            with sp.Fori(1, B) as b:
                sp.wait_ge(xt_used, b)
                sp.dma_start(xp[:, :, 1:T + 1], xT[bass.ds(b, 1), :, :].rearrange("o (k p) t -> p (o k) t", p=P)
                             ).then_inc(xt_loaded, 16)
                sp.wait_ge(ctx_used, b)
                sp.dma_start(ct[:, :, :], ctxT[bass.ds(b, 1), :, :].rearrange("o (k p) t -> p (o k) t", p=CP)
                             ).then_inc(ctx_loaded, 16)
                sp.wait_ge(s_step, S_STEPS * b + FIRST_STEPS)
                sp.dma_start(xr[:, :, :], x[bass.ds(b, 1), :, :].rearrange("o (j p) n -> p (o j) n", p=P)
                             ).then_inc(xr_loaded, 16)

            def load_expert(e, s):
                sp.dma_start(we[:, s, :, :], wgu[e, :, :].rearrange("o (k p) n -> p (o k) n", p=P)
                             ).then_inc(ex_loaded[s], 16)
                sp.dma_start(wd[:, s, :], wdn[e, :, :].rearrange("o p n -> p (o n)")
                             ).then_inc(ex_loaded[s], 16)

            def load_slots(c, s):
                sp.dma_start(xe[s], slots[c, :].rearrange("(k p) n -> p k n", p=P)
                             ).then_inc(ex_loaded[s], 16)

            sp.wait_ge(zeroed, ZEROED)
            sp.wait_ge(o_done, all_o + RO)
            for s in range(NE):
                load_expert(slice(s, s + 1), s)
            sp.wait_ge(scattered, 16 * N * K // P)
            for s in range(NE):
                load_slots(slice(s * CAP, (s + 1) * CAP), s)
            sp.wait_ge(owned, 16 * N * K // P)
            sp.dma_start(own_s[:, :], owners[0:SLOTS, :].rearrange("(a b) o -> a (b o)", b=P)).then_inc(own_loaded, 16)
            with sp.Fori(1, E // NE) as i:
                for s in range(NE):
                    sp.wait_ge(ye_ready, NE * i + (s - NE + 1))
                    load_expert(bass.ds(NE * i + s, 1), s)
                    load_slots(bass.ds((NE * i + s) * CAP, CAP), s)
            for t in range(N // P):
                sp.wait_ge(yo_ready, t + 1)
                sp.dma_start(out[t * P:(t + 1) * P, :], yo[:, t // NC % 2, t % NC, :]).then_inc(stored[t % (2 * NC)], 16)
            for s in range(2 * NC):
                sp.wait_ge(stored[s], 16 * ROUNDS // 2)

        @block.tensor
        def _(pe):
            pe.wait_ge(loaded, 16 * 3)
            pe.wait_ge(prepared, 4)

            def part_a(u):
                def d_free(*n):
                    pe.wait_ge(d_done, u.d + (u.dn[n] + 1))
                    return bank[u.d_bank(*n)]

                def a_free(*n):
                    pe.wait_ge(a_done, u.a + (u.an[n] + 1))
                    return bank[u.a_bank(*n)]

                def o_free(*n):
                    pe.wait_ge(o_done, u.o + (u.on[n] + 1))

                def o_bank(*n):
                    return bank[u.o_bank(*n)]

                def vec_took(*n):
                    pe.wait_ge(d_done, u.d + (u.dn[n] + 1 + RD))

                def act_took(*n):
                    pe.wait_ge(a_done, u.a + (u.an[n] + 1 + RA))

                def divided(*n):
                    pe.wait_ge(o_done, u.o + (u.on[n] + 1 + RO))

                def proj(j):
                    if j == 0:
                        pe.wait_ge(xt_loaded, 16 * u.s + 16)
                    o = d_free("g1", j)
                    for k in range(2):
                        mm = pe.matmul(o[:, :], xp[:, k, 1 + j * P:1 + (j + 1) * P],
                                       wall_s[:, k, 0:512], start=(k == 0), stop=(k == 1))
                    mm.then_inc(d_ready, 1)
                    o = d_free("g2", j)
                    for k in range(2):
                        pe.matmul(o[:, 0:448], xp[:, k, 1 + j * P:1 + (j + 1) * P],
                                  wall_s[:, k, 512:960], start=(k == 0), stop=(k == 1))
                    for k in range(2):
                        mm = pe.matmul(o[:, 448:512], xp[:, k, j * P:(j + 1) * P],
                                       wall_s[:, k, 960:1024], start=(k == 0), stop=(k == 1))
                    mm.then_inc(d_ready, 1)
                    if j == TT - 1:
                        pe.drain().then_inc(xt_used, 1)

                def moment(j):
                    pe.wait_ge(outer_done, 2 * u.s + (j + 1))
                    for f in range(2):
                        o, cols = d_free("m", j, f)[:, 0:288], slice(f * 288, (f + 1) * 288)
                        for i in range(j):
                            pe.matmul(o, ones[:, :], oo[:, i, cols], start=(i == 0), stop=False)
                        pe.matmul(o, tri, oo[:, j, cols], start=(j == 0), stop=True).then_inc(d_ready, 1)

                def turn_heads(w):
                    if w == 0:
                        if u.x is None:
                            pe.wait_ge(prepared, 5)
                        pe.wait_ge(split_ready, u.s + 1)
                    if w == 2:
                        pe.wait_ge(lines_ready, 2 * u.s + 2)
                    for n, unit in enumerate(turned(w)):
                        o = (a_free if n % 2 == 0 else d_free)(*unit)[:, :].bitcast(BF16)
                        j, f = (n // 2, n % 2) if w < 2 else (n, 0)
                        for g in range(8):
                            if w < 2:
                                mm = pe.transpose(o[0:PARTS * DH, g * P:(g + 1) * P],
                                                  qks[:, w, j * H + 8 * f + g, :], ident_b[:, :])
                            else:
                                mm = pe.transpose(o[:, g * P:(g + 1) * P],
                                                  lqk[:, w - 2, j * H + 2 * g:j * H + 2 * g + 2, :].rearrange(
                                                      "p a c -> p (a c)"), ident_b[:, :])
                        mm.then_inc(a_ready if n % 2 == 0 else d_ready, 1)
                    if w == 1:
                        pe.drain().then_inc(heads_turned, 1)

                def scores(h):
                    if h == 0:
                        act_took(*turned(3)[0])
                        vec_took(*turned(3)[1])
                    o = d_free("x", h)
                    rows = slice(0, PARTS * DH)
                    for j in range(TT):
                        cols = slice(0, P) if j == 0 else slice(P, 3 * P)
                        pe.matmul(o[:, cols], st_q[rows, h, j * P:(j + 1) * P], st_k[rows, h, 0:(j + 1) * P],
                                  start=True, stop=False)
                        mm = pe.matmul(o[:, 2 * j * P:(2 * j + 1) * P], ident_b[:, :], mask_s[:, h, :],
                                       start=False, stop=True)
                    mm.then_inc(d_ready, 1)
                    o = a_free("y", h)
                    rows = slice(64 * (h % 2), 64 * (h % 2) + PARTS * 6)
                    for j in range(TT):
                        cols = slice(0, P) if j == 0 else slice(P, 3 * P)
                        mm = pe.matmul(o[:, cols], lqt[rows, h // 2, j * P:(j + 1) * P],
                                       lkt[rows, h // 2, 0:(j + 1) * P], start=True, stop=True)
                    mm.then_inc(a_ready, 1)

                def turn(h):
                    pe.wait_ge(probs_ready, u.s16 + (h + 1))
                    o = d_free("pt", h) if h % 2 else a_free("pt", h)
                    for c in range(3):
                        mm = pe.transpose(o[:, c * P:(c + 1) * P], pr[:, h % RING, c * P:(c + 1) * P], ident)
                    mm.then_inc(d_ready if h % 2 else a_ready, 1)

                def values(h):
                    (vec_took if h % 2 else act_took)("pt", h)
                    if h % 8 == 0:
                        o_free("o", h // 8)
                    rows = slice(h % 8 // 2 * 32, h % 8 // 2 * 32 + 32)
                    o = o_bank("o", h // 8)
                    pe.matmul(o[rows, 0:T], v[:, 0, h, :], pt[:, h % RING, 0:T], start=(h % 2 == 0), stop=False)
                    mm = pe.matmul(o[rows, P:T], v[:, 1, h, :], pt[:, h % RING, T:T + P],
                                   start=False, stop=(h % 2 == 1))
                    if h % 8 == 7:
                        mm.then_inc(o_ready, 1)

                def turn_out():
                    pe.wait_ge(sums_ready, u.s + 1)
                    o = a_free("ot")
                    for j in range(TT):
                        for f in range(2):
                            mm = pe.transpose(o[:, f * T + j * P:f * T + (j + 1) * P],
                                              rib[:, j, f * P:(f + 1) * P], ident)
                    mm.then_inc(a_ready, 1)

                def out():
                    divided("o", 1)
                    o = d_free("out")
                    for j in range(TT):
                        for k in range(2):
                            mm = pe.matmul(o[:, j * D:(j + 1) * D], oht[:, k, j * P:(j + 1) * P],
                                           wout_s[:, k, :], start=(k == 0), stop=(k == 1))
                    mm.then_inc(d_ready, 1)

                def keys(n):
                    if n == 0:
                        pe.wait_ge(ctx_loaded, 16 * u.s + 16)
                    o = a_free("k", n)
                    for c in range(2):
                        for k in range(2):
                            mm = pe.matmul(o[:, c * T:(c + 1) * T],
                                           wkv_s[:, k, (2 * n + c) * P:(2 * n + c + 1) * P], ct[:, k, :],
                                           start=(k == 0), stop=(k == 1))
                    mm.then_inc(a_ready, 1)

                def vals(n):
                    cols = slice(XH * XD + n % 2 * 512, XH * XD + (n % 2 + 1) * 512)
                    o = a_free("v", n)
                    for k in range(2):
                        mm = pe.matmul(o[:, :], ct[:, k, n // 2 * P:(n // 2 + 1) * P], wkv_s[:, k, cols],
                                       start=(k == 0), stop=(k == 1))
                    mm.then_inc(a_ready, 1)
                    if n == 3:
                        pe.drain().then_inc(ctx_used, 1)

                def queries():
                    pe.wait_ge(x1_ready, 2 * u.s + 2)
                    o = d_free("x1t")
                    for j in range(TT):
                        for k in range(2):
                            mm = pe.transpose(o[:, k * T + j * P:k * T + (j + 1) * P],
                                              x1[:, j, k * P:(k + 1) * P], ident)
                    mm.then_inc(d_ready, 1)
                    vec_took("x1t")
                    for n in range(4):
                        o = a_free("q", n)
                        for c in range(2):
                            for k in range(2):
                                mm = pe.matmul(o[:, c * T:(c + 1) * T],
                                               wq_s[:, k, (2 * n + c) * P:(2 * n + c + 1) * P], x1t[:, k, :],
                                               start=(k == 0), stop=(k == 1))
                        mm.then_inc(a_ready, 1)

                def scores2(h):
                    if h == 0:
                        pe.wait_ge(queries_ready, u.x + 1)
                    r, c = XD * (h % 2), h // 2
                    o = a_free("s", h)
                    for j in range(TT):
                        mm = pe.matmul(o[:, j * T:(j + 1) * T], qt[r:r + XD, c, j * P:(j + 1) * P],
                                       kt2[r:r + XD, c, :], start=True, stop=True)
                    mm.then_inc(a_ready, 1)

                def keep_warm(n):
                    o = d_free("out2")
                    for _ in range(n):
                        pe.matmul(o[:, :], ident, wall_s[:, 0, 0:512], start=True, stop=True)

                def turn2(h):
                    act_took("s", h)
                    o = a_free("pt2", h)
                    for j in range(TT):
                        for i in range(TT):
                            mm = pe.transpose(o[:, i * T + j * P:i * T + (j + 1) * P],
                                              pr[:, h % RING, j * T + i * P:j * T + (i + 1) * P], ident)
                    mm.then_inc(a_ready, 1)

                def values2(h):
                    act_took("pt2", h)
                    if h % 4 == 0:
                        o_free("o2", h // 4)
                    for j in range(TT):
                        o = o_bank("o2", h // 4)[:, j * T + (h % 4) * XD:j * T + (h % 4 + 1) * XD]
                        for i in range(TT):
                            mm = pe.matmul(o, pt[:, h % RING, i * T + j * P:i * T + (j + 1) * P],
                                           v2[:, i, h * XD:(h + 1) * XD], start=(i == 0), stop=(i == 1))
                    if h % 4 == 3:
                        mm.then_inc(o_ready, 1)

                def turn_out2():
                    for n in range(4):
                        divided("o2", n)
                        o = a_free("o2t", n)
                        for c in range(2):
                            for j in range(TT):
                                mm = pe.transpose(o[:, c * T + j * P:c * T + (j + 1) * P],
                                                  o2[:, j, (2 * n + c) * P:(2 * n + c + 1) * P], ident)
                        mm.then_inc(a_ready, 1)

                def out2():
                    o = d_free("out2")
                    act_took("o2t", 3)
                    for j in range(TT):
                        for k in range(8):
                            mm = pe.matmul(o[:, j * D:(j + 1) * D], o2t[:, k, j * P:(j + 1) * P],
                                           wo_s[:, k, :], start=(k == 0), stop=(k == 7))
                    mm.then_inc(d_ready, 1)

                def turn_x2():
                    pe.wait_ge(x2_ready, 2 * u.x + 2)
                    o = d_free("x2t")
                    for j in range(TT):
                        for k in range(2):
                            mm = pe.transpose(o[:, k * T + j * P:k * T + (j + 1) * P],
                                              x2[:, j, k * P:(k + 1) * P], ident)
                    mm.then_inc(d_ready, 1)

                def gate_logits():
                    o = d_free("lg")
                    vec_took("x2t")
                    for j in range(TT):
                        for k in range(2):
                            mm = pe.matmul(o[:, j * E:(j + 1) * E], x2t[:, k, j * P:(j + 1) * P],
                                           gate_s[:, k, :], start=(k == 0), stop=(k == 1))
                    mm.then_inc(d_ready, 1)

                def shared_up():
                    vec_took("x2t")
                    for c in range(2):
                        o = a_free("sg", c)
                        for k in range(2):
                            mm = pe.matmul(o[:, 0:T], shgu_s[:, k, c * I:(c + 1) * I], x2t[:, k, :],
                                           start=(k == 0), stop=(k == 1))
                        mm.then_inc(a_ready, 1)

                def shared_down():
                    pe.wait_ge(sgh_ready, u.x + 1)
                    o = d_free("sh")
                    for j in range(TT):
                        mm = pe.matmul(o[:, j * D:(j + 1) * D], sgh[:, j * P:(j + 1) * P], shdn_s[:, :],
                                       start=True, stop=True)
                    mm.then_inc(d_ready, 1)

                def places():
                    pe.wait_ge(chosen_ready, u.x + 1)
                    bk = d_free("pos")
                    for j in range(TT):
                        o = bk[:, j * E:(j + 1) * E]
                        pe.matmul(o, ones_b[:, :], before[:, :], start=True, stop=False)
                        for i in range(j):
                            pe.matmul(o, ones_b[:, :], chosen[:, i, :], start=False, stop=False)
                        mm = pe.matmul(o, before_b[:, :], chosen[:, j, :], start=False, stop=True)
                    mm.then_inc(d_ready, 1)

                for name, n in u.steps:
                    if name == "proj":
                        proj(n)
                    elif name == "moment":
                        moment(n)
                    elif name == "turn_heads":
                        turn_heads(n)
                    elif name == "self":
                        if n < H:
                            scores(n)
                        if 0 <= n - 3 < H:
                            turn(n - 3)
                        if 0 <= n - 5 < H:
                            values(n - 5)
                    elif name == "turn_out":
                        turn_out()
                    elif name == "out":
                        out()
                    elif name == "keys":
                        if n == 0 and u.x is None:
                            pe.wait_ge(loaded2, 16 * 7)
                            pe.wait_ge(prepared2, 1)
                        keys(n)
                    elif name == "vals":
                        vals(n)
                    elif name == "queries":
                        queries()
                    elif name == "cross":
                        if n < XH:
                            scores2(n)
                        if u.s is None and n < len(WARM):
                            keep_warm(WARM[n])
                        if 0 <= n - 2 < XH:
                            turn2(n - 2)
                        if 0 <= n - 3 < XH:
                            values2(n - 3)
                    elif name == "turn_out2":
                        turn_out2()
                    elif name == "out2":
                        out2()
                    elif name == "x2t":
                        turn_x2()
                    elif name == "shared":
                        (shared_down if n else shared_up)()
                    elif name == "gate":
                        gate_logits()
                    elif name == "place" and n == 0:
                        places()
                for units, ready_sem in ((u.dn, d_ready), (u.an, a_ready)):
                    pads = len([k for k in units if k[0] == "pad"])
                    if pads:
                        pe.drain().then_inc(ready_sem, pads)

            for u in passes(pe):
                part_a(u)

            pe.wait_ge(d_done, all_d + RD)
            pe.wait_ge(a_done, all_a + RA)
            pe.wait_ge(o_done, all_o + RO)

            def turn_slots(e, s, i48):
                pe.wait_ge(ex_loaded[s % NE], i48 + 48)
                pe.wait_ge(xet_done, e + 1)
                for k in range(2):
                    for c in range(2):
                        mm = pe.transpose(bank[s % 2][:, k * CAP + c * P:k * CAP + (c + 1) * P],
                                          xe[s % NE][:, c, k * P:(k + 1) * P], ident)
                mm.then_inc(xet_ready, 1)

            def gate_up(e, s):
                pe.wait_ge(xet_done, e + 3)
                pe.wait_ge(he_ready, e + 1)
                for c in range(2):
                    for k in range(2):
                        mm = pe.matmul(bank[2 + s % 2][:, c * CAP:(c + 1) * CAP],
                                       we[:, s % NE, k, c * I:(c + 1) * I], xet[:, s % 4, k, :],
                                       start=(k == 0), stop=(k == 1))
                mm.then_inc(gu_ready, 1)

            def down(e, s):
                pe.wait_ge(he_ready, e + 3)
                pe.wait_ge(ye_done, e + 1)
                for c in range(2):
                    mm = pe.matmul(bank[4 + s % 2][:, c * D:(c + 1) * D], he[:, s % 4, c * P:(c + 1) * P],
                                   wd[:, s % NE, :], start=True, stop=True)
                mm.then_inc(ye_ready, 1)

            turn_slots(0, 0, 0)
            turn_slots(1, 1, 0)
            gate_up(0, 0)

            def experts(i):
                first = isinstance(i, int)
                e0, i48 = (0, 0) if first else (pe.snap(NE * i), pe.snap(48 * i))
                for s in range(NE):
                    turn_slots(e0 + (s + 2), s + 2, i48 + (48 if s >= NE - 2 else 0))
                    gate_up(e0 + (s + 1), s + 1)
                    down(e0 + s, s)
                    if first and s == OWN_AT:
                        pe.wait_ge(own_loaded, 16)
                        pe.transpose(bank[7][:, 0:NS], own_s[:, :], ident[0:NS, 0:NS]).then_inc(own_turned, 1)

            experts(0)
            with pe.Fori(1, E // NE - 1) as i:
                experts(i)
            for s in range(NE):
                if s < NE - 2:
                    turn_slots(E - NE + s + 2, s + 2, 48 * (E // NE - 1))
                if s < NE - 1:
                    gate_up(E - NE + s + 1, s + 1)
                down(E - NE + s, s)

        @block.scalar
        def _(act):
            act.wait_ge(loaded, 16 * 3)
            for r in range(RA):
                nc.scalar.copy(turn_a[:, r:r + 1], ident[:, 0:1]).then_inc(a_done, 1)

            def part_a(u):
                def ready(*n):
                    act.wait_ge(a_ready, u.a + (u.an[n] + 1))
                    return bank[u.a_bank(*n)]

                def exps(h):
                    act.wait_ge(d_done, u.d + (u.dn["x", h] + 1 + RD))
                    for j in range(TT):
                        cols = slice(0, P) if j == 0 else slice(P, 3 * P)
                        ins = nc.scalar.activation(pr[:, h % RING, cols], nl[:, h % RING, cols], ACT.Exp,
                                                   bias=nm[:, h % RING, j:j + 1], scale=-1.0,
                                                   accum_out=rs[:, j, h:h + 1])
                    ins.then_inc(probs_ready, 1)

                def exps2(h):
                    o = bank[u.a_bank("s", h)]
                    act.wait_ge(rowmax_ready, u.x16 + (h + 1))
                    for j in range(TT):
                        ins = nc.scalar.activation(pr[:, h % RING, j * T:(j + 1) * T], o[:, j * T:(j + 1) * T],
                                                   ACT.Exp, bias=nm2[:, h % RING, j:j + 1], scale=1.0,
                                                   accum_out=rs2[:, j, h:h + 1])
                    ins.then_inc(a_done, 1)

                for name, n in u.steps:
                    if name == "turn_heads":
                        for m, unit in enumerate(turned(n)):
                            if m % 2 == 0:
                                dst, src = turned_to(n, m, ready(*unit))
                                nc.scalar.copy(dst, src).then_inc(a_done, 1)
                    elif name == "self":
                        for h in {H: [H - 2, H - 1], H + 1: []}.get(n, [n - 2]):
                            if 0 <= h < H:
                                exps(h)
                        if 0 <= n - 4 < H and n % 2 == 0:
                            nc.scalar.copy(pt[:, n % RING, 0:384], ready("pt", n - 4)[:, 0:384]
                                           ).then_inc(a_done, 1)
                        if n < H:
                            nc.scalar.activation(ab[:, n % RING, :], ready("y", n)[:, 0:384], ACT.Abs
                                                 ).then_inc(a_done, 1)
                    elif name == "turn_out":
                        nc.scalar.copy(rit[:, :, :, :].rearrange("p f j t -> p (f j t)"), ready("ot")[:, :]
                                       ).then_inc(a_done, 1)
                    elif name == "keys":
                        nc.scalar.copy(kt2[:, 2 * n:2 * n + 2, :].rearrange("p c t -> p (c t)"),
                                       ready("k", n)[:, :]).then_inc(a_done, 1)
                    elif name == "vals":
                        nc.scalar.copy(v2[:, n // 2, n % 2 * 512:(n % 2 + 1) * 512], ready("v", n)[:, :]
                                       ).then_inc(a_done, 1)
                    elif name == "queries":
                        for c in range(4):
                            nc.scalar.copy(qt[:, 2 * c:2 * c + 2, :].rearrange("p c t -> p (c t)"),
                                           ready("q", c)[:, :]).then_inc(a_done, 1)
                        for p in range(len([k for k in u.an if k[0] == "pad"])):
                            nc.scalar.copy(turn_a[:, p:p + 1], ident[:, 0:1]).then_inc(a_done, 1)
                        act.drain().then_inc(queries_ready, 1)
                    elif name == "cross":
                        if 0 <= n - 3 < XH:
                            nc.scalar.copy(pt[:, (n - 3) % RING, :], ready("pt2", n - 3)[:, :]
                                           ).then_inc(a_done, 1)
                        if n < XH:
                            exps2(n)
                    elif name == "turn_out2":
                        for c in range(4):
                            nc.scalar.copy(o2t[:, 2 * c:2 * c + 2, :].rearrange("p c t -> p (c t)"),
                                           ready("o2t", c)[:, :]).then_inc(a_done, 1)
                    elif name == "shared" and n == 0:
                        o = ready("sg", 0)
                        nc.scalar.activation(sge[:, :], o[:, 0:T], ACT.Exp, scale=-1.0)
                        nc.scalar.copy(sgg[:, :], o[:, 0:T]).then_inc(a_done, 1)
                        nc.scalar.copy(sgu[:, :], ready("sg", 1)[:, 0:T]).then_inc(a_done, 1)
                    elif name == "choose" and n:
                        act.wait_ge(top_ready, u.x + 1)
                        for j in range(TT):
                            ins = nc.scalar.activation(ew[:, j, :], m8[:, j, 0:K], ACT.Exp, bias=nmx[:, j:j + 1],
                                                       scale=1.0, accum_out=ws[:, j:j + 1])
                        ins.then_inc(ew_ready, 1)
                if u.s is None:
                    for p in range(len([k for k in u.an if k[0] == "pad"])):
                        nc.scalar.copy(turn_a[:, p:p + 1], ident[:, 0:1]).then_inc(a_done, 1)

            for u in passes(act):
                part_a(u)

            act.sem_inc(ye_done, 2)

            def experts(i):
                first = isinstance(i, int)
                e0, i64 = (0, 0) if first else (act.snap(NE * i), act.snap(32 * NE // 4 * i))

                def silu(s):
                    act.wait_ge(gu_ready, e0 + (s + 1))
                    nc.scalar.activation(sl[:, s % 4, :], bank[2 + s % 2][:, 0:CAP], ACT.Silu).then_inc(sl_ready, 1)

                def rows_out(s):
                    if not (first and s < 4):
                        act.wait_ge(ye_stored[s % 4], i64 + 32 * (s // 4))
                    act.wait_ge(ye_ready, e0 + (s + 1))
                    nc.scalar.copy(ye[:, s % 4, :, :].rearrange("p c n -> p (c n)"), bank[4 + s % 2][:, :]
                                   ).then_inc(ye_done, 1)

                for s in range(NE + 1):
                    if s < NE:
                        silu(s)
                    if s >= 1:
                        rows_out(s - 1)

            experts(0)
            with act.Fori(1, E // NE) as i:
                experts(i)

            for s in range(4):
                act.wait_ge(ye_stored[s], 32 * E // 4)
            for t in range(N // P):
                r, s = t // NC - 2, t % NC
                if r >= 0:
                    act.wait_ge(fin_step, COMBINE_STEPS * r + NC * (K - 1) + s + 1)
                act.dma_start(gr[t % (2 * NC)], by_token[SLOTS + t * P * K:SLOTS + (t + 1) * P * K, :].rearrange(
                    "(p k) n -> p k n", k=K)).then_inc(gathered[t % (2 * NC)], 16)

        @block.gpsimd
        def _(pool):
            pool.sem_inc(x2_free, 1)
            pool.memset(powers[:, :], -0.5).then_inc(pooled, 1)
            pool.wait_ge(pooled, 1)

            def part_a(u):
                base, count = None if u.s is None else (
                    0 if u.x is None else pool.snap(u.s * SPLIT_STEPS - SPLIT_STEPS // 2)), [0]

                def split_next(ins):
                    count[0] += 1
                    ins.then_inc(split_step, 1)
                    pool.wait_ge(split_step, base + count[0])

                for name, n in u.steps:
                    if name == "split" and n == 0:
                        pool.wait_ge(lines_asked, u.s + 1)
                        pool.tensor_tensor(rn[:, :], ss[:, :], powers[:, :], ALU.pow).then_inc(lines_done, 1)
                        if u.x is None:
                            continue
                        pool.wait_ge(raw_ready, u.s + 1)
                        pool.tensor_tensor(turn_p[:, 2:3], powers[:, 0:1], powers[:, 0:1], ALU.mult
                                           ).then_inc(split_step, 1)
                        count[0] += 1
                        pool.wait_ge(split_step, base + count[0])
                        split(heads, pool.tensor_tensor, split_next
                              ).then_inc(split_ready, 1)
                    elif name == "split" and n == 1:
                        pool.wait_ge(outer_done, 2 * u.s + 2)
                        pool.tensor_tensor(turn_p[:, 5:6], powers[:, 0:1], powers[:, 0:1], ALU.mult
                                           ).then_inc(split_step, 1)
                        count[0] += 1
                        pool.wait_ge(split_step, base + count[0])
                        split([(lraw[:, 1, :, :], line_parts(1), 1)], pool.tensor_tensor, split_next
                              ).then_inc(lines_ready, 1)
                    elif name == "out":
                        pool.wait_ge(var1_asked, u.s + 1)
                        pool.tensor_tensor(rv[:, 0, :, 0], va[:, 0, :, 0], powers[:, 0:TT], ALU.pow
                                           ).then_inc(var1_done, 1)
                    elif name == "norm2" and n:
                        pool.wait_ge(var2_asked, u.x + 1)
                        pool.tensor_tensor(rv[:, 1, :, 0], va[:, 1, :, 0], powers[:, 0:TT], ALU.pow
                                           ).then_inc(var2_done, 1)
                    elif name == "place" and n == 1:
                        pool.wait_ge(zeroed, ZEROED)
                        pool.wait_ge(slots_known, u.x + 1)
                        pool.tensor_tensor(turn_p[:, 0:1], powers[:, 0:1], powers[:, 0:1], ALU.mult)
                        for j in range(TT):
                            for k in range(K):
                                c = j * K + k
                                pool.indirect_dma_start(
                                    out=slots[:, :],
                                    out_offset=bass.IndirectOffsetOnAxis(ap=slot_i[:, c:c + 1], axis=0),
                                    in_=x2[:, j, :], in_offset=None).then_inc(scattered, 16)
                        for c in range(TT * K):
                            pool.indirect_dma_start(
                                out=owners[:, :],
                                out_offset=bass.IndirectOffsetOnAxis(ap=slot_i[:, c:c + 1], axis=0),
                                in_=ids[:, c:c + 1], in_offset=None).then_inc(owned, 16)
                        pool.wait_ge(scattered, 16 * TT * K * u.x + 16 * TT * K)
                        pool.wait_ge(owned, 16 * TT * K * u.x + 16 * TT * K)
                        pool.tensor_tensor(turn_p[:, 3:4], powers[:, 0:1], powers[:, 0:1], ALU.mult
                                           ).then_inc(x2_free, 1)

            for u in passes(pool):
                part_a(u)
            pool.wait_ge(own_ready, 1)

            def experts(i):
                first = isinstance(i, int)
                e0, i64 = (0, 0) if first else (pool.snap(NE * i), pool.snap(32 * NE // 4 * i))
                if not first:
                    for s in range(4):
                        pool.wait_ge(ye_stored[s], i64)
                pool.tensor_tensor(turn_p[:, 6:7], powers[:, 0:1], powers[:, 0:1], ALU.mult)
                tiles = slice(0, 2 * NE) if first else bass.ds(i * 2 * NE, 2 * NE)
                pool.tensor_copy(own_now[:, :], own_i[:, tiles]).then_inc(own_step, 1)
                pool.wait_ge(own_step, i + 1)
                for s in range(NE):
                    pool.wait_ge(ye_done, e0 + (s + 3))
                    pool.tensor_tensor(turn_p[:, 7 + s:8 + s], powers[:, 0:1], powers[:, 0:1], ALU.mult)
                    for c in range(2):
                        pool.indirect_dma_start(
                            out=by_token[:, :],
                            out_offset=bass.IndirectOffsetOnAxis(ap=own_now[:, 2 * s + c:2 * s + c + 1], axis=0),
                            in_=ye[:, s % 4, c, :], in_offset=None).then_inc(ye_stored[s % 4], 16)

            experts(0)
            with pool.Fori(1, E // NE) as i:
                experts(i)

            for r in range(ROUNDS):
                pool.wait_ge(var_ready, r + 1)
                tiles = slice(NC * r, NC * (r + 1))
                pool.tensor_tensor(rv3[:, tiles], va3[:, tiles], powers[:, 0:NC], ALU.pow).then_inc(rstd_ready, 1)

        @block.vector
        def _(dve):
            def tt(o, a, c, op):
                return nc.vector.tensor_tensor(o, a, c, op)

            nc.vector.memset(zero[:, :], 0.0).then_inc(prepared, 1)
            nc.vector.memset(lqk[:, :, :, :], 0.0)
            nc.vector.memset(v[:, :, :, :], 0.0)
            nc.vector.memset(nm[:, :, :], 0.0)
            nc.vector.memset(before[:, :], 0.0)
            nc.vector.memset(xp[:, :, 0:1], 0.0)
            nc.vector.memset(ones_b[:, :], 1.0)
            nc.vector.memset(ones[:, :], 1.0).then_inc(setup, 1)
            dve.wait_ge(loaded, 16 * 3)
            dve.wait_ge(setup, 1)
            nc.vector.tensor_scalar(sgn[:, :], bscale, 0.0, 2.0, ALU.is_ge, ALU.mult).then_inc(setup, 1)
            dve.wait_ge(setup, 2)
            nc.vector.tensor_scalar(sgn[:, :], sgn[:, :], -1.0, None, ALU.add).then_inc(setup, 1)
            dve.wait_ge(setup, 3)
            sg3 = sgn[:, :].unsqueeze(2).to_broadcast([P, H, DH])
            for w in (bqkv[:, 0:D], wall_s[:, 0, 0:D], wall_s[:, 1, 0:D]):
                w3 = w.rearrange("p (h d) -> p h d", d=DH)
                nc.vector.scalar_tensor_tensor(out=w3, in0=w3, scalar=float(DH) ** -0.5, in1=sg3,
                                               op0=ALU.mult, op1=ALU.mult).then_inc(prepared, 1)
            for r in range(RD):
                nc.vector.memset(scratch[:, 3 + r:4 + r], 0.0).then_inc(d_done, 1)
            for r in range(RO):
                nc.vector.memset(scratch[:, 6 + r:7 + r], 0.0).then_inc(o_done, 1)
            for h in range(H):
                nc.vector.tensor_scalar(mask_s[:, h, :], mask, sgn[:, h:h + 1], None, ALU.mult)
            nc.vector.tensor_scalar(nsgn[:, :], sgn[:, :], -1.0, None, ALU.mult)
            tt(absb[:, :], bscale, sgn[:, :], ALU.mult)
            nc.vector.tensor_copy(ident_b[:, :], ident)
            tt(before_b[:, :], tri, ident, ALU.subtract)
            nc.vector.tensor_copy(spare[:, :], spare0).then_inc(prepared, 1)
            dve.wait_ge(prepared, 5)

            def part_a(u):
                count = {"s": 0, "x": 0}
                s_base = None if u.s is None else (0 if u.x is None else dve.snap(u.s * S_STEPS + FIRST_STEPS))
                x_base = None if u.x is None else (u.x * X_STEPS if isinstance(u.x, int) else dve.snap(u.x * X_STEPS))

                def s_next(ins, carry=False):
                    count["s"] += 1
                    ins.then_inc(s_step, 1)
                    dve.wait_ge(s_step, s_base + count["s"])
                    if carry:
                        nc.vector.memset(scratch[:, 11:12], 0.0)

                def x_next(ins, carry=False):
                    count["x"] += 1
                    ins.then_inc(x_step, 1)
                    dve.wait_ge(x_step, x_base + count["x"])
                    if carry:
                        nc.vector.memset(scratch[:, 12:13], 0.0)

                def ready(*n):
                    dve.wait_ge(d_ready, u.d + (u.dn[n] + 1))
                    return bank[u.d_bank(*n)]

                def took(*n):
                    dve.wait_ge(d_done, u.d + (u.dn[n] + 1 + RD))

                half = TT * H

                def proj(j):
                    hs = slice(j * H, (j + 1) * H)
                    g1 = ready("g1", j)
                    tt(raw[:, :, hs, :], g1[:, :].rearrange("p (w h d) -> p w h d", w=2, d=DH),
                       bqkv[:, 0:2 * D].rearrange("p (w h d) -> p w h d", w=2, d=DH), ALU.add).then_inc(d_done, 1)
                    g2 = ready("g2", j)
                    for b in range(2):
                        def of(w):
                            return w.rearrange("p (a b d) -> p a b d", b=2, d=DH)[:, :, b, :]
                        tt(v[:, j, :, b * DH:(b + 1) * DH].rearrange("p (a b) d -> p a b d", b=2)[:, :, b, :],
                           of(g2[:, 0:D]), of(bqkv[:, 2 * D:3 * D]), ALU.add)
                    nc.vector.tensor_copy(lw[:, :, j * 64:(j + 1) * 64],
                                          g2[:, D:2 * D].rearrange("p (c n) -> p c n", c=4)).then_inc(d_done, 1)

                def points(c):
                    return lw[:, c, :].rearrange("p (h i) -> p h i", i=4)

                def lines0():
                    wide = [P, half, 4, 4]
                    took("g2", TT - 1)
                    nc.vector.memset(scratch[:, 15:16], 0.0).then_inc(raw_ready, 1)
                    for w, (p1, p2) in enumerate(((3, 0), (1, 2))):
                        ins = tt(pp[:, w, :, :, :], points(p1).unsqueeze(3).to_broadcast(wide),
                                 points(p2).unsqueeze(2).to_broadcast(wide), ALU.mult)
                    s_next(ins)

                def lines1():
                    for c, (i, k) in enumerate(((2, 3), (3, 1), (1, 2), (0, 3), (2, 0), (0, 1))):
                        tt(ll[:, 0, :, c:c + 1], pp[:, 0, :, i, k:k + 1], pp[:, 0, :, k, i:i + 1], ALU.subtract)
                    for c, i, n in ((0, 0, 3), (3, 1, 2), (5, 2, 1)):
                        ins = tt(ll[:, 1, :, c:c + n], pp[:, 1, :, i, i + 1:i + 1 + n],
                                 pp[:, 1, :, i + 1:i + 1 + n, i], ALU.subtract)
                    s_next(ins)

                def lines2():
                    lf = ll[:, :, :, :].rearrange("p w h c -> p (w h) c")
                    s_next(tt(sq[:, :, :], lf, lf, ALU.mult))
                    s_next(nc.vector.tensor_reduce(ss[:, :], sq[:, :, :], X, ALU.add))
                    nc.vector.tensor_scalar(ss[:, :], ss[:, :], 1e-24, None, ALU.max).then_inc(lines_asked, 1)

                def outer0():
                    dve.wait_ge(lines_done, u.s + 1)
                    tt(rd[:, :, :], ll[:, 1, :, :],
                       rn[:, half:2 * half].unsqueeze(2).to_broadcast([P, half, 6]), ALU.mult)
                    s_next(tt(lraw[:, 1, :, :], ll[:, 0, :, :],
                              rn[:, 0:half].unsqueeze(2).to_broadcast([P, half, 6]), ALU.mult))

                def outer1():
                    for j in range(TT):
                        jw = lraw[:, 1, j * H:(j + 1) * H, :]
                        tt(oo[:, j, :].rearrange("p (h a c) -> p h a c", a=6, c=6),
                           jw.unsqueeze(3).to_broadcast([P, H, 6, 6]), jw.unsqueeze(2).to_broadcast([P, H, 6, 6]),
                           ALU.mult).then_inc(outer_done, 1)

                def moment(j):
                    for f in range(2):
                        h0 = j * H + f * 8
                        tt(mr[:, 2 * j + f, :, :].rearrange("p (h a) c -> p h a c", a=6),
                           ready("m", j, f)[:, 0:288].rearrange("p (h a c) -> p h a c", a=6, c=6),
                           rd[:, h0:h0 + 8, :].unsqueeze(2).to_broadcast([P, 8, 6, 6]), ALU.mult
                           ).then_inc(d_done, 1)
                    took("m", j, 1)
                    hs = slice(j * H, (j + 1) * H)
                    s_next(nc.vector.tensor_reduce(
                        rm[:, hs, :].rearrange("p h c -> p (h c)"),
                        mr[:, 2 * j:2 * j + 2, :, :].rearrange("p a n c -> p (a n) c"), X, ALU.add))
                    s_next(tt(lraw[:, 0, hs, :], rm[:, hs, :], absb[:, :].unsqueeze(2).to_broadcast([P, H, 6]),
                              ALU.mult))

                def logits(h):
                    o = ready("x", h)
                    dve.wait_ge(a_done, u.a + (u.an["y", h] + 1 + RA))
                    nc.vector.memset(scratch[:, 32 + h:33 + h], 0.0)
                    for j in range(TT):
                        cols = slice(0, P) if j == 0 else slice(P, 3 * P)
                        ins = nc.vector.tensor_tensor_reduce(
                            out=nl[:, h % RING, cols], in0=ab[:, h % RING, cols], in1=o[:, cols],
                            scale=nsgn[:, h:h + 1], scalar=3e38, op0=ALU.add, op1=ALU.min,
                            accum_out=nm[:, h % RING, j:j + 1])
                    ins.then_inc(d_done, 1)

                def sums():
                    dve.wait_ge(probs_ready, u.s16 + H)
                    nc.vector.memset(scratch[:, 16:17], 0.0)
                    s_next(nc.vector.reciprocal(ri[:, :, :], rs[:, :, :]))
                    nc.vector.tensor_copy(rib[:, :, :].rearrange("p j (h d) -> p (j h) d", d=DH),
                                          ri[:, :, :].rearrange("p j h -> p (j h)").unsqueeze(2).to_broadcast(
                                              [P, TT * H, DH])).then_inc(sums_ready, 1)

                def outputs():
                    dve.wait_ge(a_done, u.a + (u.an["ot",] + 1 + RA))
                    nc.vector.memset(scratch[:, 17:18], 0.0)
                    for f in range(2):
                        dve.wait_ge(o_ready, u.o + (u.on["o", f] + 1))
                        tt(oht[:, f, :], bank[u.o_bank("o", f)][:, 0:T], rit[:, f, :, :].rearrange(
                            "p j t -> p (j t)"), ALU.mult).then_inc(o_done, 1)

                flat = "p j n -> p (j n)"

                def moments(w, src, nxt, asked):
                    for j in range(TT):
                        ins = nc.vector.bn_stats(st[:, w, j, :], src[:, j, :])
                    nxt(ins, carry=True)
                    for j in range(TT):
                        ins = nc.vector.bn_aggr(mv[:, w, j, :], st[:, w, j, :])
                    nxt(ins)
                    nc.vector.tensor_scalar(va[:, w, :, 0], mv[:, w, :, 1], EPS, None, ALU.add).then_inc(asked, 1)

                def apply(w, src, dst, done, at, ready_sem):
                    dve.wait_ge(done, at + 1)
                    for j in range(TT):
                        nc.vector.tensor_scalar(dst[:, j, :], src[:, j, :], mv[:, w, j, 0:1], rv[:, w, j, :],
                                                ALU.subtract, ALU.mult).then_inc(ready_sem, 1)

                def out():
                    dve.wait_ge(xr_loaded, 16 * u.s + 16)
                    s_next(tt(xr[:, :, :], xr[:, :, :], bout.unsqueeze(1).to_broadcast([P, TT, D]), ALU.add))
                    o = ready("out")
                    tt(y1[:, :, :].rearrange(flat), o[:, :], xr[:, :, :].rearrange(flat), ALU.add
                       ).then_inc(d_done, 1)
                    took("out")
                    moments(0, y1, s_next, var1_asked)

                def queries():
                    nc.vector.tensor_copy(x1t[:, :, :].rearrange("p k t -> p (k t)"), ready("x1t")[:, :]
                                          ).then_inc(d_done, 1)

                def rowmax(h):
                    dve.wait_ge(a_ready, u.a + (u.an["s", h] + 1))
                    nc.vector.tensor_reduce(nm2[:, h % RING, :], bank[u.a_bank("s", h)][:, :].rearrange(
                        "p (j t) -> p j t", j=TT), X, ALU.max, negate=True).then_inc(rowmax_ready, 1)

                def outputs2(n):
                    hs = slice(4 * n, 4 * n + 4)
                    dve.wait_ge(o_ready, u.o + (u.on["o2", n] + 1))
                    x_next(nc.vector.reciprocal(ri2[:, :, hs], rs2[:, :, hs]))
                    tt(o2[:, :, n * T:(n + 1) * T].rearrange("p j (h d) -> p j h d", d=XD),
                       bank[u.o_bank("o2", n)][:, :].rearrange("p (j h d) -> p j h d", j=TT, d=XD),
                       ri2[:, :, hs].unsqueeze(3).to_broadcast([P, TT, 4, XD]), ALU.mult).then_inc(o_done, 1)

                def out2():
                    x_next(tt(x1[:, :, :], x1[:, :, :], bo.unsqueeze(1).to_broadcast([P, TT, D]), ALU.add))
                    tt(y2[:, :, :].rearrange(flat), ready("out2")[:, :], x1[:, :, :].rearrange(flat), ALU.add
                       ).then_inc(d_done, 1)

                def norm2(half):
                    if half == 0:
                        took("out2")
                        moments(1, y2, x_next, var2_asked)
                    else:
                        dve.wait_ge(x2_free, u.x + 1)
                        apply(1, y2, x2, var2_done, u.x, x2_ready)

                def turn_x2():
                    nc.vector.tensor_copy(x2t[:, :, :].rearrange("p k t -> p (k t)"), ready("x2t")[:, :]
                                          ).then_inc(d_done, 1)

                def gate_logits():
                    nc.vector.tensor_copy(lg[:, :, :].rearrange("p j e -> p (j e)"), ready("lg")[:, 0:TT * E]
                                          ).then_inc(d_done, 1)
                    took("lg")
                    nc.vector.memset(scratch[:, 13:14], 0.0)

                def choose():
                    for j in range(TT):
                        ins = nc.vector.max(m8[:, j, :], lg[:, j, :])
                    x_next(ins)
                    nc.vector.tensor_scalar(nmx[:, :], m8[:, :, 0], -1.0, None, ALU.mult).then_inc(top_ready, 1)

                def choose_index():
                    for j in range(TT):
                        ins = nc.vector.max_index(i8[:, j, :], m8[:, j, :], lg[:, j, :])
                    x_next(ins)
                    x_next(nc.vector.tensor_copy(ix[:, :].rearrange("p (j k) -> p j k", k=K), i8[:, :, 0:K]))
                    many = [P, TT * K, E]
                    x_next(tt(hot[:, :, :], iota.unsqueeze(1).to_broadcast(many),
                              ix[:, :].unsqueeze(2).to_broadcast(many), ALU.is_equal))
                    for j in range(TT):
                        ins = nc.vector.tensor_reduce(
                            chosen[:, j, :], hot[:, j * K:(j + 1) * K, :].rearrange("p k e -> p e k"), X, ALU.max)
                    ins.then_inc(chosen_ready, 1)

                def shared_up():
                    dve.wait_ge(a_done, u.a + (u.an["sg", 1] + 1 + RA))
                    tt(sgr[:, :], sgg[:, :], sgu[:, :], ALU.mult)
                    x_next(nc.vector.tensor_scalar(sge[:, :], sge[:, :], 1.0, None, ALU.add))
                    x_next(nc.vector.reciprocal(sge[:, :], sge[:, :]))
                    tt(sgh[:, :], sgr[:, :], sge[:, :], ALU.mult).then_inc(sgh_ready, 1)

                def shared_down():
                    o = ready("sh")
                    b = slice(u.x, u.x + 1) if isinstance(u.x, int) else bass.ds(u.x, 1)
                    tt(base_all[:, b, :, :].rearrange("p o j n -> p (o j n)"), o[:, :],
                       x2[:, :, :].rearrange(flat), ALU.add).then_inc(d_done, 1)

                def places():
                    o = ready("pos")
                    for j in range(TT):
                        ks = slice(j * K, (j + 1) * K)
                        ins = tt(hp[:, ks, :], hot[:, ks, :], o[:, j * E:(j + 1) * E].unsqueeze(1)
                                 .to_broadcast([P, K, E]), ALU.mult)
                    ins.then_inc(d_done, 1)

                def places_found():
                    took("pos")
                    x_next(tt(before[:, :], before[:, :], chosen[:, 0, :], ALU.add))
                    tt(before[:, :], before[:, :], chosen[:, 1, :], ALU.add)
                    x_next(nc.vector.tensor_reduce(ps[:, :], hp[:, :, :], X, ALU.add))
                    nc.vector.tensor_scalar(vd[:, :], ps[:, :], float(CAP), None, ALU.is_lt)
                    nc.vector.scalar_tensor_tensor(out=fl[:, :], in0=ix[:, :], scalar=float(CAP), in1=ps[:, :],
                                                   op0=ALU.mult, op1=ALU.add)
                    x_next(nc.vector.tensor_copy(ids[:, :], spare[:, :]))
                    x_next(tt(fd[:, :], fl[:, :], spare[:, :], ALU.subtract))
                    x_next(tt(fd[:, :], fd[:, :], vd[:, :], ALU.mult))
                    x_next(tt(fd[:, :], fd[:, :], spare[:, :], ALU.add))
                    nc.vector.tensor_copy(slot_i[:, :], fd[:, :]).then_inc(slots_known, 1)

                def weigh():
                    b = slice(u.x, u.x + 1) if isinstance(u.x, int) else bass.ds(u.x, 1)
                    x_next(nc.vector.tensor_scalar(spare[:, :], spare[:, :], float(TT * P * K), None, ALU.add))
                    dve.wait_ge(ew_ready, u.x + 1)
                    x_next(nc.vector.reciprocal(wi[:, :], ws[:, :]))
                    x_next(tt(vd[:, :].rearrange("p (j k) -> p j k", k=K),
                              vd[:, :].rearrange("p (j k) -> p j k", k=K),
                              wi[:, :].unsqueeze(2).to_broadcast([P, TT, K]), ALU.mult))
                    x_next(tt(gates_all[:, b, :].rearrange("p o c -> p (o c)"), vd[:, :],
                              ew[:, :, :].rearrange("p j k -> p (j k)"), ALU.mult))

                for name, n in u.steps:
                    if name == "take_proj":
                        proj(n)
                    elif name == "lines":
                        (lines0, lines1, lines2)[n]()
                    elif name == "split" and n == 0 and u.x is None:
                        split(heads, tt, s_next).then_inc(split_ready, 1)
                    elif name == "outer":
                        (outer1 if n else outer0)()
                    elif name == "take_moment":
                        moment(n)
                    elif name == "turn_heads":
                        for m, unit in enumerate(turned(n)):
                            if m % 2:
                                dst, src = turned_to(n, m, ready(*unit))
                                nc.vector.tensor_copy(dst, src).then_inc(d_done, 1)
                    elif name == "self":
                        if 0 <= n - 4 < H and n % 2:
                            nc.vector.tensor_copy(pt[:, n % RING, 0:384], ready("pt", n - 4)[:, 0:384]
                                                  ).then_inc(d_done, 1)
                        if n < H:
                            logits(n)
                    elif name == "sums":
                        sums()
                    elif name == "turn_out":
                        outputs()
                    elif name == "out":
                        out()
                    elif name == "queries":
                        queries()
                    elif name == "keys" and n == 0 and u.x is None:
                        dve.wait_ge(loaded2, 16 * 7)
                        nc.vector.tensor_scalar(wq_s[:, :, :], wq_s[:, :, :], float(XD) ** -0.5, None, ALU.mult
                                                ).then_inc(prepared2, 1)
                    elif name == "cross":
                        if n < XH:
                            rowmax(n)
                        if n in (7, 11, 15):
                            outputs2((n - 7) // 4)
                        if n == CROSS_SLOTS - 1:
                            outputs2(3)
                    elif name == "out2":
                        out2()
                    elif name == "norm1":
                        apply(0, y1, x1, var1_done, u.s, x1_ready)
                    elif name == "norm2":
                        norm2(n)
                    elif name == "x2t":
                        turn_x2()
                    elif name == "gate":
                        gate_logits()
                    elif name == "silu":
                        shared_up()
                    elif name == "shared" and n:
                        shared_down()
                    elif name == "choose":
                        (choose_index if n else choose)()
                    elif name == "place":
                        (places, places_found, weigh)[n]()
                    elif name == "split" and n == 2:
                        split([(lraw[:, 0, :, :], line_parts(0), 0)], tt, s_next).then_inc(lines_ready, 1)
                for p in range(len([k for k in u.dn if k[0] == "pad"])):
                    nc.vector.memset(scratch[:, 8 + p:9 + p], 0.0).then_inc(d_done, 1)
                assert count["s"] == (0 if u.s is None else S_STEPS + (FIRST_STEPS if u.x is None else 0)), count
                assert count["x"] == (0 if u.x is None else X_STEPS), count

            for u in passes(dve):
                part_a(u)

            dve.sem_inc(xet_done, 2)
            dve.sem_inc(he_ready, 2)

            def experts(i):
                first = isinstance(i, int)
                e0 = 0 if first else dve.snap(NE * i)

                def slots_turned(s):
                    dve.wait_ge(xet_ready, e0 + (s + 1))
                    nc.vector.tensor_copy(xet[:, s % 4, :, :].rearrange("p k t -> p (k t)"), bank[s % 2][:, :]
                                          ).then_inc(xet_done, 1)

                def hidden(s):
                    dve.wait_ge(sl_ready, e0 + (s + 1))
                    tt(he[:, s % 4, :], bank[2 + s % 2][:, CAP:2 * CAP], sl[:, s % 4, :], ALU.mult).then_inc(he_ready, 1)

                slots_turned(0)
                for s in range(NE):
                    if s < NE - 1:
                        slots_turned(s + 1)
                    hidden(s)
                    if first and s == OWN_AT + 1:
                        dve.wait_ge(own_turned, 1)
                        nc.vector.tensor_copy(own_i[:, :], bank[7][:, 0:NS]).then_inc(own_ready, 1)

            experts(0)
            with dve.Fori(1, E // NE) as i:
                experts(i)

            base_flat = base_all[:, :, :, :].rearrange("p b j n -> p (b j n)")
            gates_flat = gates_all[:, :, :].rearrange("p b c -> p (b c)")

            def fin(r, n):
                dve.wait_ge(fin_step, COMBINE_STEPS * r + n + 1)

            def add_up(r):
                if r >= 2:
                    dve.wait_ge(yo_ready, NC * (r - 1))
                for k in range(K):
                    for s in range(NC):
                        t = NC * r + s
                        if k == 0:
                            dve.wait_ge(gathered[t % (2 * NC)], 16 * (t // (2 * NC)) + 16)
                            prev = base_flat[:, t * D:(t + 1) * D]
                        else:
                            fin(r, NC * (k - 1) + s)
                            prev = acc[:, r % 2, s, :]
                        nc.vector.scalar_tensor_tensor(
                            out=acc[:, r % 2, s, :], in0=gr[t % (2 * NC)][:, k, :],
                            scalar=gates_flat[:, t * K + k:t * K + k + 1], in1=prev,
                            op0=ALU.mult, op1=ALU.add).then_inc(fin_step, 1)

            def moments3(r):
                for s in range(NC):
                    fin(r, NC * (K - 1) + s)
                    nc.vector.bn_stats(st3[:, NC * r + s, :], acc[:, r % 2, s, :]).then_inc(fin_step, 1)
                for s in range(NC):
                    fin(r, NC * K + s)
                    nc.vector.bn_aggr(mv3[:, NC * r + s, :], st3[:, NC * r + s, :]).then_inc(fin_step, 1)
                fin(r, COMBINE_STEPS - 1)
                tiles = slice(NC * r, NC * (r + 1))
                nc.vector.tensor_scalar(va3[:, tiles], mv3[:, tiles, 1], EPS, None, ALU.add).then_inc(var_ready, 1)

            def apply3(r):
                dve.wait_ge(rstd_ready, r + 1)
                for s in range(NC):
                    t = NC * r + s
                    if r >= 2:
                        dve.wait_ge(stored[t % (2 * NC)], 16)
                    nc.vector.tensor_scalar(yo[:, r % 2, s, :], acc[:, r % 2, s, :], mv3[:, t, 0:1], rv3[:, t:t + 1],
                                            ALU.subtract, ALU.mult).then_inc(yo_ready, 1)

            for r in range(ROUNDS):
                add_up(r)
                if r:
                    apply3(r - 1)
                moments3(r)
            apply3(ROUNDS - 1)


def kernel(**a):
    import concourse.bacc as _bacc
    from concourse.bass_utils import run_bass_kernel_spmd as _run

    a = {k: np.asarray(v) for k, v in a.items()}

    def rows(v):
        return np.broadcast_to(v.reshape(1, -1), (P, v.size))

    r = np.arange(P)
    spare = SLOTS + (np.arange(TT)[None, :, None] * P + r[:, None, None]) * K + np.arange(K)
    const = np.concatenate([
        np.eye(P), r[:, None] <= r[None, :], np.where(r[None, :] > r[:, None], NEG, 0.0),
        np.broadcast_to(np.arange(E), (P, E)), spare.reshape(P, TT * K)], axis=1).astype(np.float32)
    x = a["x"]
    arrays = {
        "x": x,
        "xT": x.transpose(0, 2, 1),
        "ctxT": a["ctx_768"].transpose(0, 2, 1),
        "wall": np.concatenate([a["L0_attn_Wqkv"], a["L0_attn_W2w"], a["L0_attn_W1r"], a["L0_attn_W2r"],
                                a["L0_attn_W1w"]], axis=0).T,
        "bias": np.concatenate([rows(a["L0_attn_bqkv"]), rows(a["L0_attn_bout"]), rows(a["L0_xattn_b_out"]),
                                rows(a["L0_attn_bias_scale"])], axis=1),
        "wout": a["L0_attn_Wout"].T,
        "wq": a["L0_xattn_w_q"],
        "wkv": a["L0_xattn_w_kv"],
        "wo": a["L0_xattn_w_out"],
        "gate": a["L0_ffn_gate_w"].T,
        "wgu": a["L0_ffn_w_gate_up"],
        "wdn": a["L0_ffn_w_down"],
        "shgu": a["L0_ffn_shared_w_gate_up"],
        "shdn": a["L0_ffn_shared_w_down"],
        "const": const,
        "own": np.arange(SLOTS, dtype=np.float32).reshape(SLOTS, 1),
    }
    nc = _bacc.Bacc("TRN2", target_bir_lowering=False, num_devices=1)
    args = []
    for name, v in arrays.items():
        arrays[name] = v = np.ascontiguousarray(v)
        args.append(nc.dram_tensor(name, v.shape, mybir.dt.from_np(v.dtype), kind="ExternalInput").ap())
    args.append(nc.dram_tensor("out", (N, D), F32, kind="ExternalOutput").ap())
    build(nc, *args)
    got = _run(nc, [arrays], core_ids=[0])
    return got.results[0]["out"].reshape(B, T, D)
```
